# Optimizing a Trainium2 kernel written in Bass

```python
import numpy as np
import jax
import jax.numpy as jnp

def _softmax(x, axis=-1):
    return jax.nn.softmax(x, axis=axis)

def _gelu(x):
    return jax.nn.gelu(x, approximate=True)

def _silu(x):
    return jax.nn.silu(x)

def _sigmoid(x):
    return jax.nn.sigmoid(x)

def _layernorm(x, axis=-1, eps=1e-05):
    m = jnp.mean(x, axis=axis, keepdims=True)
    v = jnp.var(x, axis=axis, keepdims=True)
    return (x - m) / jnp.sqrt(v + eps)

def _scatter_add(tgt, idx, src, axis=0):
    return tgt.at[idx].add(src)

def _segment_sum(src, seg, n):
    return jax.ops.segment_sum(src, seg, n)
kernel_name = 'mk_metaformer_d4_conv_nhwc128_r4_2532b5'

def setup_inputs(seed: int=0):
    np.random.seed(seed)
    _w = jnp.asarray

    def _rec_inputs():
        import jax
        import jax.numpy as jnp
        _gk = jax.random.key(seed)
        x = -0.000125 + 0.9999 * jax.random.normal(jax.random.fold_in(_gk, 1), (1, 128, 128, 32), jnp.float32)
        return x
    x = _rec_inputs()

    def _L0_conv_setup():
        import jax, jax.numpy as jnp
        import numpy as np
        B, L, D, C = (1, 128, 32, 32)

        def _layernorm(x, w, b, eps=1e-05):
            mu = jnp.mean(x, axis=-1, keepdims=True)
            var = jnp.var(x, axis=-1, keepdims=True)
            return (x - mu) * jax.lax.rsqrt(var + eps) * w + b
        key = jax.random.key(seed)
        ks = jax.random.split(key, 12)
        s = 0.05
        f32 = jnp.float32
        return {'z': jax.random.normal(ks[0], (B, L, L, D), f32), 'ln_in_w': jnp.ones((D,), f32), 'ln_in_b': jnp.zeros((D,), f32), 'Wga': jax.random.normal(ks[1], (D, C), f32) * s, 'bga': jnp.zeros((C,), f32), 'Wla': jax.random.normal(ks[2], (D, C), f32) * s, 'bla': jnp.zeros((C,), f32), 'Wgb': jax.random.normal(ks[3], (D, C), f32) * s, 'bgb': jnp.zeros((C,), f32), 'Wlb': jax.random.normal(ks[4], (D, C), f32) * s, 'blb': jnp.zeros((C,), f32), 'ln_o_w': jnp.ones((C,), f32), 'ln_o_b': jnp.zeros((C,), f32), 'Wgo': jax.random.normal(ks[5], (D, D), f32) * s, 'bgo': jnp.zeros((D,), f32), 'Wlo': jax.random.normal(ks[6], (C, D), f32) * s, 'blo': jnp.zeros((D,), f32)}
    _L0_conv_all = _L0_conv_setup()
    _L0_conv_in = {k: v for k, v in _L0_conv_all.items() if k in ('ln_in_w', 'ln_in_b', 'Wga', 'bga', 'Wla', 'bla', 'Wgb', 'bgb', 'Wlb', 'blb', 'ln_o_w', 'ln_o_b', 'Wgo', 'bgo', 'Wlo', 'blo')}
    del _L0_conv_all

    def _L0_ffn_setup():
        import jax, jax.numpy as jnp
        import numpy as np
        B, S, D, E, H, O, K = (128, 512, 32, 16, 128, 32, 8)
        key = jax.random.key(seed)
        k0, k1, k2, k3 = jax.random.split(key, 4)
        x = jax.random.normal(k0, (B, S, D), dtype=jnp.float32)
        gate_w = jax.random.normal(k1, (E, D), dtype=jnp.float32) * (1.0 / np.sqrt(D))
        gate_b = jnp.zeros((E,), dtype=jnp.float32)
        weight1 = jax.random.uniform(k2, (E, D + 1, H), dtype=jnp.float32, minval=-1.0, maxval=1.0) * (1.0 / np.sqrt(D + 1))
        weight2 = jax.random.uniform(k3, (E, H + 1, O), dtype=jnp.float32, minval=-1.0, maxval=1.0) * (1.0 / np.sqrt(H + 1))
        return {'x': x, 'gate_w': gate_w, 'gate_b': gate_b, 'weight1': weight1, 'weight2': weight2}
    _L0_ffn_all = _L0_ffn_setup()
    _L0_ffn_in = {k: v for k, v in _L0_ffn_all.items() if k in ('gate_w', 'gate_b', 'weight1', 'weight2')}
    del _L0_ffn_all

    def _L1_conv_setup():
        import jax, jax.numpy as jnp
        import numpy as np
        C_Z = 32
        C_HIDDEN = 32
        EPS = 1e-05

        def _layer_norm(x, w, b):
            mu = jnp.mean(x, axis=-1, keepdims=True)
            var = jnp.var(x, axis=-1, keepdims=True)
            return (x - mu) * jax.lax.rsqrt(var + EPS) * w + b
        key = jax.random.key(seed)
        ks = jax.random.split(key, 8)
        B, N = (1, 128)
        z = jax.random.normal(ks[0], (B, N, N, C_Z), dtype=jnp.float32)
        mask = jnp.ones((B, N, N), dtype=jnp.float32)
        s = 0.02
        params = {'w_ap': jax.random.normal(ks[1], (C_Z, C_HIDDEN), jnp.float32) * s, 'b_ap': jnp.zeros((C_HIDDEN,), jnp.float32), 'w_ag': jax.random.normal(ks[2], (C_Z, C_HIDDEN), jnp.float32) * s, 'b_ag': jnp.ones((C_HIDDEN,), jnp.float32), 'w_bp': jax.random.normal(ks[3], (C_Z, C_HIDDEN), jnp.float32) * s, 'b_bp': jnp.zeros((C_HIDDEN,), jnp.float32), 'w_bg': jax.random.normal(ks[4], (C_Z, C_HIDDEN), jnp.float32) * s, 'b_bg': jnp.ones((C_HIDDEN,), jnp.float32), 'w_g': jax.random.normal(ks[5], (C_Z, C_Z), jnp.float32) * s, 'b_g': jnp.ones((C_Z,), jnp.float32), 'w_z': jax.random.normal(ks[6], (C_HIDDEN, C_Z), jnp.float32) * s, 'b_z': jnp.zeros((C_Z,), jnp.float32), 'ln_in_w': jnp.ones((C_Z,), jnp.float32), 'ln_in_b': jnp.zeros((C_Z,), jnp.float32), 'ln_out_w': jnp.ones((C_HIDDEN,), jnp.float32), 'ln_out_b': jnp.zeros((C_HIDDEN,), jnp.float32)}
        return {'z': z, 'mask': mask, **params}
    _L1_conv_all = _L1_conv_setup()
    _L1_conv_in = {k: v for k, v in _L1_conv_all.items() if k in ('mask', 'w_ap', 'b_ap', 'w_ag', 'b_ag', 'w_bp', 'b_bp', 'w_bg', 'b_bg', 'w_g', 'b_g', 'w_z', 'b_z', 'ln_in_w', 'ln_in_b', 'ln_out_w', 'ln_out_b')}
    del _L1_conv_all

    def _L1_ffn_setup():
        import jax, jax.numpy as jnp
        import numpy as np
        BN_EPS = 1e-05
        key = jax.random.key(seed)
        k1, k2, k3 = jax.random.split(key, 3)
        B, T, I, H = (16, 512, 32, 32)
        x = jax.random.normal(k1, (B, T, I), dtype=jnp.float32)
        W = jax.random.normal(k2, (H, I), dtype=jnp.float32) * (1.0 / np.sqrt(I))
        V = jnp.linalg.qr(jax.random.normal(k3, (H, H), dtype=jnp.float32))[0]
        gamma = jnp.ones((H,), dtype=jnp.float32)
        beta = jnp.zeros((H,), dtype=jnp.float32)
        return {'x': x, 'W': W, 'V': V, 'gamma': gamma, 'beta': beta}
    _L1_ffn_all = _L1_ffn_setup()
    _L1_ffn_in = {k: v for k, v in _L1_ffn_all.items() if k in ('W', 'V', 'gamma', 'beta')}
    del _L1_ffn_all

    def _L2_conv_setup():
        import jax, jax.numpy as jnp
        import numpy as np
        B, H, W_DIM, C = (8, 32, 64, 32)
        K = 9

        def conv1d_same(y, W):
            return jax.lax.conv_general_dilated(y, W, window_strides=(1,), padding='SAME', dimension_numbers=('NWC', 'WIO', 'NWC'))
        key = jax.random.key(seed)
        kx, kw = jax.random.split(key)
        x = jax.random.normal(kx, (B, H, W_DIM, C), dtype=jnp.float32)
        W = jax.random.normal(kw, (K, C, C), dtype=jnp.float32) * 0.02
        return {'x': x, 'W': W}
    _L2_conv_all = _L2_conv_setup()
    _L2_conv_in = {k: v for k, v in _L2_conv_all.items() if k in ('W',)}
    del _L2_conv_all

    def _L2_ffn_setup():
        import jax, jax.numpy as jnp
        import numpy as np
        BN_EPS = 1e-05
        key = jax.random.key(seed)
        k1, k2, k3 = jax.random.split(key, 3)
        B, T, I, H = (16, 512, 32, 32)
        x = jax.random.normal(k1, (B, T, I), dtype=jnp.float32)
        W = jax.random.normal(k2, (H, I), dtype=jnp.float32) * (1.0 / np.sqrt(I))
        V = jnp.linalg.qr(jax.random.normal(k3, (H, H), dtype=jnp.float32))[0]
        gamma = jnp.ones((H,), dtype=jnp.float32)
        beta = jnp.zeros((H,), dtype=jnp.float32)
        return {'x': x, 'W': W, 'V': V, 'gamma': gamma, 'beta': beta}
    _L2_ffn_all = _L2_ffn_setup()
    _L2_ffn_in = {k: v for k, v in _L2_ffn_all.items() if k in ('W', 'V', 'gamma', 'beta')}
    del _L2_ffn_all

    def _L3_conv_setup():
        import jax, jax.numpy as jnp
        import numpy as np
        IN_DIM = 32
        DIM = 32
        EPS = 1e-05

        def layernorm(x, g, b):
            m = jnp.mean(x, axis=-1, keepdims=True)
            v = jnp.var(x, axis=-1, keepdims=True)
            return (x - m) * jax.lax.rsqrt(v + EPS) * g + b
        key = jax.random.key(seed)
        ks = jax.random.split(key, 12)
        s1 = 1.0 / np.sqrt(IN_DIM)
        s2 = 1.0 / np.sqrt(DIM)
        return {'z': jax.random.normal(ks[0], (1, 128, 128, IN_DIM), jnp.float32), 'norm_g': jnp.ones((IN_DIM,), jnp.float32), 'norm_b': jnp.zeros((IN_DIM,), jnp.float32), 'w1': jax.random.uniform(ks[1], (IN_DIM, 2 * DIM), jnp.float32, -s1, s1), 'b1': jax.random.uniform(ks[2], (2 * DIM,), jnp.float32, -s1, s1), 'w2': jax.random.uniform(ks[3], (IN_DIM, 2 * DIM), jnp.float32, -s1, s1), 'b2': jax.random.uniform(ks[4], (2 * DIM,), jnp.float32, -s1, s1), 'wg': jax.random.uniform(ks[5], (IN_DIM, IN_DIM), jnp.float32, -s1, s1), 'bg': jax.random.uniform(ks[6], (IN_DIM,), jnp.float32, -s1, s1), 'onorm_g': jnp.ones((DIM,), jnp.float32), 'onorm_b': jnp.zeros((DIM,), jnp.float32), 'wo': jax.random.uniform(ks[7], (DIM, IN_DIM), jnp.float32, -s2, s2), 'bo': jax.random.uniform(ks[8], (IN_DIM,), jnp.float32, -s2, s2)}
    _L3_conv_all = _L3_conv_setup()
    _L3_conv_in = {k: v for k, v in _L3_conv_all.items() if k in ('norm_g', 'norm_b', 'w1', 'b1', 'w2', 'b2', 'wg', 'bg', 'onorm_g', 'onorm_b', 'wo', 'bo')}
    del _L3_conv_all

    def _L3_ffn_setup():
        import jax, jax.numpy as jnp
        import numpy as np
        B, N, D, C, E, K = (8, 2048, 32, 32, 8, 2)
        key = jax.random.key(seed)
        k0, k1, k2 = jax.random.split(key, 3)
        x = jax.random.normal(k0, (B, N, D), dtype=jnp.float32)
        router_w = jax.random.normal(k1, (D, E), dtype=jnp.float32) * 0.05
        router_b = jnp.zeros((E,), dtype=jnp.float32)
        expert_w = jax.random.normal(k2, (E, D, C), dtype=jnp.float32) * (1.0 / np.sqrt(D))
        expert_b = jnp.zeros((E, C), dtype=jnp.float32)
        return {'x': x, 'router_w': router_w, 'router_b': router_b, 'expert_w': expert_w, 'expert_b': expert_b}
    _L3_ffn_all = _L3_ffn_setup()
    _L3_ffn_in = {k: v for k, v in _L3_ffn_all.items() if k in ('router_w', 'router_b', 'expert_w', 'expert_b')}
    del _L3_ffn_all
    return {'x': x, 'L0_conv_ln_in_w': _L0_conv_in['ln_in_w'], 'L0_conv_ln_in_b': _L0_conv_in['ln_in_b'], 'L0_conv_Wga': _L0_conv_in['Wga'], 'L0_conv_bga': _L0_conv_in['bga'], 'L0_conv_Wla': _L0_conv_in['Wla'], 'L0_conv_bla': _L0_conv_in['bla'], 'L0_conv_Wgb': _L0_conv_in['Wgb'], 'L0_conv_bgb': _L0_conv_in['bgb'], 'L0_conv_Wlb': _L0_conv_in['Wlb'], 'L0_conv_blb': _L0_conv_in['blb'], 'L0_conv_ln_o_w': _L0_conv_in['ln_o_w'], 'L0_conv_ln_o_b': _L0_conv_in['ln_o_b'], 'L0_conv_Wgo': _L0_conv_in['Wgo'], 'L0_conv_bgo': _L0_conv_in['bgo'], 'L0_conv_Wlo': _L0_conv_in['Wlo'], 'L0_conv_blo': _L0_conv_in['blo'], 'L0_ffn_gate_w': _L0_ffn_in['gate_w'], 'L0_ffn_gate_b': _L0_ffn_in['gate_b'], 'L0_ffn_weight1': _L0_ffn_in['weight1'], 'L0_ffn_weight2': _L0_ffn_in['weight2'], 'L1_conv_mask': _L1_conv_in['mask'], 'L1_conv_w_ap': _L1_conv_in['w_ap'], 'L1_conv_b_ap': _L1_conv_in['b_ap'], 'L1_conv_w_ag': _L1_conv_in['w_ag'], 'L1_conv_b_ag': _L1_conv_in['b_ag'], 'L1_conv_w_bp': _L1_conv_in['w_bp'], 'L1_conv_b_bp': _L1_conv_in['b_bp'], 'L1_conv_w_bg': _L1_conv_in['w_bg'], 'L1_conv_b_bg': _L1_conv_in['b_bg'], 'L1_conv_w_g': _L1_conv_in['w_g'], 'L1_conv_b_g': _L1_conv_in['b_g'], 'L1_conv_w_z': _L1_conv_in['w_z'], 'L1_conv_b_z': _L1_conv_in['b_z'], 'L1_conv_ln_in_w': _L1_conv_in['ln_in_w'], 'L1_conv_ln_in_b': _L1_conv_in['ln_in_b'], 'L1_conv_ln_out_w': _L1_conv_in['ln_out_w'], 'L1_conv_ln_out_b': _L1_conv_in['ln_out_b'], 'L1_ffn_W': _L1_ffn_in['W'], 'L1_ffn_V': _L1_ffn_in['V'], 'L1_ffn_gamma': _L1_ffn_in['gamma'], 'L1_ffn_beta': _L1_ffn_in['beta'], 'L2_conv_W': _L2_conv_in['W'], 'L2_ffn_W': _L2_ffn_in['W'], 'L2_ffn_V': _L2_ffn_in['V'], 'L2_ffn_gamma': _L2_ffn_in['gamma'], 'L2_ffn_beta': _L2_ffn_in['beta'], 'L3_conv_norm_g': _L3_conv_in['norm_g'], 'L3_conv_norm_b': _L3_conv_in['norm_b'], 'L3_conv_w1': _L3_conv_in['w1'], 'L3_conv_b1': _L3_conv_in['b1'], 'L3_conv_w2': _L3_conv_in['w2'], 'L3_conv_b2': _L3_conv_in['b2'], 'L3_conv_wg': _L3_conv_in['wg'], 'L3_conv_bg': _L3_conv_in['bg'], 'L3_conv_onorm_g': _L3_conv_in['onorm_g'], 'L3_conv_onorm_b': _L3_conv_in['onorm_b'], 'L3_conv_wo': _L3_conv_in['wo'], 'L3_conv_bo': _L3_conv_in['bo'], 'L3_ffn_router_w': _L3_ffn_in['router_w'], 'L3_ffn_router_b': _L3_ffn_in['router_b'], 'L3_ffn_expert_w': _L3_ffn_in['expert_w'], 'L3_ffn_expert_b': _L3_ffn_in['expert_b']}

def reference(x, L0_conv_ln_in_w, L0_conv_ln_in_b, L0_conv_Wga, L0_conv_bga, L0_conv_Wla, L0_conv_bla, L0_conv_Wgb, L0_conv_bgb, L0_conv_Wlb, L0_conv_blb, L0_conv_ln_o_w, L0_conv_ln_o_b, L0_conv_Wgo, L0_conv_bgo, L0_conv_Wlo, L0_conv_blo, L0_ffn_gate_w, L0_ffn_gate_b, L0_ffn_weight1, L0_ffn_weight2, L1_conv_mask, L1_conv_w_ap, L1_conv_b_ap, L1_conv_w_ag, L1_conv_b_ag, L1_conv_w_bp, L1_conv_b_bp, L1_conv_w_bg, L1_conv_b_bg, L1_conv_w_g, L1_conv_b_g, L1_conv_w_z, L1_conv_b_z, L1_conv_ln_in_w, L1_conv_ln_in_b, L1_conv_ln_out_w, L1_conv_ln_out_b, L1_ffn_W, L1_ffn_V, L1_ffn_gamma, L1_ffn_beta, L2_conv_W, L2_ffn_W, L2_ffn_V, L2_ffn_gamma, L2_ffn_beta, L3_conv_norm_g, L3_conv_norm_b, L3_conv_w1, L3_conv_b1, L3_conv_w2, L3_conv_b2, L3_conv_wg, L3_conv_bg, L3_conv_onorm_g, L3_conv_onorm_b, L3_conv_wo, L3_conv_bo, L3_ffn_router_w, L3_ffn_router_b, L3_ffn_expert_w, L3_ffn_expert_b):
    import jax
    import jax.numpy as jnp

    def _L0_conv_ref(z, ln_in_w, ln_in_b, Wga, bga, Wla, bla, Wgb, bgb, Wlb, blb, ln_o_w, ln_o_b, Wgo, bgo, Wlo, blo):
        import jax, jax.numpy as jnp
        import numpy as np
        B, L, D, C = (1, 128, 32, 32)

        def _layernorm(x, w, b, eps=1e-05):
            mu = jnp.mean(x, axis=-1, keepdims=True)
            var = jnp.var(x, axis=-1, keepdims=True)
            return (x - mu) * jax.lax.rsqrt(var + eps) * w + b
        zn = _layernorm(z, ln_in_w, ln_in_b)
        a = jax.nn.sigmoid(zn @ Wga + bga) * (zn @ Wla + bla)
        b = jax.nn.sigmoid(zn @ Wgb + bgb) * (zn @ Wlb + blb)
        k = jnp.einsum('bimc,bmjc->bijc', a, b)
        out = jax.nn.sigmoid(zn @ Wgo + bgo) * (_layernorm(k, ln_o_w, ln_o_b) @ Wlo + blo)
        return out

    def _L0_ffn_ref(x, gate_w, gate_b, weight1, weight2):
        import jax, jax.numpy as jnp
        import numpy as np
        B, S, D, E, H, O, K = (128, 512, 32, 16, 128, 32, 8)
        Bn, Sn, Dn = x.shape
        logits = jnp.einsum('bsd,ed->bse', x, gate_w) + gate_b
        probs = jax.nn.softmax(logits, axis=1)
        vals, idx = jax.lax.top_k(probs.transpose(0, 2, 1), K)
        topv = vals.transpose(0, 2, 1)
        topi = idx.transpose(0, 2, 1)
        flat_idx = topi.reshape(Bn, K * E)
        gathered = jnp.take_along_axis(x, flat_idx[:, :, None], axis=1)
        gathered = gathered.reshape(Bn, K, E, Dn)
        pooled = jnp.einsum('bked,bke->bed', gathered, topv)
        ones = jnp.ones((E, Bn, 1), dtype=x.dtype)
        h = jnp.concatenate([pooled.transpose(1, 0, 2), ones], axis=-1)
        h = jax.nn.gelu(jnp.einsum('ebd,edh->ebh', h, weight1), approximate=False)
        h = jnp.concatenate([h, ones], axis=-1)
        out = jnp.einsum('ebh,eho->ebo', h, weight2)
        out = out.transpose(1, 0, 2)
        weighted = jnp.einsum('beo,bke->bkeo', out, topv).reshape(Bn, K * E, O)
        outputs = jnp.zeros((Bn, Sn, O), dtype=x.dtype)
        outputs = outputs.at[jnp.arange(Bn)[:, None], flat_idx].add(weighted)
        return outputs

    def _L1_conv_ref(z, mask, w_ap, b_ap, w_ag, b_ag, w_bp, b_bp, w_bg, b_bg, w_g, b_g, w_z, b_z, ln_in_w, ln_in_b, ln_out_w, ln_out_b):
        import jax, jax.numpy as jnp
        import numpy as np
        C_Z = 32
        C_HIDDEN = 32
        EPS = 1e-05

        def _layer_norm(x, w, b):
            mu = jnp.mean(x, axis=-1, keepdims=True)
            var = jnp.var(x, axis=-1, keepdims=True)
            return (x - mu) * jax.lax.rsqrt(var + EPS) * w + b
        m = mask[..., None]
        zn = _layer_norm(z, ln_in_w, ln_in_b)
        a = (zn @ w_ap + b_ap) * jax.nn.sigmoid(zn @ w_ag + b_ag) * m
        b = (zn @ w_bp + b_bp) * jax.nn.sigmoid(zn @ w_bg + b_bg) * m
        x = jnp.einsum('bikc,bjkc->bijc', a, b)
        x = _layer_norm(x, ln_out_w, ln_out_b) @ w_z + b_z
        g = jax.nn.sigmoid(zn @ w_g + b_g)
        return x * g

    def _L1_ffn_ref(x, W, V, gamma, beta):
        import jax, jax.numpy as jnp
        import numpy as np
        BN_EPS = 1e-05
        B, T, H = (x.shape[0], x.shape[1], W.shape[0])
        Wx = jnp.einsum('bti,hi->bth', x, W)
        flat = Wx.reshape(B * T, H)
        mean = jnp.mean(flat, axis=0)
        var = jnp.var(flat, axis=0)
        Wx = ((flat - mean) * jax.lax.rsqrt(var + BN_EPS) * gamma + beta).reshape(B, T, H)
        Vt = V.T

        def step(yt, wx_t):
            yt = jax.nn.sigmoid(wx_t + yt @ Vt)
            return (yt, yt)
        y0 = jnp.zeros((B, H), dtype=Wx.dtype)
        _, ys = jax.lax.scan(step, y0, jnp.swapaxes(Wx, 0, 1))
        return jnp.swapaxes(ys, 0, 1)

    def _L2_conv_ref(x, W):
        import jax, jax.numpy as jnp
        import numpy as np
        B, H, W_DIM, C = (8, 32, 64, 32)
        K = 9

        def conv1d_same(y, W):
            return jax.lax.conv_general_dilated(y, W, window_strides=(1,), padding='SAME', dimension_numbers=('NWC', 'WIO', 'NWC'))
        rows = jnp.moveaxis(x, 1, 0)
        row0 = rows[0]

        def step(carry, row):
            new = row + jax.nn.relu(conv1d_same(carry, W))
            return (new, new)
        _, outs = jax.lax.scan(step, row0, rows[1:])
        out = jnp.concatenate([row0[None], outs], axis=0)
        return jnp.moveaxis(out, 0, 1)

    def _L2_ffn_ref(x, W, V, gamma, beta):
        import jax, jax.numpy as jnp
        import numpy as np
        BN_EPS = 1e-05
        B, T, H = (x.shape[0], x.shape[1], W.shape[0])
        Wx = jnp.einsum('bti,hi->bth', x, W)
        flat = Wx.reshape(B * T, H)
        mean = jnp.mean(flat, axis=0)
        var = jnp.var(flat, axis=0)
        Wx = ((flat - mean) * jax.lax.rsqrt(var + BN_EPS) * gamma + beta).reshape(B, T, H)
        Vt = V.T

        def step(yt, wx_t):
            yt = jax.nn.sigmoid(wx_t + yt @ Vt)
            return (yt, yt)
        y0 = jnp.zeros((B, H), dtype=Wx.dtype)
        _, ys = jax.lax.scan(step, y0, jnp.swapaxes(Wx, 0, 1))
        return jnp.swapaxes(ys, 0, 1)

    def _L3_conv_ref(z, norm_g, norm_b, w1, b1, w2, b2, wg, bg, onorm_g, onorm_b, wo, bo):
        import jax, jax.numpy as jnp
        import numpy as np
        IN_DIM = 32
        DIM = 32
        EPS = 1e-05

        def layernorm(x, g, b):
            m = jnp.mean(x, axis=-1, keepdims=True)
            v = jnp.var(x, axis=-1, keepdims=True)
            return (x - m) * jax.lax.rsqrt(v + EPS) * g + b
        zn = layernorm(z, norm_g, norm_b)
        p1 = zn @ w1 + b1
        p2 = jax.nn.sigmoid(zn @ w2 + b2)
        ab = p2 * p1
        a, b = jnp.split(ab, 2, axis=-1)
        gate = jax.nn.sigmoid(zn @ wg + bg)
        prod = jnp.einsum('bikd,bjkd->bijd', a, b)
        out = gate * (layernorm(prod, onorm_g, onorm_b) @ wo + bo)
        return out

    def _L3_ffn_ref(x, router_w, router_b, expert_w, expert_b):
        import jax, jax.numpy as jnp
        import numpy as np
        B, N, D, C, E, K = (8, 2048, 32, 32, 8, 2)
        router_probs = jax.nn.softmax(x @ router_w + router_b, axis=-1)
        top_p, top_i = jax.lax.top_k(router_probs, K)
        top_p = top_p / jnp.sum(top_p, axis=-1, keepdims=True)
        expert_out = jnp.einsum('bnd,edc->bnec', x, expert_w) + expert_b
        gathered = jnp.take_along_axis(expert_out, top_i[..., None], axis=2)
        return jnp.einsum('bnk,bnkc->bnc', top_p, gathered)

    def _gn(v, G=32, eps=1e-05):
        B_, H_, W_, C_ = v.shape
        g = v.reshape(B_, H_, W_, G, C_ // G)
        m = jnp.mean(g, axis=(1, 2, 4), keepdims=True)
        s = jnp.var(g, axis=(1, 2, 4), keepdims=True)
        return ((g - m) / jnp.sqrt(s + eps)).reshape(v.shape)

    def _ln_c(v, eps=1e-06):
        m = jnp.mean(v, axis=-1, keepdims=True)
        s = jnp.var(v, axis=-1, keepdims=True)
        return (v - m) / jnp.sqrt(s + eps)

    def _ln_t(v, eps=1e-05):
        m = jnp.mean(v, axis=-1, keepdims=True)
        s = jnp.var(v, axis=-1, keepdims=True)
        return (v - m) / jnp.sqrt(s + eps)

    def _to_tokens(v):
        B_, H_, W_, C_ = v.shape
        return v.reshape(B_, H_ * W_, C_)

    def _from_tokens(t, like):
        return t.reshape(like.shape)
    x = x + _L0_conv_ref(_ln_c(x), L0_conv_ln_in_w, L0_conv_ln_in_b, L0_conv_Wga, L0_conv_bga, L0_conv_Wla, L0_conv_bla, L0_conv_Wgb, L0_conv_bgb, L0_conv_Wlb, L0_conv_blb, L0_conv_ln_o_w, L0_conv_ln_o_b, L0_conv_Wgo, L0_conv_bgo, L0_conv_Wlo, L0_conv_blo)
    t = _to_tokens(x)
    t = t + _L0_ffn_ref(_ln_t(t), L0_ffn_gate_w, L0_ffn_gate_b, L0_ffn_weight1, L0_ffn_weight2)
    x = _from_tokens(t, x)
    x = x + _L1_conv_ref(_ln_c(x), L1_conv_mask, L1_conv_w_ap, L1_conv_b_ap, L1_conv_w_ag, L1_conv_b_ag, L1_conv_w_bp, L1_conv_b_bp, L1_conv_w_bg, L1_conv_b_bg, L1_conv_w_g, L1_conv_b_g, L1_conv_w_z, L1_conv_b_z, L1_conv_ln_in_w, L1_conv_ln_in_b, L1_conv_ln_out_w, L1_conv_ln_out_b)
    t = _to_tokens(x)
    t = t + _L1_ffn_ref(_ln_t(t), L1_ffn_W, L1_ffn_V, L1_ffn_gamma, L1_ffn_beta)
    x = _from_tokens(t, x)
    x = x + _L2_conv_ref(_ln_c(x), L2_conv_W)
    t = _to_tokens(x)
    t = t + _L2_ffn_ref(_ln_t(t), L2_ffn_W, L2_ffn_V, L2_ffn_gamma, L2_ffn_beta)
    x = _from_tokens(t, x)
    x = x + _L3_conv_ref(_ln_c(x), L3_conv_norm_g, L3_conv_norm_b, L3_conv_w1, L3_conv_b1, L3_conv_w2, L3_conv_b2, L3_conv_wg, L3_conv_bg, L3_conv_onorm_g, L3_conv_onorm_b, L3_conv_wo, L3_conv_bo)
    t = _to_tokens(x)
    t = t + _L3_ffn_ref(_ln_t(t), L3_ffn_router_w, L3_ffn_router_b, L3_ffn_expert_w, L3_ffn_expert_b)
    x = _from_tokens(t, x)
    return x

_drawn_inputs = setup_inputs


def setup_inputs(seed=0):
    import zlib

    import numpy as np

    out = dict(_drawn_inputs(seed))
    spreads = {'L0_conv_ln_in_w': (1.0, 0.2),
     'L0_conv_ln_in_b': (0.0, 0.1),
     'L0_conv_bga': (0.0, 0.354),
     'L0_conv_bla': (0.0, 0.1),
     'L0_conv_bgb': (0.0, 0.328),
     'L0_conv_blb': (0.0, 0.1),
     'L0_conv_ln_o_w': (1.0, 0.2),
     'L0_conv_ln_o_b': (0.0, 0.1),
     'L0_conv_bgo': (0.0, 0.1),
     'L0_conv_blo': (0.0, 0.1),
     'L0_ffn_gate_b': (0.0, 0.1),
     'L1_conv_b_ap': (0.0, 0.1),
     'L1_conv_b_ag': (1.0, 0.6),
     'L1_conv_b_bp': (0.0, 0.1),
     'L1_conv_b_bg': (1.0, 0.6),
     'L1_conv_b_g': (1.0, 0.6),
     'L1_conv_b_z': (0.0, 0.1),
     'L1_conv_ln_in_w': (1.0, 0.6),
     'L1_conv_ln_in_b': (0.0, 0.1),
     'L1_conv_ln_out_w': (1.0, 0.562),
     'L1_conv_ln_out_b': (0.0, 0.348),
     'L1_ffn_gamma': (1.0, 0.2),
     'L1_ffn_beta': (0.0, 0.1),
     'L2_ffn_gamma': (1.0, 0.2),
     'L2_ffn_beta': (0.0, 0.27),
     'L3_conv_norm_g': (1.0, 0.2),
     'L3_conv_norm_b': (0.0, 0.1),
     'L3_conv_onorm_g': (1.0, 0.2),
     'L3_conv_onorm_b': (0.0, 0.1),
     'L3_ffn_router_b': (0.0, 0.1),
     'L3_ffn_expert_b': (0.0, 0.3)}
    factors = {'L0_ffn_gate_w': 8.0,
     'L0_ffn_weight1': 8.0,
     'L0_ffn_weight2': 8.0,
     'L1_conv_w_ag': 7.358,
     'L1_conv_w_bg': 8.0,
     'L1_conv_w_g': 4.06,
     'L3_conv_b2': 2.719}
    for name, (base, spread) in spreads.items():
        noise = np.random.default_rng([zlib.crc32(name.encode()), seed]).standard_normal(out[name].shape)
        drawn = base * np.exp(spread * noise) if base else spread * noise
        out[name] = jnp.asarray(drawn.astype(out[name].dtype))
    for name, factor in factors.items():
        out[name] = (out[name] * factor).astype(out[name].dtype)
    return out
```

```python
from contextlib import ExitStack

import concourse.bass as bass
from concourse import mybir
from concourse.alu_op_type import AluOpType as ALU

F32 = mybir.dt.float32
I32 = mybir.dt.int32
ACT = mybir.ActivationFunctionType
AX = mybir.AxisListType

N = 128
C = 32
G, S = 4, 32
NC = N * C
GC = G * C
BANK = 512
Q = 8
LOADS = 4
SQ = S // Q
E0, K0, H0 = 16, 8, 128
SEG = N // E0
SEGI = N // SEG
SEGT = SEGI * N
E3 = 8
TAPS = 9
CHUNK = 16
WARM = 12
ROUNDS = ((CHUNK - WARM, WARM, 0), (0, CHUNK, WARM))
STEPS = WARM + CHUNK
STREAMS = 2
NCH = NC // CHUNK
NS = NCH // STREAMS
ROWCH = N // CHUNK
ROWS_S = ROWCH // STREAMS
GENERAL_ROUNDS = G * NCH - 1
GENERAL_SCANS = ROWCH - 1
EPS, EPS_C = 1e-5, 1e-6
TRIS = ("L0", "L1", "L3")
POOL_CONSTS = 11
DVE_CONSTS = 11
PAR_FIRST = 16 * 2
PAR_LOADS = 16 * 4
SCAN_COPIES = 36
FAR = 1.0e30
FIXED_TOL = 2.0 ** -22

PAR = {}
_at = 0
for _name, _count in (
    [(f"{l}_w", 160) for l in ("L0", "L1", "L3")] + [(f"{l}_wo", 32) for l in ("L0", "L1", "L3")]
    + [(f"{l}_{v}", 1) for l in ("L0", "L1", "L3") for v in ("lnw", "lnb", "low", "lob")]
    + [("gate", E0), ("gate_b", 1), ("conv", TAPS * C)]
    + [(f"{l}_{v}", n) for l in ("R1", "R2") for v, n in (("W", C), ("VT", C), ("gamma", 1), ("beta", 1))]
    + [("router", E3), ("expert", E3 * C)]
):
    PAR[_name] = (_at, _count)
    _at += _count
NPAR = _at
ROW = {}
_at = 0
for _name, _count in ([(f"{l}_b", 160) for l in ("L0", "L1", "L3")] + [(f"{l}_bo", 32) for l in ("L0", "L1", "L3")]
                      + [("router_b", E3), ("expert_b", E3 * C)]):
    ROW[_name] = (_at, _count)
    _at += _count
NROW = _at



class Stage:

    def __init__(self, name, src, dst, scratch, eps, e2):
        self.name, self.s, self.at = name, {}, {}
        self.src, self.dst, self.scratch = src, dst, scratch
        self.eps, self.e2 = eps, e2
        self.ready = None
        self.banks_free = []
        self.wbank = self.wcol = 0


def build(nc, x_d, par_d, row_d, mask_d, w1_d, w2_d, w2l_d, out_d):
    with ExitStack() as ctx:
        def sb(name, shape, dt=F32):
            return ctx.enter_context(nc.sbuf_tensor(name, shape, dt))

        def sem(name):
            return ctx.enter_context(nc.semaphore(name))

        XR = sb("x_rows", [N, NC])
        XC = sb("x_cols", [N, NC])
        Z = sb("z", [N, NC])
        SQR = sb("squares", [N, NC])
        ZT = sb("z_t", [GC, S, N])
        AB = sb("ab", [N, 2 * NC])
        AT = ZT
        GATE = sb("gate", [N, NC])
        SIG = sb("sig", [N, 2, 2 * GC])
        TMP = sb("tmp", [N, 2, 2 * BANK])
        par = sb("par", [GC, NPAR])
        row = sb("row", [1, NROW])
        mask = sb("mask", [N, N])
        stats = sb("stats", [N, 4, N])
        ident = sb("ident", [N, N])
        d32 = sb("d32", [N, C])
        d16 = sb("d16", [N, E0])
        e16 = sb("e16", [E0, SEG, E0])
        m4 = sb("m4", [N, G])
        m8 = sb("m8", [N, SEG])
        cent = sb("cent", [GC, GC])
        same32 = sb("same32", [N, G, C])
        same16 = sb("same16", [N, SEG, E0])
        shift = sb("shift", [N, N])
        eps = sb("eps", [N, 4])
        onesf = sb("onesf", [1, N])
        warm_out = sb("warm_out", [1, 32])
        wp = {l: sb(f"wp_{l}", [GC, 5, GC]) for l in TRIS}
        wo = {l: sb(f"wo_{l}", [GC, 2, GC]) for l in TRIS}
        bo = {l: sb(f"bo_{l}", [N, C]) for l in TRIS}
        scaled = {l: sb(f"scaled_{l}", [GC, 5 * C]) for l in TRIS}
        wotmp = {l: sb(f"wotmp_{l}", [GC, GC + C]) for l in TRIS}
        lnb_at = {l: sb(f"lnb_at_{l}", [C, GC]) for l in TRIS}
        last = sb("last", [C, G, C])
        fold = sb("fold", [GC, GC])
        gw = sb("gw", [GC, 2, N])
        PSUM = ctx.enter_context(nc.psum_tensor("psum", [N, 8 * BANK], F32))

        def bank(b, cols=BANK, n=1):
            return PSUM[:, b * BANK:b * BANK + (n - 1) * BANK + cols]

        def blocks(t):
            return t[:, 0:NC].rearrange("p (g s c) -> p g s c", g=G, s=S)

        def pcol(name, rows=GC):
            a, n = PAR[name]
            return par[0:rows, a:a + n]

        def prow(name):
            a, n = ROW[name]
            return row[0:1, a:a + n]

        ABt = AB[:, :].rearrange("p (a c n) -> p a c n", a=2, c=C)

        x_in = [sem(f"x_in{q}") for q in range(LOADS)]
        par_first = sem("par_first")
        par_in = sem("par_in")
        out_stored = sem("out_stored")
        const_pool = sem("const_pool")
        const_dve = sem("const_dve")
        const_act = sem("const_act")
        X_LOADED = [[(x_in[q * LOADS // Q], 16)] for q in range(Q)]

        families = {
            "norm": "sum:8 mean:8 centred:8 square:8 sumsq:8 std:8 rstd:8 z:8",
            "turn": "zt_ps:8 zt:8",
            "weights": "w_half:4 w_dve:4 w_pe:1",
            "ones": "one:8",
            "tri": "zt_ps:8 zt:8 proj:32 sig:32 gate_ps:8 gate:8 lin:32 k_ps:8 k_act:4 k_dve:4 kt_ps:8 kt:8"
                   " o_ps:8 o_sq:8 o_sum:8 o_std:8 o_rstd:8 o_rg:8 o_mul:8 xg:8 xb:8 done:8",
            "turn_x": "ps:8 act:4 dve:4",
            "rec": "w_half:2 w_dve:1 w_pe:1 wx_ps:8 wx:8 bn:4 bnc:2 bn_ps:3 std1:1 bnw:5 step_ps:56 step_y0:29 step_y1:29 edge_ps:2"
                   " edge:2 chk:3 chk_ps:1 flag:3 y_ps:8 done:8",
        }
        shared = {}

        def stage(name, kinds, own="", src=None, dst=None, scratch=None, eps=0, e2=0.0):
            L = Stage(name, src, dst, scratch, eps, e2)
            for kind in kinds.split():
                if kind not in shared:
                    shared[kind] = [0, {}]
                    for word in families[kind].split():
                        shared[kind][1][word.split(":")[0]] = sem(f"{kind}_{word.split(':')[0]}")
                before, sems = shared[kind]
                shared[kind][0] += 1
                for word in families[kind].split():
                    key, n = word.split(":")
                    L.s[key], L.at[key] = sems[key], before * int(n)
            for key in own.split():
                L.s[key], L.at[key] = sem(f"{name}_{key}"), 0
            return L

        def wait_all(eng, levels):
            for s, v in levels:
                eng.wait_ge(s, v)

        t0 = stage("L0", "norm weights ones tri", "at_ps at_act at_dve", src=XR, scratch=XC, eps=0, e2=EPS)
        v0 = stage("V0", "turn_x", src=XR, dst=XC)
        f0 = stage("F0", "norm turn", "w_dve lg_ps lg_act pad top cand_ps cand fin mk_ps mk sel exp tot_ps tot w wt_ps"
                   " wt_act wt_dve pool_ps pl plt_ps plt h_ps h o_ps outm_ps outm y_ps done", src=XC, eps=1, e2=0.0)
        t1 = stage("L1", "norm weights ones tri", "ab", src=XC, scratch=XR, eps=0, e2=EPS)
        r1 = stage("R1", "norm turn rec", "g_ps g_y0 g_y1 g_edge_ps g_edge", src=XC, eps=1, e2=0.0)
        v1 = stage("V1", "turn_x", src=XC, dst=XR)
        sc = stage("SC", "norm turn", "pads w_dve w_pool conv row0 row1 kept chk chk_ps flag g_conv g_row0 g_row1"
                   " y_ps done", src=XR, eps=2, e2=0.0)
        v2 = stage("V2", "turn_x", src=XR, dst=XC)
        r2 = stage("R2", "norm turn rec", "g_ps g_y0 g_y1 g_edge_ps g_edge", src=XC, eps=1, e2=0.0)
        t3 = stage("L3", "norm weights ones tri", src=XC, scratch=XR, eps=0, e2=EPS)
        f3 = stage("F3", "norm ones turn", "w_dve w_pe rank rt_ps rt top diff sg e_ps e_mul e_half e_sum done", src=XC, eps=1, e2=0.0)

        x_done = lambda L: [(L.s["done"], L.at["done"] + S // 4)]
        x_chunks = lambda L: [[(L.s["done"], L.at["done"] + q + 1)] for q in range(Q)]
        turned = lambda L: [(L.s["act"], L.at["act"] + 4), (L.s["dve"], L.at["dve"] + 4)]
        t0.ready = X_LOADED
        v0.ready = x_done(t0)
        f0.ready = [turned(v0)] * Q
        t1.ready = [[(f0.s["done"], SEGI // 2)]] * Q
        r1.ready = x_chunks(t1)
        v1.ready = x_done(r1)
        sc.ready = [turned(v1)] * Q
        v2.ready = x_done(sc)
        r2.ready = [turned(v2)] * Q
        t3.ready = x_chunks(r2)
        f3.ready = x_chunks(t3)
        r1.banks_free = [(t1.s["o_mul"], t1.at["o_mul"] + S // 4)]
        t3.banks_free = x_done(r2)
        f3.banks_free = [(t3.s["o_mul"], t3.at["o_mul"] + S // 4)]

        def ln_parts():
            return [stats[:, k, :].rearrange("p (q s g) -> p q s g", q=Q, g=G) for k in range(4)]

        def over_c(t):
            return t.unsqueeze(3).to_broadcast([N, SQ, G, C])

        def by_block(t):
            return t[:, 0:NC].rearrange("p (s g c) -> p s g c", g=G, s=S)

        LN_STEPS = Q + 3

        def ln_dve_step(dve, L, u):
            X4 = by_block(L.src) if L is sc else blocks(L.src).rearrange("p g s c -> p s g c")
            Z4, SQ4 = by_block(Z), by_block(SQR)
            SUM, MEAN, SS, RSTD = ln_parts()
            q = u
            if 0 <= q < Q:
                wait_all(dve, L.ready[q])
                r = slice(SQ * q, SQ * (q + 1))
                dve.tensor_reduce(SUM[:, q], X4[:, r], AX.X, ALU.add).then_inc(L.s["sum"], 1)
                dve.wait_ge(L.s["sum"], L.at["sum"] + q + 1)
                dve.tensor_scalar(MEAN[:, q], SUM[:, q], 1.0 / C, None, ALU.mult).then_inc(L.s["mean"], 1)
                dve.wait_ge(L.s["mean"], L.at["mean"] + q + 1)
                dve.tensor_tensor(Z4[:, r], X4[:, r], over_c(MEAN[:, q]), ALU.subtract).then_inc(L.s["centred"], 1)
            q = u - 1
            if 0 <= q < Q:
                dve.wait_ge(L.s["square"], L.at["square"] + q + 1)
                dve.tensor_reduce(SS[:, q], SQ4[:, SQ * q:SQ * (q + 1)], AX.X, ALU.add).then_inc(L.s["sumsq"], 1)
            q = u - 2
            if 0 <= q < Q:
                dve.wait_ge(L.s["std"], L.at["std"] + q + 1)
                dve.reciprocal(RSTD[:, q], SUM[:, q]).then_inc(L.s["rstd"], 1)

        def ln_act_step(act, L, u):
            Z4, SQ4 = by_block(Z), by_block(SQR)
            SUM, _, SS, _ = ln_parts()
            q = u
            if 0 <= q < Q:
                r = slice(SQ * q, SQ * (q + 1))
                act.wait_ge(L.s["centred"], L.at["centred"] + q + 1)
                act.activation(SQ4[:, r], Z4[:, r], ACT.Square).then_inc(L.s["square"], 1)
            q = u - 1
            if 0 <= q < Q:
                act.wait_ge(L.s["sumsq"], L.at["sumsq"] + q + 1)
                act.activation(SUM[:, q], SS[:, q], ACT.Sqrt, bias=eps[:, L.eps:L.eps + 1],
                               scale=(1.0 + L.e2) / C).then_inc(L.s["std"], 1)
            q = u - 3
            if 0 <= q < Q:
                act.wait_ge(L.s["zt_ps"], L.at["zt_ps"] + q + 1)
                dst = ZT[:, 4 * q:4 * q + 4, :]
                if L is sc:
                    dst = RIN[:, :, 4 * q:4 * q + 4].rearrange("p i n -> p n i")
                act.activation(dst, bank(q % 2), ACT.Copy).then_inc(L.s["zt"], 1)

        def ln_pool_step(pool, L, u):
            q = u - 2
            if 0 <= q < Q:
                Z4, r = by_block(Z), slice(SQ * q, SQ * (q + 1))
                pool.wait_ge(L.s["square"], L.at["square"] + q + 1)
                last_c = C
                if "one" in L.s:
                    last_c = C - 1
                    pool.memset(Z4[:, r, :, last_c:], 1.0).then_inc(L.s["one"], 1)
                pool.wait_ge(L.s["rstd"], L.at["rstd"] + q + 1)
                rstd = ln_parts()[3][:, q].unsqueeze(3).to_broadcast([N, SQ, G, last_c])
                pool.tensor_tensor(Z4[:, r, :, 0:last_c], Z4[:, r, :, 0:last_c], rstd, ALU.mult).then_inc(L.s["z"], 1)

        def ln_dve(dve, L):
            for u in range(LN_STEPS):
                ln_dve_step(dve, L, u)

        def ln_act(act, L):
            warm_table(act, ACT.Sqrt)
            act.wait_ge(const_pool, POOL_CONSTS)
            for u in range(LN_STEPS):
                ln_act_step(act, L, u)

        def ln_pool(pool, L):
            for u in range(LN_STEPS):
                ln_pool_step(pool, L, u)

        warmed = [0]

        def warm_table(act, function):
            k = warmed[0]
            warmed[0] += 1
            if k == 0:
                act.wait_ge(const_pool, POOL_CONSTS)
            act.activation(warm_out[:, k:k + 1], onesf[0:1, 0:1], function)

        def turn_pe(pe, L, b, src, ps="zt_ps", act="zt_act", dve="zt_dve"):
            if b >= 2:
                pe.wait_ge(L.s[dve if b % 2 else act], L.at[dve if b % 2 else act] + b // 2)
            for k in range(4):
                m = pe.transpose(bank(b % 2)[:, k * N:(k + 1) * N], src(4 * b + k), ident[:, :])
            m.then_inc(L.s[ps], 1)

        def turn_copy(eng, L, b, dst, done, ps="zt_ps"):
            eng.wait_ge(L.s[ps], L.at[ps] + b + 1)
            if b % 2:
                eng.tensor_copy(dst, bank(b % 2)).then_inc(L.s[done], 1)
            else:
                eng.activation(dst, bank(b % 2), ACT.Copy).then_inc(L.s[done], 1)

        def block_of(t):
            return lambda s: t[:, s * GC:(s + 1) * GC]

        def turn_z_pe(pe, L, b):
            pe.wait_ge(L.s["z"], L.at["z"] + b + 1)
            if "one" in L.s:
                pe.wait_ge(L.s["one"], L.at["one"] + b + 1)
            if b >= 2:
                pe.wait_ge(L.s["zt"], L.at["zt"] + b - 1)
            for k in range(4):
                m = pe.transpose(bank(b % 2)[:, k * N:(k + 1) * N], block_of(Z)(4 * b + k), ident[:, :])
            m.then_inc(L.s["zt_ps"], 1)

        def turn_all_z_pe(pe, L):
            for b in range(S // 4):
                turn_z_pe(pe, L, b)

        def consts_pool(pool):
            pool.memset(ident[:, :], 0.0).then_inc(const_pool, 1)
            pool.wait_ge(const_pool, 1)
            pool.affine_select(out=ident[:, :], in_=ident[:, :], compare_op=ALU.not_equal, fill=1.0, base=0,
                               pattern=[[-1, N]], channel_multiplier=1).then_inc(const_pool, 1)
            pool.memset(shift[:, :], 0.0).then_inc(const_pool, 1)
            pool.wait_ge(const_pool, 3)
            pool.affine_select(out=shift[:, :], in_=shift[:, :], compare_op=ALU.not_equal, fill=1.0, base=C,
                               pattern=[[-1, N]], channel_multiplier=1).then_inc(const_pool, 1)
            for k, v in enumerate((EPS_C * EPS, EPS, EPS_C)):
                pool.memset(eps[:, k:k + 1], v).then_inc(const_pool, 1)
            pool.memset(onesf[:, :], 1.0).then_inc(const_pool, 1)
            pool.memset(last[:, :, 0:C - 1], 0.0).then_inc(const_pool, 1)
            pool.memset(last[:, :, C - 1:], 1.0).then_inc(const_pool, 1)
            pool.memset(gw[:, :, :], 0.0).then_inc(const_pool, 1)

        def consts_dve(dve):
            dve.wait_ge(const_pool, POOL_CONSTS)
            i3 = ident[:, :]
            dve.tensor_reduce(d32[:, :], i3.rearrange("p (g c) -> p c g", g=G), AX.X, ALU.add).then_inc(const_dve, 1)
            dve.tensor_reduce(m4[:, :], i3.rearrange("p (g c) -> p g c", g=G), AX.X, ALU.add).then_inc(const_dve, 1)
            dve.tensor_reduce(d16[:, :], i3.rearrange("p (s e) -> p e s", e=E0), AX.X, ALU.add).then_inc(const_dve, 1)
            dve.tensor_reduce(m8[:, :], i3.rearrange("p (s e) -> p s e", e=E0), AX.X, ALU.add).then_inc(const_dve, 1)
            dve.wait_ge(const_dve, 4)
            g_c = [N, G, C]
            dve.tensor_scalar(cent[:, :].rearrange("p (g c) -> p g c", g=G), m4[:, :].unsqueeze(2).to_broadcast(g_c),
                              -1.0 / C, None, ALU.mult).then_inc(const_dve, 1)
            dve.wait_ge(const_dve, 5)
            dve.tensor_tensor(cent[:, :], cent[:, :], ident[:, :], ALU.add).then_inc(const_dve, 1)
            dve.tensor_scalar(same32[:, :, :], d32[:, :].unsqueeze(1).to_broadcast(g_c), 1.0 / G, None, ALU.mult)\
                .then_inc(const_dve, 1)
            dve.tensor_copy(same16[:, :, :], d16[:, :].unsqueeze(1).to_broadcast([N, SEG, E0])).then_inc(const_dve, 1)
            dve.tensor_copy(e16[:, :, :], d16[0:E0, :].unsqueeze(1).to_broadcast([E0, SEG, E0])).then_inc(const_dve, 1)
            dve.tensor_scalar(fold[:, :].rearrange("p (g c) -> p g c", g=G), m4[:, :].unsqueeze(2).to_broadcast(g_c),
                              d32[:, C - 1:C], -1.0, ALU.mult, ALU.mult).then_inc(const_dve, 1)
            dve.wait_ge(const_dve, 10)
            dve.tensor_tensor(fold[:, :], fold[:, :], ident[:, :], ALU.add).then_inc(const_dve, 1)

        def fold_biases(pe, out, w, b, lnb_at=None, w0=None):
            pe.matmul(out, fold[:, :], w, start=True, stop=False)
            if lnb_at is not None:
                pe.matmul(out, lnb_at, w0, start=False, stop=False)
            return pe.matmul(out, last[0:1, :, :], b, start=False, stop=True)

        def by_groups(w, k):
            shape = [GC, k, G, C]
            return w.rearrange("p (k c) -> p k c", k=k).unsqueeze(2).to_broadcast(shape), \
                m4[:, :].unsqueeze(1).unsqueeze(3).to_broadcast(shape)

        TRI_W = 4

        def tri_weights1_dve(dve, L):
            l, sm = L.name, L.s["w_half"]
            dve.tensor_scalar(scaled[l][:, :], pcol(f"{l}_w"), pcol(f"{l}_lnw"), None, ALU.mult).then_inc(sm, 1)
            dve.tensor_scalar(wotmp[l][:, GC:], pcol(f"{l}_wo"), pcol(f"{l}_low"), None, ALU.mult).then_inc(sm, 1)
            dve.tensor_scalar(lnb_at[l][:, :], last[:, :, :].rearrange("p g c -> p (g c)"), pcol(f"{l}_lnb", C), None,
                              ALU.mult).then_inc(sm, 1)
            dve.wait_ge(sm, L.at["w_half"] + 2)
            dve.tensor_tensor(wotmp[l][:, 0:GC].rearrange("p (g c) -> p g c", g=G),
                              wotmp[l][:, GC:].unsqueeze(1).to_broadcast([GC, G, C]),
                              m4[:, :].unsqueeze(2).to_broadcast([GC, G, C]), ALU.mult).then_inc(sm, 1)

        def tri_weights2_dve(dve, L):
            l, sm = L.name, L.s["w_dve"]
            dve.wait_ge(L.s["w_pe"], L.at["w_pe"] + 1)
            w, m = by_groups(bank(L.wbank)[:, 0:5 * C], 5)
            dve.tensor_tensor(wp[l][:, :, :].rearrange("p k (g c) -> p k g c", g=G), w, m, ALU.mult).then_inc(sm, 1)
            dve.tensor_copy(bo[l][:, :], bank(L.wbank)[:, 160:192]).then_inc(sm, 1)
            dve.tensor_copy(wo[l][:, 0, :], bank(L.wbank)[:, 192:320]).then_inc(sm, 1)
            dve.tensor_copy(wo[l][:, 1, :], cent[:, :]).then_inc(sm, 1)

        def tri_weights_pe(pe, L):
            l = L.name
            pe.wait_ge(const_dve, DVE_CONSTS)
            pe.wait_ge(L.s["w_half"], L.at["w_half"] + TRI_W)
            pe.matmul(bank(L.wbank)[:, 160:192], pcol(f"{l}_lob", C).to_broadcast([C, N]), pcol(f"{l}_wo", C),
                      start=True, stop=False)
            pe.matmul(bank(L.wbank)[:, 160:192], onesf[:, :], prow(f"{l}_bo"), start=False, stop=True)
            pe.matmul(bank(L.wbank)[:, 192:320], cent[:, :], wotmp[l][:, 0:GC], start=True, stop=True)
            fold_biases(pe, bank(L.wbank)[:, 0:5 * C], scaled[l][:, :], prow(f"{l}_b"), lnb_at[l][:, :], pcol(f"{l}_w", C))\
                .then_inc(L.s["w_pe"], 1)

        LIN = BANK // 2
        TRI_LN = 5
        KB = [2, 3, 4, 5]
        GB = [6, 7]

        def tri_pe(pe, L):
            l = L.name
            freed = "lin"

            def project(b):
                pe.wait_ge(L.s["zt"], L.at["zt"] + b + 1)
                if b >= 2:
                    pe.wait_ge(L.s["gate"], L.at["gate"] + b - 1)
                for k in range(4):
                    s = 4 * b + k
                    if s >= 4:
                        pe.wait_ge(L.s[freed], L.at[freed] + s - 3)
                    pe.matmul(bank(KB[s % 4]), ZT[:, s, :], wp[l][:, 0:4, :], start=True, stop=True)\
                        .then_inc(L.s["proj"], 1)
                    m = pe.matmul(bank(GB[b % 2])[:, k * GC:(k + 1) * GC], ZT[:, s, :], wp[l][:, 4, :],
                                  start=True, stop=True)
                m.then_inc(L.s["gate_ps"], 1)

            for b in range(S // 4):
                turn_z_pe(pe, L, b)
                if b == 4:
                    pe.wait_ge(L.s["w_dve"], L.at["w_dve"] + TRI_W)
                    wait_all(pe, L.banks_free)
                    project(0)
            for b in range(1, S // 4):
                project(b)
            pe.wait_ge(L.s["ab" if L is t1 else "lin"], L.at["ab" if L is t1 else "lin"] + S)
            pe.wait_ge(L.s["zt"], L.at["zt"] + S // 4)
            lhs, rhs = ABt[:, 1], ABt[:, 0]
            if L is t0:
                lhs, rhs = AT, ABt[:, 1]
                for b in range(C // 4):
                    turn_pe(pe, L, b, lambda c: ABt[:, 0, c, :], "at_ps", "at_act", "at_dve")
            for b in range(C // 4):
                if L is t0:
                    pe.wait_ge(L.s["at_dve" if b % 2 else "at_act"], L.at["at_dve" if b % 2 else "at_act"] + b // 2 + 1)
                if b >= 4:
                    pe.wait_ge(L.s["k_dve" if b % 2 else "k_act"], L.at["k_dve" if b % 2 else "k_act"] + b // 2 - 1)
                for k in range(4):
                    c = 4 * b + k
                    m = pe.matmul(bank(KB[b % 4])[:, k * N:(k + 1) * N], lhs[:, c, :], rhs[:, c, :],
                                  start=True, stop=True)
                m.then_inc(L.s["k_ps"], 1)

            def out_project(b):
                pe.wait_ge(L.s["kt"], L.at["kt"] + b + 1)
                if b >= 3:
                    pe.wait_ge(L.s["o_mul"], L.at["o_mul"] + b - 2)
                for k in range(4):
                    m = pe.matmul(PSUM[:, (2 + 2 * (b % 3)) * BANK + k * 2 * GC:(2 + 2 * (b % 3)) * BANK + (k + 1) * 2 * GC],
                                  ZT[:, 4 * b + k, :], wo[l][:, :, :], start=True, stop=True)
                m.then_inc(L.s["o_ps"], 1)

            pe.wait_ge(L.s["k_act"], L.at["k_act"] + 4)
            pe.wait_ge(L.s["k_dve"], L.at["k_dve"] + 4)
            for b in range(S // 4):
                if b >= 2:
                    pe.wait_ge(L.s["kt"], L.at["kt"] + b - 1)
                for k in range(4):
                    m = pe.transpose(bank(b % 2)[:, k * N:(k + 1) * N], block_of(Z)(4 * b + k), ident[:, :])
                m.then_inc(L.s["kt_ps"], 1)
                if b >= 1:
                    out_project(b - 1)
            out_project(S // 4 - 1)

        def o_bank(b):
            o = (2 + 2 * (b % 3)) * BANK
            return PSUM[:, o:o + 2 * BANK].rearrange("p (s w f) -> p s w f", s=4, w=2)

        def k_copy(eng, L, b):
            eng.wait_ge(L.s["k_ps"], L.at["k_ps"] + b + 1)
            out = Z[:, :].rearrange("p (s g c) -> p c g s", g=G, c=C)[:, 4 * b:4 * b + 4]
            src = bank(KB[b % 4]).rearrange("p (c g s) -> p c g s", c=4, g=G)
            if b % 2:
                eng.tensor_copy(out, src).then_inc(L.s["k_dve"], 1)
            else:
                eng.activation(out, src, ACT.Copy).then_inc(L.s["k_act"], 1)

        def tri_act(act, L, after):
            warm_table(act, ACT.Sigmoid)
            for b in range(S // 4):
                for k in range(4):
                    s = 4 * b + k
                    act.wait_ge(L.s["proj"], L.at["proj"] + s + 1)
                    if s >= 2:
                        act.wait_ge(L.s["lin"], L.at["lin"] + s - 1)
                    act.activation(SIG[:, s % 2, :], bank(KB[s % 4], LIN), ACT.Sigmoid).then_inc(L.s["sig"], 1)
                act.wait_ge(L.s["gate_ps"], L.at["gate_ps"] + b + 1)
                act.activation(GATE[:, b * BANK:(b + 1) * BANK], bank(GB[b % 2]), ACT.Sigmoid).then_inc(L.s["gate"], 1)
            if L is t0:
                for b in range(0, C // 4, 2):
                    turn_copy(act, L, b, AT[:, 4 * b:4 * b + 4, :], "at_act", "at_ps")
            warm_table(act, ACT.Sqrt)
            for b in range(0, C // 4, 2):
                k_copy(act, L, b)

            def out_square(b):
                act.wait_ge(L.s["o_ps"], L.at["o_ps"] + b + 1)
                act.activation(SQR[:, b * BANK:(b + 1) * BANK].rearrange("p (s f) -> p s f", s=4),
                               o_bank(b)[:, :, 1, :], ACT.Square).then_inc(L.s["o_sq"], 1)

            def out_deviation(b):
                act.wait_ge(L.s["o_sum"], L.at["o_sum"] + b + 1)
                act.activation(stats[:, 0, 16 * b:16 * b + 16], stats[:, 2, 16 * b:16 * b + 16], ACT.Sqrt,
                               bias=eps[:, 1:2], scale=1.0 / C).then_inc(L.s["o_std"], 1)

            for t in range(TRI_LN + LN_STEPS if after else S // 4 + 2):
                if t < S // 4:
                    act.wait_ge(L.s["kt_ps"], L.at["kt_ps"] + t + 1)
                    act.activation(ZT[:, 4 * t:4 * t + 4, :], bank(t % 2), ACT.Copy).then_inc(L.s["kt"], 1)
                if 1 <= t <= S // 4:
                    out_square(t - 1)
                if 2 <= t < S // 4 + 2:
                    out_deviation(t - 2)
                if after:
                    ln_act_step(act, after, t - TRI_LN)

        def tri_dve(dve, L, after, between={}):
            to_ab = AB[:, :].rearrange("p (a c g s) -> p a g s c", a=2, c=C, g=G)
            for s in range(S):
                if s in between:
                    between[s](dve)
                dve.wait_ge(L.s["sig"], L.at["sig"] + s + 1)
                lin = bank(KB[s % 4])[:, LIN:].rearrange("p (a g c) -> p a g c", a=2, g=G)
                sig = SIG[:, s % 2, :].rearrange("p (a g c) -> p a g c", a=2, g=G)
                if L is t1:
                    if s >= 2:
                        dve.wait_ge(L.s["ab"], L.at["ab"] + s - 1)
                    dst = TMP[:, s % 2, 0:LIN].rearrange("p (a g c) -> p a g c", a=2, g=G)
                else:
                    dst = to_ab[:, :, :, s, :]
                dve.tensor_tensor(dst, lin, sig, ALU.mult).then_inc(L.s["lin"], 1)
            if L is t0:
                for b in range(1, C // 4, 2):
                    turn_copy(dve, L, b, AT[:, 4 * b:4 * b + 4, :], "at_dve", "at_ps")
            for b in range(1, C // 4, 2):
                k_copy(dve, L, b)

            def out_sum(b):
                dve.wait_ge(L.s["o_sq"], L.at["o_sq"] + b + 1)
                dve.tensor_reduce(stats[:, 2, 16 * b:16 * b + 16],
                                  SQR[:, b * BANK:(b + 1) * BANK].rearrange("p (n c) -> p n c", c=C), AX.X, ALU.add)\
                    .then_inc(L.s["o_sum"], 1)

            def out_inverse(b):
                dve.wait_ge(L.s["o_std"], L.at["o_std"] + b + 1)
                dve.reciprocal(stats[:, 3, 16 * b:16 * b + 16], stats[:, 0, 16 * b:16 * b + 16]).then_inc(L.s["o_rstd"], 1)

            def out_gate(b):
                dve.wait_ge(L.s["o_rg"], L.at["o_rg"] + b + 1)
                if b >= 2:
                    dve.wait_ge(L.s["done"], L.at["done"] + b - 1)
                dve.tensor_tensor(TMP[:, b % 2, 0:BANK].rearrange("p (s f) -> p s f", s=4), o_bank(b)[:, :, 0, :],
                                  GATE[:, b * BANK:(b + 1) * BANK].rearrange("p (s f) -> p s f", s=4), ALU.mult)\
                    .then_inc(L.s["o_mul"], 1)

            for t in range(TRI_LN + LN_STEPS if after else S // 4 + 4):
                if 4 <= t < S // 4 + 4:
                    out_gate(t - 4)
                if 3 <= t < S // 4 + 3:
                    out_inverse(t - 3)
                if 2 <= t < S // 4 + 2:
                    out_sum(t - 2)
                if after:
                    ln_dve_step(dve, after, t - TRI_LN)

        def tri_pool(pool, L, after):
            X4 = blocks(L.src)
            XB = L.scratch
            if L is t1:
                to_ab = AB[:, :].rearrange("p (a c g s) -> p a g s c", a=2, c=C, g=G)
                m = mask[:, :].rearrange("p (g s) -> p g s", g=G)
                for s in range(S):
                    pool.wait_ge(L.s["lin"], L.at["lin"] + s + 1)
                    pool.tensor_tensor(to_ab[:, :, :, s, :],
                                       TMP[:, s % 2, 0:LIN].rearrange("p (a g c) -> p a g c", a=2, g=G),
                                       m[:, :, s].unsqueeze(1).unsqueeze(3).to_broadcast([N, 2, G, C]), ALU.mult)\
                        .then_inc(L.s["ab"], 1)
            for b in range(S // 4):
                cols = slice(b * BANK, (b + 1) * BANK)
                pool.wait_ge(L.s["gate"], L.at["gate"] + b + 1)
                pool.tensor_tensor(XB[:, cols].rearrange("p (n c) -> p n c", c=C),
                                   GATE[:, cols].rearrange("p (n c) -> p n c", c=C),
                                   bo[L.name][:, :].unsqueeze(1).to_broadcast([N, 16, C]), ALU.mult)\
                    .then_inc(L.s["xg"], 1)
                pool.wait_ge(L.s["xg"], L.at["xg"] + b + 1)
                pool.tensor_tensor(XB[:, cols].rearrange("p (s g c) -> p s g c", s=4, g=G),
                                   XB[:, cols].rearrange("p (s g c) -> p s g c", s=4, g=G),
                                   X4[:, :, 4 * b:4 * b + 4, :].rearrange("p g s c -> p s g c"), ALU.add)\
                    .then_inc(L.s["xb"], 1)
            pool.wait_ge(L.s["xb"], L.at["xb"] + S // 4)
            for t in range(TRI_LN + LN_STEPS if after else S // 4 + 4):
                b = t - 3
                if 0 <= b < S // 4:
                    pool.wait_ge(L.s["o_rstd"], L.at["o_rstd"] + b + 1)
                    g = GATE[:, b * BANK:(b + 1) * BANK].rearrange("p (n c) -> p n c", c=C)
                    pool.tensor_tensor(g, g, stats[:, 3, 16 * b:16 * b + 16].unsqueeze(2).to_broadcast([N, 16, C]),
                                       ALU.mult).then_inc(L.s["o_rg"], 1)
                b = t - 4
                if 0 <= b < S // 4:
                    pool.wait_ge(L.s["o_mul"], L.at["o_mul"] + b + 1)
                    pool.tensor_tensor(X4[:, :, 4 * b:4 * b + 4, :].rearrange("p g s c -> p s g c"),
                                       XB[:, b * BANK:(b + 1) * BANK].rearrange("p (s g c) -> p s g c", s=4, g=G),
                                       TMP[:, b % 2, 0:BANK].rearrange("p (s g c) -> p s g c", s=4, g=G), ALU.add)\
                        .then_inc(L.s["done"], 1)
                if after:
                    ln_pool_step(pool, after, t - TRI_LN)

        def turn_x_pe(pe, V):
            src = V.src[:, :].rearrange("p (n c) -> p c n", c=C)
            wait_all(pe, V.ready)
            for b in range(C // 4):
                if b >= 4:
                    pe.wait_ge(V.s["dve" if b % 2 else "act"], V.at["dve" if b % 2 else "act"] + b // 2 - 1)
                for k in range(4):
                    m = pe.transpose(bank(b % 4)[:, k * N:(k + 1) * N], src[:, 4 * b + k, :], ident[:, :])
                m.then_inc(V.s["ps"], 1)

        def turn_x_copy(eng, V, odd):
            dst = V.dst[:, :].rearrange("p (n c) -> p c n", c=C)
            for b in range(odd, C // 4, 2):
                eng.wait_ge(V.s["ps"], V.at["ps"] + b + 1)
                src = bank(b % 4).rearrange("p (c n) -> p c n", c=4)
                if odd:
                    eng.tensor_copy(dst[:, 4 * b:4 * b + 4, :], src).then_inc(V.s["dve"], 1)
                else:
                    eng.activation(dst[:, 4 * b:4 * b + 4, :], src, ACT.Copy).then_inc(V.s["act"], 1)
        LOG = AB[:, 0:SEGT + K0]
        REPL = AB[:, SEGT + K0:2 * (SEGT + K0)]
        PROB = SQR[:, 0:SEGT]
        WGT = SQR[:, SEGT:2 * SEGT]
        WT = GATE[:, 0:SEGI * N].rearrange("p (i f) -> p i f", i=SEGI)
        PM = TMP[:, 0, 0:SEG * C].rearrange("p (s c) -> p s c", s=SEG)
        top = sb("top", [N, 6, K0])
        cand = sb("cand", [E0, 4, SEG * K0 + 1])
        small = sb("small", [N, 16])
        pool32 = sb("pool32", [N, C])
        w1 = sb("w1", [C + 1, E0, H0])
        w2 = sb("w2", [H0, E0, C])
        w2l = sb("w2l", [C, E0])
        hid = sb("hid", [N, 2, E0])
        o2 = sb("o2", [C, SEG, E0])
        outm = sb("outm", [N, SEG, C])

        def f0_weights_dve(dve):
            v = gw[:, :, :].rearrange("p q (b r e) -> p q b r e", b=G, r=2)
            for q in range(2):
                dve.tensor_tensor(v[:, q, :, q, :], pcol("gate").unsqueeze(1).to_broadcast([GC, G, E0]),
                                  m4[:, :].unsqueeze(2).to_broadcast([GC, G, E0]), ALU.mult).then_inc(f0.s["w_dve"], 1)

        def f0_pe(pe):
            L = f0
            turn_all_z_pe(pe, L)
            pe.wait_ge(L.s["zt"], L.at["zt"] + S // 4)
            pe.wait_ge(L.s["w_dve"], L.at["w_dve"] + 2)
            for b in range(4):
                for q in range(2):
                    m = pe.matmul(bank(2 + b), gw[:, q, :], ZT[:, 16 * q + 4 * b:16 * q + 4 * b + 4, :],
                                  start=(q == 0), stop=(q == 1))
                m.then_inc(L.s["lg_ps"], 1)
            pe.wait_ge(L.s["top"], L.at["top"] + 1)
            for s in range(SEG):
                m = pe.matmul(bank(6)[0:E0, s * K0:(s + 1) * K0], ident[:, s * E0:(s + 1) * E0], top[:, 0, :],
                              start=True, stop=True)
            m.then_inc(L.s["cand_ps"], 1)
            pe.wait_ge(L.s["fin"], L.at["fin"] + 4)
            pe.matmul(bank(7)[:, 0:SEG * K0 + 1], e16[:, :, :], cand[:, 3, :], start=True, stop=True)\
                .then_inc(L.s["mk_ps"], 1)
            pe.wait_ge(L.s["lg_act"], L.at["lg_act"] + 4)
            later_weights_pe(pe)
            pe.wait_ge(L.s["exp"], L.at["exp"] + 1)
            pe.matmul(bank(6)[:, 256:257], same16[:, :, :], small[:, 1:2], start=True, stop=True)\
                .then_inc(L.s["tot_ps"], 1)
            pe.wait_ge(L.s["w"], L.at["w"] + 1)
            for b in range(SEGI // 4):
                if b >= 2:
                    pe.wait_ge(L.s["wt_dve" if b % 2 else "wt_act"], L.at["wt_dve" if b % 2 else "wt_act"] + b // 2)
                for k in range(4):
                    i = 4 * b + k
                    m = pe.transpose(bank(b % 2)[:, k * N:(k + 1) * N], WGT[:, i * N:(i + 1) * N], ident[:, :])
                m.then_inc(L.s["wt_ps"], 1)
            pe.wait_ge(L.s["wt_act"], L.at["wt_act"] + 2)
            pe.wait_ge(L.s["wt_dve"], L.at["wt_dve"] + 2)
            zi = Z[:, :].rearrange("p (r i g c) -> p i g r c", r=2, i=SEGI, g=G)
            for i in range(SEGI):
                m = pe.matmul(bank(7)[:, 128:128 + SEG * C], WT[:, i, :], zi[:, i], start=(i == 0), stop=(i == SEGI - 1))
            m.then_inc(L.s["pool_ps"], 1)
            pe.wait_ge(L.s["pl"], L.at["pl"] + 2)
            pe.matmul(bank(6)[0:C, 264:264 + E0], pool32[:, :], d16[:, :], start=True, stop=True).then_inc(L.s["plt_ps"], 1)
            pe.wait_ge(L.s["plt"], L.at["plt"] + 1)
            pe.wait_ge(L.s["pad"], L.at["pad"] + 2)
            pe.wait_ge(par_in, PAR_LOADS)
            for e in range(E0):
                m = pe.matmul(bank(6)[:, 288 + e:289 + e], w1[:, e, :], hid[0:C + 1, 0, e:e + 1], start=True, stop=True)
            m.then_inc(L.s["h_ps"], 1)
            pe.wait_ge(L.s["h"], L.at["h"] + 1)
            for e in range(E0):
                m = pe.matmul(bank(6)[0:C, 320 + e:321 + e], w2[:, e, :], hid[:, 1, e:e + 1], start=True, stop=True)
            m.then_inc(L.s["o_ps"], 1)
            pe.wait_ge(L.s["plt"], L.at["plt"] + 2)
            pe.matmul(bank(6)[:, 352:352 + C], o2[:, :, :], ident[0:C, 0:C], start=True, stop=True).then_inc(L.s["outm_ps"], 1)
            pe.wait_ge(L.s["outm"], L.at["outm"] + 1)
            for V in (t1, t3):
                pe.wait_ge(V.s["w_dve"], V.at["w_dve"] + TRI_W)
            for b in range(SEGI // 2):
                if b >= 4:
                    pe.wait_ge(L.s["done"], L.at["done"] + b - 3)
                for k in range(2):
                    i = 2 * b + k
                    m = pe.matmul(bank(b % 4)[:, k * SEG * C:(k + 1) * SEG * C], WGT[:, i * N:(i + 1) * N],
                                  outm[:, :, :], start=True, stop=True)
                m.then_inc(L.s["y_ps"], 1)

        def f0_act(act):
            L = f0
            warm_table(act, ACT.Exp)
            for b in range(4):
                act.wait_ge(L.s["lg_ps"], L.at["lg_ps"] + b + 1)
                act.activation(LOG[:, b * BANK:(b + 1) * BANK], bank(2 + b), ACT.Identity, bias=pcol("gate_b"))\
                    .then_inc(L.s["lg_act"], 1)
            act.wait_ge(L.s["mk"], L.at["mk"] + 2)
            act.activation(PROB, LOG[:, 0:SEGT], ACT.Exp, bias=small[:, 0:1], accum_out=small[:, 1:2])\
                .then_inc(L.s["exp"], 1)
            warm_table(act, ACT.Gelu)
            for b in range(0, SEGI // 4, 2):
                act.wait_ge(L.s["wt_ps"], L.at["wt_ps"] + b + 1)
                act.activation(WT[:, 4 * b:4 * b + 4, :], bank(b % 2), ACT.Copy).then_inc(L.s["wt_act"], 1)
            act.wait_ge(L.s["h_ps"], L.at["h_ps"] + 1)
            act.activation(hid[:, 1, :], bank(6)[:, 288:288 + E0], ACT.Gelu).then_inc(L.s["h"], 1)

        def f0_pool(pool):
            pool.memset(LOG[:, SEGT:], -FAR).then_inc(f0.s["pad"], 1)
            pool.wait_ge(f0.s["pad"], 1)
            pool.memset(hid[C:C + 1, 0, :], 1.0).then_inc(f0.s["pad"], 1)
            pool.wait_ge(f0.s["pad"], 2)

        def f0_dve(dve):
            L = f0
            dve.wait_ge(L.s["lg_act"], L.at["lg_act"] + 4)
            dve.wait_ge(L.s["pad"], L.at["pad"] + 2)
            dve.max(top[:, 0, :], LOG[:, 0:SEGT]).then_inc(L.s["top"], 1)
            dve.wait_ge(L.s["cand_ps"], L.at["cand_ps"] + 1)
            nk = SEG * K0
            dve.tensor_copy(cand[:, 0, 0:nk], bank(6)[0:E0, 0:nk]).then_inc(L.s["cand"], 1)
            dve.wait_ge(L.s["cand"], L.at["cand"] + 1)
            dve.max(cand[:, 1, 0:K0], cand[:, 0, 0:nk]).then_inc(L.s["fin"], 1)
            dve.wait_ge(L.s["fin"], L.at["fin"] + 1)
            dve.match_replace(out=cand[:, 2, 0:nk], in_to_replace=cand[:, 1, 0:K0], in_values=cand[:, 0, 0:nk],
                              imm_value=-3.0 * FAR).then_inc(L.s["fin"], 1)
            dve.wait_ge(L.s["fin"], L.at["fin"] + 2)
            dve.tensor_tensor(cand[:, 3, 0:nk], cand[:, 2, 0:nk], cand[:, 0, 0:nk], ALU.not_equal).then_inc(L.s["fin"], 1)
            dve.tensor_copy(cand[:, 3, nk:nk + 1], cand[:, 1, 0:1]).then_inc(L.s["fin"], 1)
            dve.wait_ge(L.s["mk_ps"], L.at["mk_ps"] + 1)
            seg = TMP[:, 1, 0:nk].rearrange("p (s k) -> p s k", s=SEG)
            dve.tensor_tensor(seg, bank(7, nk).rearrange("p (s k) -> p s k", s=SEG),
                              m8[:, :].unsqueeze(2).to_broadcast([N, SEG, K0]), ALU.mult).then_inc(L.s["mk"], 1)
            dve.tensor_scalar(small[:, 0:1], bank(7)[:, nk:nk + 1], -1.0, None, ALU.mult).then_inc(L.s["mk"], 1)
            dve.wait_ge(L.s["mk"], L.at["mk"] + 2)
            dve.tensor_reduce(top[:, 1, :], seg.rearrange("p s k -> p k s"), AX.X, ALU.add).then_inc(L.s["sel"], 1)
            dve.wait_ge(L.s["sel"], L.at["sel"] + 1)
            dve.tensor_tensor(top[:, 2, :], top[:, 1, :], top[:, 0, :], ALU.mult).then_inc(L.s["sel"], 1)
            dve.tensor_scalar(top[:, 3, :], top[:, 1, :], -1.0, FAR, ALU.add, ALU.mult).then_inc(L.s["sel"], 1)
            dve.wait_ge(L.s["sel"], L.at["sel"] + 3)
            dve.tensor_tensor(top[:, 4, :], top[:, 2, :], top[:, 3, :], ALU.add).then_inc(L.s["sel"], 1)
            dve.wait_ge(L.s["sel"], L.at["sel"] + 4)
            dve.match_replace(out=REPL, in_to_replace=top[:, 4, :], in_values=LOG, imm_value=-3.0 * FAR)\
                .then_inc(L.s["sel"], 1)
            dve.wait_ge(L.s["sel"], L.at["sel"] + 5)
            dve.tensor_tensor(WGT, REPL[:, 0:SEGT], LOG[:, 0:SEGT], ALU.not_equal).then_inc(L.s["sel"], 1)
            dve.wait_ge(L.s["tot_ps"], L.at["tot_ps"] + 1)
            dve.reciprocal(small[:, 2:3], bank(6)[:, 256:257]).then_inc(L.s["tot"], 1)
            dve.wait_ge(L.s["tot"], L.at["tot"] + 1)
            dve.wait_ge(L.s["sel"], L.at["sel"] + 6)
            dve.scalar_tensor_tensor(out=WGT, in0=WGT, scalar=small[:, 2:3], in1=PROB, op0=ALU.mult, op1=ALU.mult)\
                .then_inc(L.s["w"], 1)
            for b in range(1, SEGI // 4, 2):
                dve.wait_ge(L.s["wt_ps"], L.at["wt_ps"] + b + 1)
                dve.tensor_copy(WT[:, 4 * b:4 * b + 4, :], bank(b % 2)).then_inc(L.s["wt_dve"], 1)
            later_weights_dve(dve)
            dve.wait_ge(L.s["pool_ps"], L.at["pool_ps"] + 1)
            own = m8[:, :].unsqueeze(2).to_broadcast([N, SEG, C])
            dve.tensor_tensor(PM, bank(7)[:, 128:128 + SEG * C].rearrange("p (s c) -> p s c", s=SEG), own, ALU.mult)\
                .then_inc(L.s["pl"], 1)
            dve.wait_ge(L.s["pl"], L.at["pl"] + 1)
            dve.tensor_reduce(pool32[:, :], PM.rearrange("p s c -> p c s"), AX.X, ALU.add).then_inc(L.s["pl"], 1)
            dve.wait_ge(L.s["plt_ps"], L.at["plt_ps"] + 1)
            dve.tensor_copy(hid[0:C, 0, :], bank(6)[0:C, 264:264 + E0]).then_inc(L.s["plt"], 1)
            dve.wait_ge(L.s["o_ps"], L.at["o_ps"] + 1)
            dve.tensor_tensor(o2[:, :, :], bank(6)[0:C, 320:320 + E0].unsqueeze(1).to_broadcast([C, SEG, E0]),
                              w2l[:, :].unsqueeze(1).to_broadcast([C, SEG, E0]), ALU.add).then_inc(L.s["plt"], 1)
            dve.wait_ge(L.s["outm_ps"], L.at["outm_ps"] + 1)
            dve.tensor_tensor(outm[:, :, :], bank(6)[:, 352:352 + C].unsqueeze(1).to_broadcast([N, SEG, C]), own, ALU.mult)\
                .then_inc(L.s["outm"], 1)
            xi = XC[:, :].rearrange("p (s i c) -> p i s c", s=SEG, i=SEGI)
            for b in range(SEGI // 2):
                dve.wait_ge(L.s["y_ps"], L.at["y_ps"] + b + 1)
                for k in range(2):
                    x = xi[:, 2 * b + k]
                    i = dve.tensor_tensor(x, x, bank(b % 4)[:, k * SEG * C:(k + 1) * SEG * C]
                                          .rearrange("p (s c) -> p s c", s=SEG), ALU.add)
                i.then_inc(L.s["done"], 1)

        Y = AB[:, 0:NC + 1]
        starts = Y[:, 0:NC:CHUNK]
        old = sb("old", [GC, 2, NCH])
        bns = sb("bns", [GC, 8, 6])
        mv = sb("mv", [GC, 12])
        flag_f = sb("flag_f", [1, 2])
        flag_i = sb("flag_i", [1, 1], I32)
        wbn = sb("wbn", [GC, GC])
        wbnt = sb("wbnt", [GC, GC])
        rec_w = {}
        for L in (r1, r2):
            rec_w[L.name] = {k: sb(f"{L.name}_{k}", [GC, GC]) for k in ("wbd", "wraw", "vt")}
            rec_w[L.name] |= {"wbn": wbn, "wbnt": wbnt}

        def rec_weights1_dve(dve, L):
            W = rec_w[L.name]
            for name, key in (("W", "wbd"), ("VT", "vt")):
                dve.tensor_tensor(W[key][:, :].rearrange("p (g c) -> p g c", g=G),
                                  pcol(f"{L.name}_{name}").unsqueeze(1).to_broadcast([GC, G, C]),
                                  m4[:, :].unsqueeze(2).to_broadcast([GC, G, C]), ALU.mult).then_inc(L.s["w_half"], 1)

        def rec_weights2_dve(dve, L):
            dve.wait_ge(L.s["w_pe"], L.at["w_pe"] + 1)
            dve.tensor_copy(rec_w[L.name]["wraw"][:, :], bank(L.wbank)[:, L.wcol:L.wcol + GC]).then_inc(L.s["w_dve"], 1)

        def rec_weights_pe(pe, L):
            pe.wait_ge(L.s["w_half"], L.at["w_half"] + 2)
            pe.transpose(bank(L.wbank)[:, L.wcol:L.wcol + GC], rec_w[L.name]["wbd"][:, :], ident[:, :])\
                .then_inc(L.s["w_pe"], 1)

        ztk = ZT[:, :, :].rearrange("p s f -> p (s f)")

        def chunks(t, off, h):
            return t[:, bass.ds(off + h * NS * CHUNK, NS, CHUNK)]

        def rec_step(pe, L, off, k, h):
            W, o = rec_w[L.name], bank(2 * h + k, NS)
            return (pe.matmul(o, W["wbnt"][:, :], chunks(ztk, off, h), start=True, stop=False),
                    lambda: pe.matmul(o, W["vt"][:, :], chunks(Y, off, h), start=False, stop=True))

        def rec_pe(pe, L):
            W = rec_w[L.name]
            pe.wait_ge(L.s["w_dve"], L.at["w_dve"] + 1)
            for b in range(-1, 8):
                if b < 7:
                    turn_z_pe(pe, L, b + 1)
                if b < 0:
                    continue
                if b == 0:
                    wait_all(pe, L.banks_free)
                pe.wait_ge(L.s["zt"], L.at["zt"] + b + 1)
                if b >= 4:
                    pe.wait_ge(L.s["wx"], L.at["wx"] + b - 3)
                pe.matmul(bank(2 + b % 4), W["wraw"][:, :], ZT[:, 4 * b:4 * b + 4, :], start=True, stop=True)\
                    .then_inc(L.s["wx_ps"], 1)
            same = same32[:, :, :]
            pe.wait_ge(L.s["bn"], L.at["bn"] + 1)
            pe.matmul(bank(6)[:, 0:1], same, mv[:, 0:1], start=True, stop=True).then_inc(L.s["bn_ps"], 1)
            pe.wait_ge(L.s["bn"], L.at["bn"] + 4)
            pe.matmul(bank(7)[:, 0:1], same, mv[:, 4:5], start=True, stop=True).then_inc(L.s["bn_ps"], 1)
            pe.wait_ge(L.s["bnw"], L.at["bnw"] + 4)
            pe.transpose(bank(6)[:, 0:GC], W["wbn"][:, :], ident[:, :]).then_inc(L.s["bn_ps"], 1)
            pe.wait_ge(L.s["bnw"], L.at["bnw"] + 5)
            for r, (first, steps, before) in enumerate(ROUNDS):
                if r >= 1:
                    for h in range(STREAMS):
                        pe.wait_ge(L.s[f"step_y{h}"], L.at[f"step_y{h}"] + before + 1)
                    pe.matmul(bank(4, 1), shift[:, :], Y[:, NC:NC + 1], start=True, stop=True)\
                        .then_inc(L.s["edge_ps"], 1)
                    pe.wait_ge(L.s["edge"], L.at["edge"] + 2 * r)
                with pe.Fori(0, steps // 2) as pair:
                    for k in range(2):
                        for h in range(STREAMS):
                            _, recur = rec_step(pe, L, pair * 2 + (first + k), k, h)
                            pe.wait_ge(L.s[f"step_y{h}"], pair * 2 + (L.at[f"step_y{h}"] + before + k + 1))
                            recur().then_inc(L.s["step_ps"], 1)
            for h in range(STREAMS):
                pe.wait_ge(L.s[f"step_y{h}"], L.at[f"step_y{h}"] + STEPS + 1)
            pe.matmul(bank(4, 1), shift[:, :], Y[:, NC:NC + 1], start=True, stop=True).then_inc(L.s["edge_ps"], 1)
            pe.wait_ge(L.s["chk"], L.at["chk"] + 3)
            pe.transpose(bank(5)[0:1, 0:GC], mv[:, 10:11], ident[:, :]).then_inc(L.s["chk_ps"], 1)
            pe.wait_ge(L.s["flag"], L.at["flag"] + 3)
            differs = pe.value_load(flag_i[0:1, 0:1], min_val=0, max_val=1)
            with pe.If(differs != 0):
                with pe.Fori(0, GENERAL_ROUNDS) as r:
                    for h in range(STREAMS):
                        pe.wait_ge(L.s[f"g_y{h}"], r * CHUNK + (L.at[f"g_y{h}"] + 1))
                    pe.matmul(bank(4, 1), shift[:, :], Y[:, NC:NC + 1], start=True, stop=True)\
                        .then_inc(L.s["g_edge_ps"], 1)
                    with pe.Fori(0, CHUNK // 2) as pair:
                        for k in range(2):
                            for h in range(STREAMS):
                                if k == h == 0:
                                    pe.wait_ge(L.s["g_edge"], L.at["g_edge"] + r + 1)
                                _, recur = rec_step(pe, L, pair * 2 + k, k, h)
                                pe.wait_ge(L.s[f"g_y{h}"], r * CHUNK + pair * 2 + (L.at[f"g_y{h}"] + k + 1))
                                recur().then_inc(L.s["g_ps"], 1)
                for h in range(STREAMS):
                    pe.wait_ge(L.s[f"g_y{h}"], L.at[f"g_y{h}"] + GENERAL_ROUNDS * CHUNK + 1)
            for b in range(S // 4):
                if b >= 4:
                    pe.wait_ge(L.s["done"], L.at["done"] + b - 3)
                for k in range(4):
                    s = 4 * b + k
                    m = pe.transpose(bank(4 + b % 4)[:, k * N:(k + 1) * N], Y[:, 1 + s * N:1 + (s + 1) * N], ident[:, :])
                m.then_inc(L.s["y_ps"], 1)

        def rec_act(act, L):
            act.wait_ge(L.s["bnc"], L.at["bnc"] + 1)
            act.activation(mv[:, 6:7], mv[:, 5:6], ACT.Sqrt, bias=eps[:, 1:2]).then_inc(L.s["std1"], 1)
            warm_table(act, ACT.Sigmoid)
            act.wait_ge(L.s["bnw"], L.at["bnw"] + 3)
            bias = mv[:, 9:10]
            for first, steps, before in ROUNDS:
                with act.Fori(0, steps // 2) as pair:
                    for k in range(2):
                        for h in range(STREAMS):
                            act.wait_ge(L.s["step_ps"], pair * 4 + (L.at["step_ps"] + 2 * (before + k) + h + 1))
                            act.activation(chunks(Y, pair * 2 + (first + k + 1), h), bank(2 * h + k, NS), ACT.Sigmoid,
                                           bias=bias).then_inc(L.s[f"step_y{h}"], 1)
            act.wait_ge(L.s["flag"], L.at["flag"] + 3)
            differs = act.value_load(flag_i[0:1, 0:1], min_val=0, max_val=1)
            with act.If(differs != 0):
                with act.Fori(0, GENERAL_ROUNDS) as r:
                    with act.Fori(0, CHUNK // 2) as pair:
                        for k in range(2):
                            for h in range(STREAMS):
                                act.wait_ge(L.s["g_ps"], r * (2 * CHUNK) + pair * 4 + (L.at["g_ps"] + 2 * k + h + 1))
                                act.activation(chunks(Y, pair * 2 + (k + 1), h), bank(2 * h + k, NS), ACT.Sigmoid,
                                               bias=bias).then_inc(L.s[f"g_y{h}"], 1)

        def rec_pool(pool, L):
            pool.wait_ge(L.s["z"], L.at["z"] + Q)
            for h in range(STREAMS):
                pool.memset(chunks(Y, CHUNK - WARM, h), 0.0).then_inc(L.s[f"step_y{h}"], 1)

        def set_flag(dve, L, differences):
            dve.wait_ge(L.s["chk_ps"], L.at["chk_ps"] + 1)
            dve.tensor_reduce(flag_f[:, 0:1], differences, AX.X, ALU.max).then_inc(L.s["flag"], 1)
            dve.wait_ge(L.s["flag"], L.at["flag"] + 1)
            dve.tensor_scalar(flag_f[:, 1:2], flag_f[:, 0:1], FIXED_TOL, None, ALU.is_gt).then_inc(L.s["flag"], 1)
            dve.wait_ge(L.s["flag"], L.at["flag"] + 2)
            dve.tensor_copy(flag_i[:, :], flag_f[:, 1:2]).then_inc(L.s["flag"], 1)

        def rec_dve(dve, L, after):
            W = rec_w[L.name]
            for b in range(8):
                dve.wait_ge(L.s["wx_ps"], L.at["wx_ps"] + b + 1)
                dve.bn_stats(bns[:, b, :], bank(2 + b % 4)).then_inc(L.s["wx"], 1)
            dve.wait_ge(L.s["wx"], L.at["wx"] + 8)
            dve.bn_aggr(mv[:, 0:2], bns[:, :, :].rearrange("p b k -> p (b k)")).then_inc(L.s["bn"], 1)
            dve.wait_ge(L.s["bn_ps"], L.at["bn_ps"] + 1)
            dve.wait_ge(L.s["bn"], L.at["bn"] + 1)
            dve.tensor_tensor(mv[:, 2:3], mv[:, 0:1], bank(6, 1), ALU.subtract).then_inc(L.s["bn"], 1)
            dve.wait_ge(L.s["bn"], L.at["bn"] + 2)
            dve.tensor_tensor(mv[:, 3:4], mv[:, 2:3], mv[:, 2:3], ALU.mult).then_inc(L.s["bn"], 1)
            dve.wait_ge(L.s["bn"], L.at["bn"] + 3)
            dve.tensor_tensor(mv[:, 4:5], mv[:, 3:4], mv[:, 1:2], ALU.add).then_inc(L.s["bn"], 1)
            dve.wait_ge(L.s["bn_ps"], L.at["bn_ps"] + 2)
            dve.tensor_copy(mv[:, 5:6], bank(7, 1)).then_inc(L.s["bnc"], 1)
            dve.wait_ge(L.s["std1"], L.at["std1"] + 1)
            dve.reciprocal(mv[:, 7:8], mv[:, 6:7]).then_inc(L.s["bnw"], 1)
            dve.wait_ge(L.s["bnw"], L.at["bnw"] + 1)
            dve.tensor_tensor(mv[:, 8:9], mv[:, 7:8], pcol(f"{L.name}_gamma"), ALU.mult).then_inc(L.s["bnw"], 1)
            dve.wait_ge(L.s["bnw"], L.at["bnw"] + 2)
            dve.tensor_tensor(mv[:, 11:12], bank(6, 1), mv[:, 8:9], ALU.mult).then_inc(L.s["bnc"], 1)
            dve.wait_ge(L.s["bnc"], L.at["bnc"] + 2)
            dve.tensor_tensor(mv[:, 9:10], pcol(f"{L.name}_beta"), mv[:, 11:12], ALU.subtract).then_inc(L.s["bnw"], 1)
            dve.tensor_scalar(W["wbn"][:, :], W["wbd"][:, :], mv[:, 8:9], None, ALU.mult).then_inc(L.s["bnw"], 1)
            dve.wait_ge(L.s["bn_ps"], L.at["bn_ps"] + 3)
            dve.tensor_copy(W["wbnt"][:, :], bank(6, GC)).then_inc(L.s["bnw"], 1)
            dve.wait_ge(L.s["edge_ps"], L.at["edge_ps"] + 1)
            dve.tensor_copy(Y[:, 0:1], bank(4, 1)).then_inc(L.s["edge"], 1)
            dve.wait_ge(L.s["edge"], L.at["edge"] + 1)
            dve.tensor_copy(old[:, 0, :], starts).then_inc(L.s["edge"], 1)
            dve.wait_ge(L.s["edge_ps"], L.at["edge_ps"] + 2)
            dve.tensor_copy(Y[:, 0:1], bank(4, 1)).then_inc(L.s["chk"], 1)
            dve.wait_ge(L.s["chk"], L.at["chk"] + 1)
            dve.tensor_tensor(old[:, 1, :], old[:, 0, :], starts, ALU.subtract).then_inc(L.s["chk"], 1)
            dve.wait_ge(L.s["chk"], L.at["chk"] + 2)
            dve.tensor_reduce(mv[:, 10:11], old[:, 1, :], AX.X, ALU.max, apply_absolute_value=True)\
                .then_inc(L.s["chk"], 1)
            set_flag(dve, L, bank(5)[0:1, 0:GC])
            for h in range(STREAMS):
                dve.engine_nop().then_inc(L.s[f"g_y{h}"], 1)
            dve.wait_ge(L.s["flag"], L.at["flag"] + 3)
            differs = dve.value_load(flag_i[0:1, 0:1], min_val=0, max_val=1)
            with dve.If(differs != 0):
                with dve.Fori(0, GENERAL_ROUNDS) as r:
                    dve.wait_ge(L.s["g_edge_ps"], L.at["g_edge_ps"] + r + 1)
                    dve.tensor_copy(Y[:, 0:1], bank(4, 1)).then_inc(L.s["g_edge"], 1)
            X4 = blocks(XC)
            for b in range(1 + LN_STEPS if after else S // 4):
                if b < S // 4:
                    dve.wait_ge(L.s["y_ps"], L.at["y_ps"] + b + 1)
                    x = X4[:, :, 4 * b:4 * b + 4, :].rearrange("p g s c -> p s g c")
                    dve.tensor_tensor(x, x, bank(4 + b % 4).rearrange("p (s g c) -> p s g c", s=4, g=G), ALU.add)\
                        .then_inc(L.s["done"], 1)
                if after:
                    ln_dve_step(dve, after, b - 1)

        NB = N // G
        ROWB = NB + 2
        RIN = GATE[:, :].rearrange("p (i n) -> p i n", i=N)
        SCN = AB[:, 0:(N + 1) * ROWB].rearrange("p (i n) -> p i n", n=ROWB)
        ends = SCN[:, 0:N:CHUNK, 1:1 + NB]
        kept = TMP[:, 0, 0:ROWCH * NB].rearrange("p (k n) -> p k n", n=NB)
        differ = TMP[:, 1, 0:ROWCH * NB]
        toep = sb("toep", [GC, 3, G, C])

        def scan_weights_pool(pool):
            pool.memset(toep[:, :, :, :], 0.0).then_inc(sc.s["w_dve"], 1)
            pool.wait_ge(sc.s["w_dve"], sc.at["w_dve"] + 1)
            pool.wait_ge(par_first, PAR_FIRST)
            a = PAR["conv"][0]
            for m in range(G):
                for b in range(3):
                    for mo in range(G):
                        tap = TAPS // 2 + G * (b - 1) + m - mo
                        if 0 <= tap < TAPS:
                            pool.tensor_copy(toep[m * C:(m + 1) * C, b, mo, :],
                                             par[m * C:(m + 1) * C, a + tap * C:a + (tap + 1) * C])\
                                .then_inc(sc.s["w_pool"], 1)
            pool.wait_ge(sc.s["w_pool"], SCAN_COPIES)

        def scan_rows(t, off, h):
            return t[:, bass.ds(off + h * ROWS_S * CHUNK, ROWS_S, CHUNK), :]

        def scan_pool(pool):
            L = sc
            pool.wait_ge(L.s["z"], L.at["z"] + Q)
            pool.memset(SCN[:, 0, :], 0.0).then_inc(L.s["pads"], 1)
            pool.memset(SCN[:, 1:, 0:ROWB:ROWB - 1], 0.0).then_inc(L.s["pads"], 1)
            pool.wait_ge(L.s["zt"], L.at["zt"] + NB // 4)
            for h in range(STREAMS):
                pool.tensor_copy(scan_rows(SCN[:, :, 1:1 + NB], CHUNK - WARM, h), scan_rows(RIN, CHUNK - WARM - 1, h))\
                    .then_inc(L.s[f"row{h}"], 1)

        def scan_pe(pe):
            L = sc
            turn_all_z_pe(pe, L)
            pe.wait_ge(L.s["pads"], L.at["pads"] + 2)
            pe.wait_ge(L.s["w_pool"], L.at["w_pool"] + SCAN_COPIES)

            def step(off, h):
                for b in range(3):
                    m = pe.matmul(bank(2 + h, ROWS_S * NB), toep[:, b, :, :], scan_rows(SCN[:, :, b:b + NB], off, h),
                                  start=(b == 0), stop=(b == 2))
                return m

            for r, (first, steps, before) in enumerate(ROUNDS):
                if r >= 1:
                    for h in range(STREAMS):
                        pe.wait_ge(L.s[f"row{h}"], L.at[f"row{h}"] + before + 1)
                    pe.wait_ge(L.s["kept"], L.at["kept"] + 1)
                with pe.Fori(0, steps // 2) as pair:
                    for k in range(2):
                        for h in range(STREAMS):
                            pe.wait_ge(L.s[f"row{h}"], pair * 2 + (L.at[f"row{h}"] + before + k + 1))
                            step(pair * 2 + (first + k), h).then_inc(L.s["conv"], 1)
            pe.wait_ge(L.s["chk"], L.at["chk"] + 2)
            pe.transpose(bank(1)[0:1, 0:GC], mv[:, 10:11], ident[:, :]).then_inc(L.s["chk_ps"], 1)
            pe.wait_ge(L.s["flag"], L.at["flag"] + 3)
            differs = pe.value_load(flag_i[0:1, 0:1], min_val=0, max_val=1)
            with pe.If(differs != 0):
                with pe.Fori(0, GENERAL_SCANS) as r:
                    with pe.Fori(0, CHUNK // 2) as pair:
                        for k in range(2):
                            for h in range(STREAMS):
                                if k == h == 0:
                                    pe.wait_ge(L.s["g_row1"], r * CHUNK + (L.at["g_row1"] + 1))
                                pe.wait_ge(L.s[f"g_row{h}"], r * CHUNK + pair * 2 + (L.at[f"g_row{h}"] + k + 1))
                                step(pair * 2 + k, h).then_inc(L.s["g_conv"], 1)
                for h in range(STREAMS):
                    pe.wait_ge(L.s[f"g_row{h}"], L.at[f"g_row{h}"] + GENERAL_SCANS * CHUNK + 1)
            for b in range(NB // 4):
                if b == 0:
                    for h in range(STREAMS):
                        pe.wait_ge(L.s[f"row{h}"], L.at[f"row{h}"] + STEPS + 1)
                if b >= 4:
                    pe.wait_ge(L.s["done"], L.at["done"] + b - 3)
                for k in range(4):
                    n = 4 * b + k
                    m = pe.transpose(bank(4 + b % 4)[:, k * N:(k + 1) * N], SCN[:, 1:, 1 + n], ident[:, :])
                m.then_inc(L.s["y_ps"], 1)

        def scan_dve(dve):
            L = sc
            dve.wait_ge(L.s["zt"], L.at["zt"] + NB // 4)

            def row_step(off, h):
                return dve.scalar_tensor_tensor(
                    out=scan_rows(SCN[:, :, 1:1 + NB], off + 1, h),
                    in0=bank(2 + h, ROWS_S * NB).rearrange("p (k n) -> p k n", n=NB), scalar=0.0,
                    in1=scan_rows(RIN, off, h), op0=ALU.max, op1=ALU.add)

            for h in range(STREAMS):
                dve.wait_ge(L.s[f"row{h}"], L.at[f"row{h}"] + 1)
            for r, (first, steps, before) in enumerate(ROUNDS):
                if r >= 1:
                    dve.wait_ge(L.s["row0"], L.at["row0"] + before + 1)
                    dve.wait_ge(L.s["row1"], L.at["row1"] + before + 1)
                    dve.tensor_copy(kept, ends).then_inc(L.s["kept"], 1)
                    dve.wait_ge(L.s["kept"], L.at["kept"] + 1)
                with dve.Fori(0, steps // 2) as pair:
                    for k in range(2):
                        for h in range(STREAMS):
                            dve.wait_ge(L.s["conv"], pair * 4 + (L.at["conv"] + 2 * (before + k) + h + 1))
                            row_step(pair * 2 + (first + k), h).then_inc(L.s[f"row{h}"], 1)
            dve.wait_ge(L.s["row0"], L.at["row0"] + STEPS + 1)
            dve.wait_ge(L.s["row1"], L.at["row1"] + STEPS + 1)
            dve.tensor_tensor(differ.rearrange("p (k n) -> p k n", n=NB), kept, ends, ALU.subtract)\
                .then_inc(L.s["chk"], 1)
            dve.wait_ge(L.s["chk"], L.at["chk"] + 1)
            dve.tensor_reduce(mv[:, 10:11], differ, AX.X, ALU.max, apply_absolute_value=True).then_inc(L.s["chk"], 1)
            set_flag(dve, L, bank(1)[0:1, 0:GC])
            for h in range(STREAMS):
                dve.engine_nop().then_inc(L.s[f"g_row{h}"], 1)
            dve.wait_ge(L.s["flag"], L.at["flag"] + 3)
            differs = dve.value_load(flag_i[0:1, 0:1], min_val=0, max_val=1)
            with dve.If(differs != 0):
                with dve.Fori(0, GENERAL_SCANS) as r:
                    with dve.Fori(0, CHUNK // 2) as pair:
                        for k in range(2):
                            for h in range(STREAMS):
                                dve.wait_ge(L.s["g_conv"], r * (2 * CHUNK) + pair * 4 + (L.at["g_conv"] + 2 * k + h + 1))
                                row_step(pair * 2 + k, h).then_inc(L.s[f"g_row{h}"], 1)
            for b in range(NB // 4):
                dve.wait_ge(L.s["y_ps"], L.at["y_ps"] + b + 1)
                x = XR[:, b * BANK:(b + 1) * BANK]
                dve.tensor_tensor(x, x, bank(4 + b % 4), ALU.add).then_inc(L.s["done"], 1)

        wr = sb("wr", [GC, G, E3])
        we = sb("we", [GC, E3, G, C])
        rank = sb("rank", [N, E3])
        NE = N * E3
        RT = [AB[:, k * NE:(k + 1) * NE].rearrange("p (n e) -> p n e", e=E3) for k in range(8)]
        M1, M2, R1M, R2M, DIF, W1S, W2S = (SQR[:, k * N:(k + 1) * N] for k in range(7))
        HALF = Z[:, 0:2 * BANK].rearrange("p (h f) -> p h f", h=2)
        F3_COLS = E3 + E3 * C

        def f3_weights_pool(pool):
            for e in range(E3):
                pool.memset(rank[:, e:e + 1], float(E3 - e)).then_inc(f3.s["rank"], 1)

        def f3_weights_dve(dve):
            L = f3
            dve.wait_ge(L.s["w_pe"], L.at["w_pe"] + 1)
            src = bank(L.wbank)
            dve.tensor_tensor(wr[:, :, :], src[:, 0:E3].unsqueeze(1).to_broadcast([GC, G, E3]),
                              m4[:, :].unsqueeze(2).to_broadcast([GC, G, E3]), ALU.mult).then_inc(L.s["w_dve"], 1)
            w, m = by_groups(src[:, E3:F3_COLS], E3)
            dve.tensor_tensor(we[:, :, :, :], w, m, ALU.mult).then_inc(L.s["w_dve"], 1)

        def f3_weights_pe(pe):
            a, b = PAR["router"][0], ROW["router_b"][0]
            fold_biases(pe, bank(f3.wbank)[:, 0:F3_COLS], par[:, a:a + F3_COLS], row[0:1, b:b + F3_COLS])\
                .then_inc(f3.s["w_pe"], 1)

        def f3_pe(pe):
            L = f3
            turn_all_z_pe(pe, L)
            pe.wait_ge(L.s["w_dve"], L.at["w_dve"] + 2)
            pe.wait_ge(L.s["zt"], L.at["zt"] + S // 4)
            wait_all(pe, L.banks_free)
            for b in range(2):
                for k in range(16):
                    m = pe.matmul(bank(2 + b)[:, k * G * E3:(k + 1) * G * E3], ZT[:, 16 * b + k, :], wr[:, :, :],
                                  start=True, stop=True)
            m.then_inc(L.s["rt_ps"], 1)
            for s in range(S):
                if s == 0:
                    pe.wait_ge(L.s["rt"], L.at["rt"] + 1)
                if s >= 3:
                    pe.wait_ge(L.s["e_mul"], L.at["e_mul"] + s - 2)
                for h in range(2):
                    o = bank(2 + 2 * (s % 3) + h)
                    e = slice(4 * h, 4 * h + 4)
                    m = pe.matmul(o, ZT[:, s, :], we[:, e, :, :], start=True, stop=True)
                m.then_inc(L.s["e_ps"], 1)

        def f3_act(act):
            L = f3
            warm_table(act, ACT.Sigmoid)
            act.wait_ge(L.s["rt_ps"], L.at["rt_ps"] + 1)
            act.activation(RT[0].rearrange("p n e -> p (n e)"), bank(2, n=2), ACT.Copy).then_inc(L.s["rt"], 1)
            act.wait_ge(L.s["diff"], L.at["diff"] + 1)
            act.activation(W1S, DIF, ACT.Sigmoid).then_inc(L.s["sg"], 1)
            act.activation(W2S, DIF, ACT.Sigmoid, scale=-1.0).then_inc(L.s["sg"], 1)

        def f3_dve(dve):
            L = f3
            n = [0]
            sm = L.s["top"]

            def then(ins):
                n[0] += 1
                ins.then_inc(sm, 1)
                dve.wait_ge(sm, n[0])

            def per_e(t):
                return t.unsqueeze(2).to_broadcast([N, N, E3])

            ranks = rank[:, :].unsqueeze(1).to_broadcast([N, N, E3])
            dve.wait_ge(L.s["rank"], L.at["rank"] + E3)
            dve.wait_ge(L.s["rt"], L.at["rt"] + 1)

            def choose(logits, m, rm, hot):
                then(dve.tensor_reduce(m, logits, AX.X, ALU.max))
                then(dve.tensor_tensor(hot, logits, per_e(m), ALU.is_equal))
                then(dve.tensor_tensor(hot, hot, ranks, ALU.mult))
                then(dve.tensor_reduce(rm, hot, AX.X, ALU.max))
                then(dve.tensor_tensor(hot, hot, per_e(rm), ALU.is_equal))

            choose(RT[0], M1, R1M, RT[1])
            then(dve.scalar_tensor_tensor(out=RT[2], in0=RT[1], scalar=-FAR, in1=RT[0], op0=ALU.mult, op1=ALU.add))
            choose(RT[2], M2, R2M, RT[3])
            dve.tensor_tensor(DIF, M1, M2, ALU.subtract).then_inc(L.s["diff"], 1)
            dve.wait_ge(L.s["sg"], L.at["sg"] + 2)
            then(dve.tensor_tensor(RT[1], RT[1], per_e(W1S), ALU.mult))
            then(dve.tensor_tensor(RT[3], RT[3], per_e(W2S), ALU.mult))
            then(dve.tensor_tensor(RT[4], RT[1], RT[3], ALU.add))
            wts = RT[4].rearrange("p (s g) e -> p s e g", g=G)

            def weigh(s):
                dve.wait_ge(L.s["e_ps"], L.at["e_ps"] + s + 1)
                if s >= 2:
                    dve.wait_ge(L.s["e_half"], L.at["e_half"] + s - 1)
                o = (2 + 2 * (s % 3)) * BANK
                dve.tensor_tensor(TMP[:, s % 2, :].rearrange("p (e g c) -> p e g c", e=E3, g=G),
                                  PSUM[:, o:o + 2 * BANK].rearrange("p (e g c) -> p e g c", e=E3, g=G),
                                  wts[:, s].unsqueeze(3).to_broadcast([N, E3, G, C]), ALU.mult).then_inc(L.s["e_mul"], 1)

            def total(s):
                dve.wait_ge(L.s["e_half"], L.at["e_half"] + s + 1)
                dve.tensor_reduce(GATE[:, s * GC:(s + 1) * GC],
                                  HALF[:, s % 2, :].rearrange("p (e f) -> p f e", e=E3 // 2), AX.X, ALU.add)\
                    .then_inc(L.s["e_sum"], 1)

            for s in range(S + 1):
                if s < S:
                    weigh(s)
                if s >= 1:
                    total(s - 1)

        def f3_pool(pool):
            L = f3
            X4 = blocks(XC)
            for s in range(S + 1):
                if s < S:
                    pool.wait_ge(L.s["e_mul"], L.at["e_mul"] + s + 1)
                    if s >= 2:
                        pool.wait_ge(L.s["e_sum"], L.at["e_sum"] + s - 1)
                    pool.tensor_tensor(HALF[:, s % 2, :], TMP[:, s % 2, 0:BANK], TMP[:, s % 2, BANK:], ALU.add)\
                        .then_inc(L.s["e_half"], 1)
                if s >= 1 and s % 4 == 0:
                    b = s // 4 - 1
                    pool.wait_ge(L.s["e_sum"], L.at["e_sum"] + s)
                    x = X4[:, :, 4 * b:4 * b + 4, :].rearrange("p g s c -> p s g c")
                    pool.tensor_tensor(x, x, GATE[:, b * BANK:(b + 1) * BANK].rearrange("p (s g c) -> p s g c", s=4, g=G),
                                       ALU.add).then_inc(L.s["done"], 1)

        for L, b, col in ((t0, 2, 0), (t1, 2, 0), (t3, 3, 0), (f3, 4, 0), (r1, 5, 0), (r2, 5, GC)):
            L.wbank, L.wcol = b, col

        def later_weights_pe(pe):
            tri_weights_pe(pe, t1)
            tri_weights_pe(pe, t3)
            f3_weights_pe(pe)
            rec_weights_pe(pe, r1)
            rec_weights_pe(pe, r2)

        def later_weights_dve(dve):
            tri_weights2_dve(dve, t1)
            tri_weights2_dve(dve, t3)
            f3_weights_dve(dve)
            rec_weights2_dve(dve, r1)
            rec_weights2_dve(dve, r2)

        block = ctx.enter_context(nc.Block())

        @block.sync
        def _(sp):
            X4, D4 = blocks(XR), x_d.rearrange("i (g s) c -> i g (s c)", g=G)
            for q in range(LOADS):
                if q == 1:
                    sp.dma_start(par[:, :], par_d).then_inc(par_first, 16)
                    sp.dma_start(row[:, :], row_d).then_inc(par_first, 16)
                f = slice(q * NC // G // LOADS, (q + 1) * NC // G // LOADS)
                sp.dma_start(XR[:, :].rearrange("p (g f) -> p g f", g=G)[:, :, f], D4[:, :, f]).then_inc(x_in[q], 16)
            sp.dma_start(mask[:, :], mask_d).then_inc(par_in, 16)
            sp.dma_start(w1[:, :, :], w1_d).then_inc(par_in, 16)
            sp.dma_start(w2[:, :, :], w2_d).then_inc(par_in, 16)
            sp.dma_start(w2l[:, :], w2l_d).then_inc(par_in, 16)
            out4 = out_d.rearrange("(g s) j c -> j g s c", g=G)
            XC4 = blocks(XC)
            for b in range(S // 4):
                sp.wait_ge(f3.s["done"], f3.at["done"] + b + 1)
                for g in range(G):
                    sp.dma_start(out4[:, g, 4 * b:4 * b + 4, :], XC4[:, g, 4 * b:4 * b + 4, :]).then_inc(out_stored, 16)
            sp.wait_ge(out_stored, 16 * G * (S // 4))

        @block.gpsimd
        def _(pool):
            consts_pool(pool)
            f3_weights_pool(pool)
            ln_pool(pool, t0)
            scan_weights_pool(pool)
            tri_pool(pool, t0, None)
            ln_pool(pool, f0)
            f0_pool(pool)
            ln_pool(pool, t1)
            tri_pool(pool, t1, r1)
            rec_pool(pool, r1)
            ln_pool(pool, sc)
            scan_pool(pool)
            ln_pool(pool, r2)
            rec_pool(pool, r2)
            ln_pool(pool, t3)
            tri_pool(pool, t3, f3)
            f3_pool(pool)

        @block.scalar
        def _(act):
            ln_act(act, t0)
            tri_act(act, t0, None)
            turn_x_copy(act, v0, 0)
            ln_act(act, f0)
            f0_act(act)
            ln_act(act, t1)
            tri_act(act, t1, r1)
            rec_act(act, r1)
            turn_x_copy(act, v1, 0)
            ln_act(act, sc)
            turn_x_copy(act, v2, 0)
            ln_act(act, r2)
            rec_act(act, r2)
            ln_act(act, t3)
            tri_act(act, t3, f3)
            f3_act(act)

        @block.vector
        def _(dve):
            consts_dve(dve)
            ln_dve_step(dve, t0, 0)
            dve.wait_ge(par_first, PAR_FIRST)
            tri_weights1_dve(dve, t0)
            for u in range(1, LN_STEPS):
                ln_dve_step(dve, t0, u)
                if u == 1:
                    tri_weights2_dve(dve, t0)

            tri_dve(dve, t0, None, {
                4: lambda dve: tri_weights1_dve(dve, t1), 8: lambda dve: tri_weights1_dve(dve, t3), 12: lambda dve: rec_weights1_dve(dve, r1),
                16: lambda dve: rec_weights1_dve(dve, r2), 20: f0_weights_dve})
            turn_x_copy(dve, v0, 1)
            ln_dve(dve, f0)
            f0_dve(dve)
            ln_dve(dve, t1)
            tri_dve(dve, t1, r1)
            rec_dve(dve, r1, None)
            turn_x_copy(dve, v1, 1)
            ln_dve(dve, sc)
            scan_dve(dve)
            turn_x_copy(dve, v2, 1)
            ln_dve(dve, r2)
            rec_dve(dve, r2, t3)
            tri_dve(dve, t3, f3)
            f3_dve(dve)

        @block.tensor
        def _(pe):
            pe.wait_ge(par_first, PAR_FIRST)
            tri_weights_pe(pe, t0)
            tri_pe(pe, t0)
            turn_x_pe(pe, v0)
            f0_pe(pe)
            tri_pe(pe, t1)
            rec_pe(pe, r1)
            turn_x_pe(pe, v1)
            scan_pe(pe)
            turn_x_pe(pe, v2)
            rec_pe(pe, r2)
            tri_pe(pe, t3)
            f3_pe(pe)


def packed(inputs, np):
    def col(a, rows=N):
        a = np.asarray(a).reshape(-1, 1)
        return np.tile(a, (rows // a.shape[0], 1))

    def mat(a):
        return np.tile(np.asarray(a), (G, 1))

    L0, L1, L3, F0, F3 = "L0_conv_", "L1_conv_", "L3_conv_", "L0_ffn_", "L3_ffn_"
    i = inputs
    parts = [mat(np.concatenate([i[L0 + n] for n in ("Wga", "Wgb", "Wla", "Wlb", "Wgo")], 1)),
             mat(np.concatenate([i[L1 + n] for n in ("w_ag", "w_bg", "w_ap", "w_bp", "w_g")], 1)),
             mat(np.concatenate([i[L3 + n] for n in ("w2", "w1", "wg")], 1)),
             mat(i[L0 + "Wlo"]), mat(i[L1 + "w_z"]), mat(i[L3 + "wo"])]
    for p, names in ((L0, ("ln_in_w", "ln_in_b", "ln_o_w", "ln_o_b")), (L1, ("ln_in_w", "ln_in_b", "ln_out_w", "ln_out_b")),
                     (L3, ("norm_g", "norm_b", "onorm_g", "onorm_b"))):
        parts += [col(i[p + n]) for n in names]
    parts += [mat(np.asarray(i[F0 + "gate_w"]).T), col(i[F0 + "gate_b"]),
              mat(np.asarray(i["L2_conv_W"]).transpose(1, 0, 2).reshape(C, TAPS * C))]
    for p in ("L1_ffn_", "L2_ffn_"):
        parts += [mat(i[p + "W"]), mat(np.asarray(i[p + "V"]).T), col(i[p + "gamma"]), col(i[p + "beta"])]
    parts += [mat(i[F3 + "router_w"]), mat(np.asarray(i[F3 + "expert_w"]).transpose(1, 0, 2).reshape(C, E3 * C))]
    par = np.concatenate(parts, 1)
    rows = [i[L0 + n] for n in ("bga", "bgb", "bla", "blb", "bgo")]
    rows += [i[L1 + n] for n in ("b_ag", "b_bg", "b_ap", "b_bp", "b_g")]
    rows += [i[L3 + n] for n in ("b2", "b1", "bg")] + [i[L0 + "blo"], i[L1 + "b_z"], i[L3 + "bo"]]
    rows += [i[F3 + "router_b"], np.asarray(i[F3 + "expert_b"]).reshape(-1)]
    row = np.concatenate([np.asarray(r) for r in rows])[None, :]
    return {
        "x": np.asarray(i["x"]).reshape(N, N, C),
        "par": par,
        "row": row,
        "mask": np.asarray(i[L1 + "mask"])[0].T,
        "w1": np.asarray(i[F0 + "weight1"]).transpose(1, 0, 2),
        "w2": np.asarray(i[F0 + "weight2"])[:, 0:H0].transpose(1, 0, 2),
        "w2l": np.asarray(i[F0 + "weight2"])[:, H0].T,
    }


def kernel(**inputs):
    import numpy as _np
    import concourse.bacc as _bacc
    from concourse.bass_utils import run_bass_kernel_spmd as _run

    nc = _bacc.Bacc("TRN2", target_bir_lowering=False, num_devices=1)
    arrays, args = {}, []
    for name, a in packed(inputs, _np).items():
        a = _np.ascontiguousarray(a)
        arrays[f"in_{name}_dram"] = a
        args.append(nc.dram_tensor(f"in_{name}_dram", a.shape, mybir.dt.from_np(a.dtype), kind="ExternalInput").ap())
    out = nc.dram_tensor("out_0_dram", (N, N, C), F32, kind="ExternalOutput").ap()
    build(nc, *args, out)
    r = _run(nc, [arrays], core_ids=[0])
    return r.results[0]["out_0_dram"].reshape(1, N, N, C)
```

```python
from contextlib import ExitStack

import concourse.bass as bass
from concourse import mybir
from concourse.alu_op_type import AluOpType as ALU

F32 = mybir.dt.float32
I32 = mybir.dt.int32
BF16 = mybir.dt.bfloat16
ACT = mybir.ActivationFunctionType
AX = mybir.AxisListType

N = 128
C = 32
G, S = 4, 32
NC = N * C
GC = G * C
BANK = 512
Q = 8
LAG = 2
LOADS = 4
SQ = S // Q
E0, K0, H0 = 16, 8, 128
SEG = N // E0
SEGI = N // SEG
SEGT = SEGI * N
E3 = 8
TAPS = 9
CHUNK = 16
WARM = 12
ROUNDS = ((CHUNK - WARM, WARM, 0), (0, CHUNK, WARM))
STEPS = WARM + CHUNK
STREAMS = 2
NCH = NC // CHUNK
NS = NCH // STREAMS
ROWCH = N // CHUNK
ROWS_S = ROWCH // STREAMS
GENERAL_ROUNDS = G * NCH - 1
GENERAL_SCANS = ROWCH - 1
EPS, EPS_C = 1e-5, 1e-6
TRIS = ("L0", "L1", "L3")
POOL_CONSTS = 11
DVE_CONSTS = 11
PAR_FIRST = 16 * 2
PAR_LOADS = 16 * 4
SCAN_COPIES = 36
FAR = 1.0e30
FIXED_TOL = 2.0 ** -22

PAR = {}
_at = 0
for _name, _count in (
    [(f"{l}_w", 160) for l in ("L0", "L1", "L3")] + [(f"{l}_wo", 32) for l in ("L0", "L1", "L3")]
    + [(f"{l}_{v}", 1) for l in ("L0", "L1", "L3") for v in ("lnw", "lnb", "low", "lob")]
    + [("gate", E0), ("gate_b", 1), ("conv", TAPS * C)]
    + [(f"{l}_{v}", n) for l in ("R1", "R2") for v, n in (("W", C), ("VT", C), ("gamma", 1), ("beta", 1))]
    + [("router", E3), ("expert", E3 * C)]
):
    PAR[_name] = (_at, _count)
    _at += _count
NPAR = _at
ROW = {}
_at = 0
for _name, _count in ([(f"{l}_b", 160) for l in ("L0", "L1", "L3")] + [(f"{l}_bo", 32) for l in ("L0", "L1", "L3")]
                      + [("router_b", E3), ("expert_b", E3 * C)]):
    ROW[_name] = (_at, _count)
    _at += _count
NROW = _at



class Stage:

    def __init__(self, name, src, dst, scratch, eps, e2):
        self.name, self.s, self.at = name, {}, {}
        self.src, self.dst, self.scratch = src, dst, scratch
        self.eps, self.e2 = eps, e2
        self.ready = None
        self.function = None
        self.banks_free = []
        self.wbank = self.wcol = 0


def build(nc, x_d, par_d, row_d, mask_d, w1_d, w2_d, w2l_d, out_d):
    with ExitStack() as ctx:
        def sb(name, shape, dt=F32):
            return ctx.enter_context(nc.sbuf_tensor(name, shape, dt))

        def sem(name):
            return ctx.enter_context(nc.semaphore(name))

        XR = sb("x_rows", [N, NC])
        XC = sb("x_cols", [N, NC])
        Z = sb("z", [N, NC])
        SQR = sb("squares", [N, NC])
        ZT = sb("z_t", [GC, S, N])
        AB = sb("ab", [N, 2 * NC])
        AT = ZT
        GATE = sb("gate", [N, NC])
        SIG = sb("sig", [N, 2, 2 * GC])
        TMP = sb("tmp", [N, 2, 2 * BANK])
        par = sb("par", [GC, NPAR])
        row = sb("row", [1, NROW])
        mask = sb("mask", [N, N])
        stats = sb("stats", [N, 4, N])
        ident = sb("ident", [N, N])
        d32 = sb("d32", [N, C])
        d16 = sb("d16", [N, E0])
        e16 = sb("e16", [E0, SEG, E0])
        m4 = sb("m4", [N, G])
        m8 = sb("m8", [N, SEG])
        cent = sb("cent", [GC, GC])
        same32 = sb("same32", [N, G, C])
        same16 = sb("same16", [N, SEG, E0])
        shift = sb("shift", [N, N])
        eps = sb("eps", [N, 4])
        onesf = sb("onesf", [1, N])
        warm_out = sb("warm_out", [1, 32])
        wp = {l: sb(f"wp_{l}", [GC, 5, GC]) for l in TRIS}
        wo = {l: sb(f"wo_{l}", [GC, 2, GC]) for l in TRIS}
        bo = {l: sb(f"bo_{l}", [N, C]) for l in TRIS}
        scaled = {l: sb(f"scaled_{l}", [GC, 5 * C]) for l in TRIS}
        wotmp = {l: sb(f"wotmp_{l}", [GC, GC + C]) for l in TRIS}
        lnb_at = {l: sb(f"lnb_at_{l}", [C, GC]) for l in TRIS}
        last = sb("last", [C, G, C])
        fold = sb("fold", [GC, GC])
        gw = sb("gw", [GC, 2, N])
        PSUM = ctx.enter_context(nc.psum_tensor("psum", [N, 8 * BANK], F32))

        def bank(b, cols=BANK, n=1):
            return PSUM[:, b * BANK:b * BANK + (n - 1) * BANK + cols]

        def blocks(t):
            return t[:, 0:NC].rearrange("p (g s c) -> p g s c", g=G, s=S)

        def pcol(name, rows=GC):
            a, n = PAR[name]
            return par[0:rows, a:a + n]

        def prow(name):
            a, n = ROW[name]
            return row[0:1, a:a + n]

        ABt = AB[:, :].rearrange("p (a c n) -> p a c n", a=2, c=C)

        x_in = [sem(f"x_in{q}") for q in range(LOADS)]
        par_first = sem("par_first")
        par_in = sem("par_in")
        out_stored = sem("out_stored")
        const_pool = sem("const_pool")
        const_dve = sem("const_dve")
        const_act = sem("const_act")
        X_LOADED = [[(x_in[q * LOADS // Q], 16)] for q in range(Q)]

        families = {
            "norm": "sum:8 mean:8 centred:8 square:8 sumsq:8 std:8 rstd:8 z:8",
            "turn": "zt_ps:8 zt:8",
            "weights": "w_half:4 w_dve:4 w_pe:1",
            "ones": "one:8",
            "tri": "zt_ps:8 zt:8 proj:32 sig:32 gate_ps:8 gate:8 lin:32 k_ps:8 k_act:4 k_dve:4 kt_ps:8 kt:8"
                   " o_ps:8 o_sq:8 o_sum:8 o_std:8 o_rstd:8 o_rg:8 o_mul:8 xg:8 xb:8 done:8",
            "turn_x": "ps:8 act:4 dve:4",
            "rec": "w_half:2 w_dve:1 w_pe:1 wx_ps:8 wx:8 bn:4 bnc:2 bn_ps:3 std1:1 bnw:5 step_ps:56 step_y0:29 step_y1:29 edge_ps:2"
                   " edge:2 chk:3 chk_ps:1 flag:2 y_ps:8 done:8",
        }
        shared = {}

        def stage(name, kinds, own="", src=None, dst=None, scratch=None, eps=0, e2=0.0):
            L = Stage(name, src, dst, scratch, eps, e2)
            for kind in kinds.split():
                if kind not in shared:
                    shared[kind] = [0, {}]
                    for word in families[kind].split():
                        shared[kind][1][word.split(":")[0]] = sem(f"{kind}_{word.split(':')[0]}")
                before, sems = shared[kind]
                shared[kind][0] += 1
                for word in families[kind].split():
                    key, n = word.split(":")
                    L.s[key], L.at[key] = sems[key], before * int(n)
            for key in own.split():
                L.s[key], L.at[key] = sem(f"{name}_{key}"), 0
            return L

        def wait_all(eng, levels):
            for s, v in levels:
                eng.wait_ge(s, v)

        t0 = stage("L0", "norm weights ones tri", "at_ps at_act at_dve", src=XR, scratch=XC, eps=0, e2=EPS)
        v0 = stage("V0", "turn_x", src=XR, dst=XC)
        f0 = stage("F0", "norm turn", "w_dve lg_ps lg_act pad best top neg cand_ps cand fin mk_ps mk sel exp esum tot_ps tot w wt_ps"
                   " wt_act wt_dve pool_ps pl plt_ps plt h_ps h o_ps outm_ps outm y_ps done", src=XC, eps=1, e2=0.0)
        t1 = stage("L1", "norm weights ones tri", "ab", src=XC, scratch=XR, eps=0, e2=EPS)
        r1 = stage("R1", "norm turn rec", "g_ps g_y0 g_y1 g_edge_ps g_edge g_turned", src=XC, eps=1, e2=0.0)
        v1 = stage("V1", "turn_x", src=XC, dst=XR)
        sc = stage("SC", "norm turn", "pads w_dve w_pool conv row0 row1 kept chk chk_ps flag g_conv g_row0 g_row1 g_turned"
                   " y_ps done", src=XR, eps=2, e2=0.0)
        v2 = stage("V2", "turn_x", src=XR, dst=XC)
        r2 = stage("R2", "norm turn rec", "g_ps g_y0 g_y1 g_edge_ps g_edge g_turned", src=XC, eps=1, e2=0.0)
        t3 = stage("L3", "norm weights ones tri", src=XC, scratch=XR, eps=0, e2=EPS)
        f3 = stage("F3", "norm ones turn", "w_dve w_pe rank hot rt_ps top diff sg e_ps e_mul e_half e_sum done", src=XC, eps=1, e2=0.0)

        x_done = lambda L: [(L.s["done"], L.at["done"] + S // 4)]
        x_chunks = lambda L: [[(L.s["done"], L.at["done"] + q + 1)] for q in range(Q)]
        turned = lambda L: [(L.s["act"], L.at["act"] + 4), (L.s["dve"], L.at["dve"] + 4)]
        t0.ready = X_LOADED
        v0.ready = x_done(t0)
        f0.ready = [turned(v0)] * Q
        t1.ready = [[(f0.s["done"], min(2 * (q % 4) + 2 + SEGI * (q // 4), SEGI // 2))] for q in range(Q)]
        r1.ready = x_chunks(t1)
        v1.ready = x_done(r1)
        sc.ready = [turned(v1)] * Q
        v2.ready = x_done(sc)
        r2.ready = [turned(v2)] * Q
        t3.ready = x_chunks(r2)
        f3.ready = x_chunks(t3)
        for L in (t0, t1, t3, f3):
            L.function = ACT.Sigmoid
        f0.function = ACT.Exp
        r1.banks_free = [(t1.s["o_mul"], t1.at["o_mul"] + S // 4)]
        t3.banks_free = x_done(r2)
        f3.early_banks_free = [(t3.s["o_mul"], t3.at["o_mul"] + S // 4 - 1)]
        f3.banks_free = [(t3.s["o_mul"], t3.at["o_mul"] + S // 4)]

        def ln_parts():
            return [stats[:, k, :].rearrange("p (q s g) -> p q s g", q=Q, g=G) for k in range(4)]

        def over_c(t):
            return t.unsqueeze(3).to_broadcast([N, SQ, G, C])

        def by_block(t):
            return t[:, 0:NC].rearrange("p (s g c) -> p s g c", g=G, s=S)

        LN_STEPS = Q + LAG + 2

        def ln_dve_step(dve, L, u):
            X4 = by_block(L.src) if L is sc else blocks(L.src).rearrange("p g s c -> p s g c")
            Z4, SQ4 = by_block(Z), by_block(SQR)
            SUM, MEAN, SS, RSTD = ln_parts()
            q, before, first = u, u - LAG, u - LAG - 1
            if 0 <= q < Q:
                wait_all(dve, L.ready[q])
                r = slice(SQ * q, SQ * (q + 1))
                dve.tensor_reduce(SUM[:, q], X4[:, r], AX.X, ALU.add).then_inc(L.s["sum"], 1)
            if 0 <= before < Q:
                dve.wait_ge(L.s["square"], L.at["square"] + before + 1)
                dve.tensor_reduce(SS[:, before], SQ4[:, SQ * before:SQ * (before + 1)], AX.X, ALU.add)\
                    .then_inc(L.s["sumsq"], 1)
            if 0 <= q < Q:
                dve.wait_ge(L.s["sum"], L.at["sum"] + q + 1)
                dve.tensor_scalar(MEAN[:, q], SUM[:, q], 1.0 / C, None, ALU.mult).then_inc(L.s["mean"], 1)
            if 0 <= first < Q:
                dve.wait_ge(L.s["std"], L.at["std"] + first + 1)
                dve.reciprocal(RSTD[:, first], SUM[:, first]).then_inc(L.s["rstd"], 1)
            if 0 <= q < Q:
                dve.wait_ge(L.s["mean"], L.at["mean"] + q + 1)
                dve.tensor_tensor(Z4[:, r], X4[:, r], over_c(MEAN[:, q]), ALU.subtract).then_inc(L.s["centred"], 1)

        def ln_act_step(act, L, u):
            Z4, SQ4 = by_block(Z), by_block(SQR)
            SUM, _, SS, _ = ln_parts()
            q = u - LAG
            if 0 <= q < Q:
                act.wait_ge(L.s["sumsq"], L.at["sumsq"] + q + 1)
                act.activation(SUM[:, q], SS[:, q], ACT.Sqrt, bias=eps[:, L.eps:L.eps + 1],
                               scale=(1.0 + L.e2) / C).then_inc(L.s["std"], 1)
                if q == Q - 1 and L.function is not None:
                    warm_table(act, L.function)
            q = u
            if 0 <= q < Q:
                r = slice(SQ * q, SQ * (q + 1))
                act.wait_ge(L.s["centred"], L.at["centred"] + q + 1)
                act.activation(SQ4[:, r], Z4[:, r], ACT.Square).then_inc(L.s["square"], 1)
            q = u - LAG - 2
            if 0 <= q < Q:
                act.wait_ge(L.s["zt_ps"], L.at["zt_ps"] + q + 1)
                dst = ZT[:, 4 * q:4 * q + 4, :]
                if L is sc:
                    dst = RIN[:, :, 4 * q:4 * q + 4].rearrange("p i n -> p n i")
                act.activation(dst, bank(q % 2), ACT.Copy).then_inc(L.s["zt"], 1)

        def ln_pool_step(pool, L, u):
            q = u - LAG - 1
            if 0 <= q < Q:
                Z4, r = by_block(Z), slice(SQ * q, SQ * (q + 1))
                pool.wait_ge(L.s["square"], L.at["square"] + q + 1)
                last_c = C
                if "one" in L.s:
                    last_c = C - 1
                    pool.memset(Z4[:, r, :, last_c:], 1.0).then_inc(L.s["one"], 1)
                pool.wait_ge(L.s["rstd"], L.at["rstd"] + q + 1)
                rstd = ln_parts()[3][:, q].unsqueeze(3).to_broadcast([N, SQ, G, last_c])
                pool.tensor_tensor(Z4[:, r, :, 0:last_c], Z4[:, r, :, 0:last_c], rstd, ALU.mult).then_inc(L.s["z"], 1)

        def ln_dve(dve, L):
            for u in range(LN_STEPS):
                ln_dve_step(dve, L, u)

        def ln_act(act, L):
            warm_table(act, ACT.Sqrt)
            act.wait_ge(const_pool, POOL_CONSTS)
            for u in range(LN_STEPS):
                ln_act_step(act, L, u)

        def ln_pool(pool, L):
            for u in range(LN_STEPS):
                ln_pool_step(pool, L, u)

        warmed = [0]

        def warm_table(act, function):
            k = warmed[0]
            warmed[0] += 1
            if k == 0:
                act.wait_ge(const_pool, POOL_CONSTS)
            act.activation(warm_out[:, k:k + 1], onesf[0:1, 0:1], function)

        def turn_pe(pe, L, b, src, ps="zt_ps", act="zt_act", dve="zt_dve"):
            if b >= 2:
                pe.wait_ge(L.s[dve if b % 2 else act], L.at[dve if b % 2 else act] + b // 2)
            for k in range(4):
                m = pe.transpose(bank(b % 2)[:, k * N:(k + 1) * N], src(4 * b + k), ident[:, :])
            m.then_inc(L.s[ps], 1)

        def turn_copy(eng, L, b, dst, done, ps="zt_ps"):
            eng.wait_ge(L.s[ps], L.at[ps] + b + 1)
            if b % 2:
                eng.tensor_copy(dst, bank(b % 2)).then_inc(L.s[done], 1)
            else:
                eng.activation(dst, bank(b % 2), ACT.Copy).then_inc(L.s[done], 1)

        def block_of(t):
            return lambda s: t[:, s * GC:(s + 1) * GC]

        def turn_z_pe(pe, L, b):
            pe.wait_ge(L.s["z"], L.at["z"] + b + 1)
            if "one" in L.s:
                pe.wait_ge(L.s["one"], L.at["one"] + b + 1)
            if b >= 2:
                pe.wait_ge(L.s["zt"], L.at["zt"] + b - 1)
            for k in range(4):
                m = pe.transpose(bank(b % 2)[:, k * N:(k + 1) * N], block_of(Z)(4 * b + k), ident[:, :])
            m.then_inc(L.s["zt_ps"], 1)

        def turn_all_z_pe(pe, L):
            for b in range(S // 4):
                turn_z_pe(pe, L, b)

        def consts_pool(pool):
            pool.memset(ident[:, :], 0.0).then_inc(const_pool, 1)
            pool.wait_ge(const_pool, 1)
            pool.affine_select(out=ident[:, :], in_=ident[:, :], compare_op=ALU.not_equal, fill=1.0, base=0,
                               pattern=[[-1, N]], channel_multiplier=1).then_inc(const_pool, 1)
            pool.memset(shift[:, :], 0.0).then_inc(const_pool, 1)
            pool.wait_ge(const_pool, 3)
            pool.affine_select(out=shift[:, :], in_=shift[:, :], compare_op=ALU.not_equal, fill=1.0, base=C,
                               pattern=[[-1, N]], channel_multiplier=1).then_inc(const_pool, 1)
            for k, v in enumerate((EPS_C * EPS, EPS, EPS_C)):
                pool.memset(eps[:, k:k + 1], v).then_inc(const_pool, 1)
            pool.memset(onesf[:, :], 1.0).then_inc(const_pool, 1)
            pool.memset(last[:, :, 0:C - 1], 0.0).then_inc(const_pool, 1)
            pool.memset(last[:, :, C - 1:], 1.0).then_inc(const_pool, 1)
            pool.memset(gw[:, :, :], 0.0).then_inc(const_pool, 1)

        def consts_dve(dve):
            dve.wait_ge(const_pool, POOL_CONSTS)
            i3 = ident[:, :]
            dve.tensor_reduce(d32[:, :], i3.rearrange("p (g c) -> p c g", g=G), AX.X, ALU.add).then_inc(const_dve, 1)
            dve.tensor_reduce(m4[:, :], i3.rearrange("p (g c) -> p g c", g=G), AX.X, ALU.add).then_inc(const_dve, 1)
            dve.tensor_reduce(d16[:, :], i3.rearrange("p (s e) -> p e s", e=E0), AX.X, ALU.add).then_inc(const_dve, 1)
            dve.tensor_reduce(m8[:, :], i3.rearrange("p (s e) -> p s e", e=E0), AX.X, ALU.add).then_inc(const_dve, 1)
            dve.wait_ge(const_dve, 4)
            g_c = [N, G, C]
            dve.tensor_scalar(cent[:, :].rearrange("p (g c) -> p g c", g=G), m4[:, :].unsqueeze(2).to_broadcast(g_c),
                              -1.0 / C, None, ALU.mult).then_inc(const_dve, 1)
            dve.wait_ge(const_dve, 5)
            dve.tensor_tensor(cent[:, :], cent[:, :], ident[:, :], ALU.add).then_inc(const_dve, 1)
            dve.tensor_scalar(same32[:, :, :], d32[:, :].unsqueeze(1).to_broadcast(g_c), 1.0 / G, None, ALU.mult)\
                .then_inc(const_dve, 1)
            dve.tensor_copy(same16[:, :, :], d16[:, :].unsqueeze(1).to_broadcast([N, SEG, E0])).then_inc(const_dve, 1)
            dve.tensor_copy(e16[:, :, :], d16[0:E0, :].unsqueeze(1).to_broadcast([E0, SEG, E0])).then_inc(const_dve, 1)
            dve.tensor_scalar(fold[:, :].rearrange("p (g c) -> p g c", g=G), m4[:, :].unsqueeze(2).to_broadcast(g_c),
                              d32[:, C - 1:C], -1.0, ALU.mult, ALU.mult).then_inc(const_dve, 1)
            dve.wait_ge(const_dve, 10)
            dve.tensor_tensor(fold[:, :], fold[:, :], ident[:, :], ALU.add).then_inc(const_dve, 1)

        def fold_biases(pe, out, w, b, lnb_at=None, w0=None):
            pe.matmul(out, fold[:, :], w, start=True, stop=False)
            if lnb_at is not None:
                pe.matmul(out, lnb_at, w0, start=False, stop=False)
            return pe.matmul(out, last[0:1, :, :], b, start=False, stop=True)

        def by_groups(w, k):
            shape = [GC, k, G, C]
            return w.rearrange("p (k c) -> p k c", k=k).unsqueeze(2).to_broadcast(shape), \
                m4[:, :].unsqueeze(1).unsqueeze(3).to_broadcast(shape)

        TRI_W = 4

        def tri_weights1_dve(dve, L):
            l, sm = L.name, L.s["w_half"]
            dve.tensor_scalar(scaled[l][:, :], pcol(f"{l}_w"), pcol(f"{l}_lnw"), None, ALU.mult).then_inc(sm, 1)
            dve.tensor_scalar(wotmp[l][:, GC:], pcol(f"{l}_wo"), pcol(f"{l}_low"), None, ALU.mult).then_inc(sm, 1)
            dve.tensor_scalar(lnb_at[l][:, :], last[:, :, :].rearrange("p g c -> p (g c)"), pcol(f"{l}_lnb", C), None,
                              ALU.mult).then_inc(sm, 1)
            dve.wait_ge(sm, L.at["w_half"] + 2)
            dve.tensor_tensor(wotmp[l][:, 0:GC].rearrange("p (g c) -> p g c", g=G),
                              wotmp[l][:, GC:].unsqueeze(1).to_broadcast([GC, G, C]),
                              m4[:, :].unsqueeze(2).to_broadcast([GC, G, C]), ALU.mult).then_inc(sm, 1)

        def tri_weights2_dve(dve, L):
            l, sm = L.name, L.s["w_dve"]
            dve.wait_ge(L.s["w_pe"], L.at["w_pe"] + 1)
            w, m = by_groups(bank(L.wbank)[:, 0:5 * C], 5)
            dve.tensor_tensor(wp[l][:, :, :].rearrange("p k (g c) -> p k g c", g=G), w, m, ALU.mult).then_inc(sm, 1)
            dve.tensor_copy(bo[l][:, :], bank(L.wbank)[:, 160:192]).then_inc(sm, 1)
            dve.tensor_copy(wo[l][:, 0, :], bank(L.wbank)[:, 192:320]).then_inc(sm, 1)
            dve.tensor_copy(wo[l][:, 1, :], cent[:, :]).then_inc(sm, 1)

        def tri_weights_pe(pe, L):
            l = L.name
            pe.wait_ge(const_dve, DVE_CONSTS)
            pe.wait_ge(L.s["w_half"], L.at["w_half"] + TRI_W)
            pe.matmul(bank(L.wbank)[:, 160:192], pcol(f"{l}_lob", C).to_broadcast([C, N]), pcol(f"{l}_wo", C),
                      start=True, stop=False)
            pe.matmul(bank(L.wbank)[:, 160:192], onesf[:, :], prow(f"{l}_bo"), start=False, stop=True)
            pe.matmul(bank(L.wbank)[:, 192:320], cent[:, :], wotmp[l][:, 0:GC], start=True, stop=True)
            fold_biases(pe, bank(L.wbank)[:, 0:5 * C], scaled[l][:, :], prow(f"{l}_b"), lnb_at[l][:, :], pcol(f"{l}_w", C))\
                .then_inc(L.s["w_pe"], 1)

        LIN = BANK // 2
        TRI_LN = 5
        KB = [2, 3, 4, 5]
        GB = [6, 7]

        def tri_pe(pe, L):
            l = L.name
            def project(s):
                b, k = s // 4, s % 4
                if k == 0:
                    pe.wait_ge(L.s["zt"], L.at["zt"] + b + 1)
                    if b >= 2:
                        pe.wait_ge(L.s["gate"], L.at["gate"] + b - 1)
                if s >= 4:
                    pe.wait_ge(L.s["lin"], L.at["lin"] + s - 3)
                pe.matmul(bank(KB[s % 4]), ZT[:, s, :], wp[l][:, 0:4, :], start=True, stop=True)\
                    .then_inc(L.s["proj"], 1)
                m = pe.matmul(bank(GB[b % 2])[:, k * GC:(k + 1) * GC], ZT[:, s, :], wp[l][:, 4, :], start=True, stop=True)
                if k == 3:
                    m.then_inc(L.s["gate_ps"], 1)

            ahead = 4 if L.banks_free else 2
            for b in range(S // 4):
                turn_z_pe(pe, L, b)
                if b == ahead:
                    pe.wait_ge(L.s["w_dve"], L.at["w_dve"] + TRI_W)
                    wait_all(pe, L.banks_free)
                if ahead <= b < ahead + 4:
                    project(b - ahead)
            for s in range(4, S):
                project(s)
            pe.wait_ge(L.s["ab" if L is t1 else "lin"], L.at["ab" if L is t1 else "lin"] + S)
            pe.wait_ge(L.s["zt"], L.at["zt"] + S // 4)
            lhs, rhs = ABt[:, 1], ABt[:, 0]
            if L is t0:
                lhs, rhs = AT, ABt[:, 1]
                for b in range(C // 4):
                    turn_pe(pe, L, b, lambda c: ABt[:, 0, c, :], "at_ps", "at_act", "at_dve")
            for b in range(C // 4):
                if L is t0:
                    pe.wait_ge(L.s["at_dve" if b % 2 else "at_act"], L.at["at_dve" if b % 2 else "at_act"] + b // 2 + 1)
                if b >= 4:
                    pe.wait_ge(L.s["k_dve" if b % 2 else "k_act"], L.at["k_dve" if b % 2 else "k_act"] + b // 2 - 1)
                for k in range(4):
                    c = 4 * b + k
                    m = pe.matmul(bank(KB[b % 4])[:, k * N:(k + 1) * N], lhs[:, c, :], rhs[:, c, :],
                                  start=True, stop=True)
                m.then_inc(L.s["k_ps"], 1)

            def out_project(b):
                pe.wait_ge(L.s["kt"], L.at["kt"] + b + 1)
                if b >= 3:
                    pe.wait_ge(L.s["o_mul"], L.at["o_mul"] + b - 2)
                for k in range(4):
                    m = pe.matmul(PSUM[:, (2 + 2 * (b % 3)) * BANK + k * 2 * GC:(2 + 2 * (b % 3)) * BANK + (k + 1) * 2 * GC],
                                  ZT[:, 4 * b + k, :], wo[l][:, :, :], start=True, stop=True)
                m.then_inc(L.s["o_ps"], 1)

            pe.wait_ge(L.s["k_act"], L.at["k_act"] + 4)
            pe.wait_ge(L.s["k_dve"], L.at["k_dve"] + 4)
            for b in range(S // 4):
                if b >= 2:
                    pe.wait_ge(L.s["kt"], L.at["kt"] + b - 1)
                for k in range(4):
                    m = pe.transpose(bank(b % 2)[:, k * N:(k + 1) * N], block_of(Z)(4 * b + k), ident[:, :])
                m.then_inc(L.s["kt_ps"], 1)
                if b >= 1:
                    out_project(b - 1)
            out_project(S // 4 - 1)

        def o_bank(b):
            o = (2 + 2 * (b % 3)) * BANK
            return PSUM[:, o:o + 2 * BANK].rearrange("p (s w f) -> p s w f", s=4, w=2)

        def k_copy(eng, L, b):
            eng.wait_ge(L.s["k_ps"], L.at["k_ps"] + b + 1)
            out = Z[:, :].rearrange("p (s g c) -> p c g s", g=G, c=C)[:, 4 * b:4 * b + 4]
            src = bank(KB[b % 4]).rearrange("p (c g s) -> p c g s", c=4, g=G)
            if b % 2:
                eng.tensor_copy(out, src).then_inc(L.s["k_dve"], 1)
            else:
                eng.activation(out, src, ACT.Copy).then_inc(L.s["k_act"], 1)

        def tri_act(act, L, after):
            for b in range(S // 4):
                for k in range(4):
                    s = 4 * b + k
                    act.wait_ge(L.s["proj"], L.at["proj"] + s + 1)
                    if s >= 2:
                        act.wait_ge(L.s["lin"], L.at["lin"] + s - 1)
                    act.activation(SIG[:, s % 2, :], bank(KB[s % 4], LIN), ACT.Sigmoid).then_inc(L.s["sig"], 1)
                act.wait_ge(L.s["gate_ps"], L.at["gate_ps"] + b + 1)
                act.activation(GATE[:, b * BANK:(b + 1) * BANK], bank(GB[b % 2]), ACT.Sigmoid).then_inc(L.s["gate"], 1)
            if L is t0:
                for b in range(0, C // 4, 2):
                    turn_copy(act, L, b, AT[:, 4 * b:4 * b + 4, :], "at_act", "at_ps")
            warm_table(act, ACT.Sqrt)
            for b in range(0, C // 4, 2):
                k_copy(act, L, b)

            def out_square(b):
                act.wait_ge(L.s["o_ps"], L.at["o_ps"] + b + 1)
                act.activation(SQR[:, b * BANK:(b + 1) * BANK].rearrange("p (s f) -> p s f", s=4),
                               o_bank(b)[:, :, 1, :], ACT.Square).then_inc(L.s["o_sq"], 1)

            def out_deviation(b):
                act.wait_ge(L.s["o_sum"], L.at["o_sum"] + b + 1)
                act.activation(stats[:, 0, 16 * b:16 * b + 16], stats[:, 2, 16 * b:16 * b + 16], ACT.Sqrt,
                               bias=eps[:, 1:2], scale=1.0 / C).then_inc(L.s["o_std"], 1)

            for t in range(TRI_LN + LN_STEPS if after else S // 4 + 2):
                if t < S // 4:
                    act.wait_ge(L.s["kt_ps"], L.at["kt_ps"] + t + 1)
                    act.activation(ZT[:, 4 * t:4 * t + 4, :], bank(t % 2), ACT.Copy).then_inc(L.s["kt"], 1)
                if 1 <= t <= S // 4:
                    out_square(t - 1)
                if 2 <= t < S // 4 + 2:
                    out_deviation(t - 2)
                if after:
                    ln_act_step(act, after, t - TRI_LN)

        def tri_dve(dve, L, after, between={}):
            to_ab = AB[:, :].rearrange("p (a c g s) -> p a g s c", a=2, c=C, g=G)
            def gate_bias(b):
                cols = slice(b * BANK, (b + 1) * BANK)
                dve.wait_ge(L.s["gate"], L.at["gate"] + b + 1)
                dve.tensor_tensor(L.scratch[:, cols].rearrange("p (n c) -> p n c", c=C),
                                  GATE[:, cols].rearrange("p (n c) -> p n c", c=C),
                                  bo[L.name][:, :].unsqueeze(1).to_broadcast([N, 16, C]), ALU.mult)\
                    .then_inc(L.s["xg"], 1)

            for s in range(S):
                if s in between:
                    between[s](dve)
                dve.wait_ge(L.s["sig"], L.at["sig"] + s + 1)
                lin = bank(KB[s % 4])[:, LIN:].rearrange("p (a g c) -> p a g c", a=2, g=G)
                sig = SIG[:, s % 2, :].rearrange("p (a g c) -> p a g c", a=2, g=G)
                if L is t1:
                    if s >= 2:
                        dve.wait_ge(L.s["ab"], L.at["ab"] + s - 1)
                    dst = TMP[:, s % 2, 0:LIN].rearrange("p (a g c) -> p a g c", a=2, g=G)
                else:
                    dst = to_ab[:, :, :, s, :]
                dve.tensor_tensor(dst, lin, sig, ALU.mult).then_inc(L.s["lin"], 1)
                if s % 4 == 2 and s > 4:
                    gate_bias(s // 4 - 1)
            gate_bias(S // 4 - 1)
            if L is t0:
                for b in range(1, C // 4, 2):
                    turn_copy(dve, L, b, AT[:, 4 * b:4 * b + 4, :], "at_dve", "at_ps")
            for b in range(1, C // 4, 2):
                k_copy(dve, L, b)

            def out_sum(b):
                dve.wait_ge(L.s["o_sq"], L.at["o_sq"] + b + 1)
                dve.tensor_reduce(stats[:, 2, 16 * b:16 * b + 16],
                                  SQR[:, b * BANK:(b + 1) * BANK].rearrange("p (n c) -> p n c", c=C), AX.X, ALU.add)\
                    .then_inc(L.s["o_sum"], 1)

            def out_inverse(b):
                dve.wait_ge(L.s["o_std"], L.at["o_std"] + b + 1)
                dve.reciprocal(stats[:, 3, 16 * b:16 * b + 16], stats[:, 0, 16 * b:16 * b + 16]).then_inc(L.s["o_rstd"], 1)

            def out_gate(b):
                dve.wait_ge(L.s["o_rg"], L.at["o_rg"] + b + 1)
                if b >= 2:
                    dve.wait_ge(L.s["done"], L.at["done"] + b - 1)
                dve.tensor_tensor(TMP[:, b % 2, 0:BANK].rearrange("p (s f) -> p s f", s=4), o_bank(b)[:, :, 0, :],
                                  GATE[:, b * BANK:(b + 1) * BANK].rearrange("p (s f) -> p s f", s=4), ALU.mult)\
                    .then_inc(L.s["o_mul"], 1)

            for t in range(TRI_LN + LN_STEPS if after else S // 4 + 4):
                if 4 <= t < S // 4 + 4:
                    out_gate(t - 4)
                if 3 <= t < S // 4 + 3:
                    out_inverse(t - 3)
                if 2 <= t < S // 4 + 2:
                    out_sum(t - 2)
                if after:
                    ln_dve_step(dve, after, t - TRI_LN)

        def tri_pool(pool, L, after):
            X4 = blocks(L.src)
            XB = L.scratch

            def add_x(b):
                x = XB[:, b * BANK:(b + 1) * BANK].rearrange("p (s g c) -> p s g c", s=4, g=G)
                pool.wait_ge(L.s["xg"], L.at["xg"] + b + 1)
                pool.tensor_tensor(x, x, X4[:, :, 4 * b:4 * b + 4, :].rearrange("p g s c -> p s g c"), ALU.add)\
                    .then_inc(L.s["xb"], 1)

            if L is t1:
                to_ab = AB[:, :].rearrange("p (a c g s) -> p a g s c", a=2, c=C, g=G)
                m = mask[:, :].rearrange("p (g s) -> p g s", g=G)
                for s in range(S):
                    pool.wait_ge(L.s["lin"], L.at["lin"] + s + 1)
                    pool.tensor_tensor(to_ab[:, :, :, s, :],
                                       TMP[:, s % 2, 0:LIN].rearrange("p (a g c) -> p a g c", a=2, g=G),
                                       m[:, :, s].unsqueeze(1).unsqueeze(3).to_broadcast([N, 2, G, C]), ALU.mult)\
                        .then_inc(L.s["ab"], 1)
                    if s % 4 == 3 and s > 4:
                        add_x(s // 4 - 1)
                add_x(S // 4 - 1)
            else:
                for b in range(S // 4):
                    add_x(b)
            pool.wait_ge(L.s["xb"], L.at["xb"] + S // 4)
            for t in range(TRI_LN + LN_STEPS if after else S // 4 + 4):
                b = t - 3
                if 0 <= b < S // 4:
                    pool.wait_ge(L.s["o_rstd"], L.at["o_rstd"] + b + 1)
                    g = GATE[:, b * BANK:(b + 1) * BANK].rearrange("p (n c) -> p n c", c=C)
                    pool.tensor_tensor(g, g, stats[:, 3, 16 * b:16 * b + 16].unsqueeze(2).to_broadcast([N, 16, C]),
                                       ALU.mult).then_inc(L.s["o_rg"], 1)
                b = t - 4
                if 0 <= b < S // 4:
                    pool.wait_ge(L.s["o_mul"], L.at["o_mul"] + b + 1)
                    pool.tensor_tensor(X4[:, :, 4 * b:4 * b + 4, :].rearrange("p g s c -> p s g c"),
                                       XB[:, b * BANK:(b + 1) * BANK].rearrange("p (s g c) -> p s g c", s=4, g=G),
                                       TMP[:, b % 2, 0:BANK].rearrange("p (s g c) -> p s g c", s=4, g=G), ALU.add)\
                        .then_inc(L.s["done"], 1)
                if after:
                    ln_pool_step(pool, after, t - TRI_LN)

        def turn_x_pe(pe, V):
            src = V.src[:, :].rearrange("p (n c) -> p c n", c=C)
            wait_all(pe, V.ready)
            for b in range(C // 4):
                if b >= 4:
                    pe.wait_ge(V.s["dve" if b % 2 else "act"], V.at["dve" if b % 2 else "act"] + b // 2 - 1)
                for k in range(4):
                    m = pe.transpose(bank(b % 4)[:, k * N:(k + 1) * N], src[:, 4 * b + k, :], ident[:, :])
                m.then_inc(V.s["ps"], 1)

        def turn_x_copy(eng, V, odd):
            dst = V.dst[:, :].rearrange("p (n c) -> p c n", c=C)
            for b in range(odd, C // 4, 2):
                eng.wait_ge(V.s["ps"], V.at["ps"] + b + 1)
                src = bank(b % 4).rearrange("p (c n) -> p c n", c=4)
                if odd:
                    eng.tensor_copy(dst[:, 4 * b:4 * b + 4, :], src).then_inc(V.s["dve"], 1)
                else:
                    eng.activation(dst[:, 4 * b:4 * b + 4, :], src, ACT.Copy).then_inc(V.s["act"], 1)
        LOG = AB[:, 0:SEGT + K0]
        REPL = AB[:, SEGT + K0:2 * (SEGT + K0)]
        PROB = SQR[:, 0:SEGT]
        WGT = SQR[:, SEGT:2 * SEGT]
        WT = GATE[:, 0:SEGI * N].rearrange("p (i f) -> p i f", i=SEGI)
        PM = TMP[:, 0, 0:SEG * C].rearrange("p (s c) -> p s c", s=SEG)
        best = sb("best", [N, 4 * K0])
        top = sb("top", [N, 6, K0])
        cand = sb("cand", [E0, 4, SEG * K0 + 1])
        small = sb("small", [N, 16])
        pool32 = sb("pool32", [N, C])
        w1 = sb("w1", [C + 1, E0, H0])
        w2 = sb("w2", [H0, E0, C])
        w2l = sb("w2l", [C, E0])
        hid = sb("hid", [N, 2, E0])
        o2 = sb("o2", [C, SEG, E0])
        outm = sb("outm", [N, SEG, C])

        def f0_weights_dve(dve):
            v = gw[:, :, :].rearrange("p q (b r e) -> p q b r e", b=G, r=2)
            for q in range(2):
                dve.tensor_tensor(v[:, q, :, q, :], pcol("gate").unsqueeze(1).to_broadcast([GC, G, E0]),
                                  m4[:, :].unsqueeze(2).to_broadcast([GC, G, E0]), ALU.mult).then_inc(f0.s["w_dve"], 1)

        def f0_pe(pe):
            L = f0
            pe.wait_ge(L.s["w_dve"], L.at["w_dve"] + 2)
            for b in range(-1, S // 4):
                if b + 1 < S // 4:
                    turn_z_pe(pe, L, b + 1)
                if b >= 0:
                    q, r = b // 4, b % 4
                    pe.wait_ge(L.s["zt"], L.at["zt"] + b + 1)
                    m = pe.matmul(bank(2 + r), gw[:, q, :], ZT[:, 4 * b:4 * b + 4, :], start=(q == 0), stop=(q == 1))
                    if q == 1:
                        m.then_inc(L.s["lg_ps"], 1)
            pe.wait_ge(L.s["top"], L.at["top"] + 1)
            for s in range(SEG):
                m = pe.matmul(bank(6)[0:E0, s * K0:(s + 1) * K0], ident[:, s * E0:(s + 1) * E0], top[:, 0, :],
                              start=True, stop=True)
            m.then_inc(L.s["cand_ps"], 1)
            pe.wait_ge(L.s["fin"], L.at["fin"] + 4)
            pe.matmul(bank(7)[:, 0:SEG * K0 + 1], e16[:, :, :], cand[:, 3, :], start=True, stop=True)\
                .then_inc(L.s["mk_ps"], 1)
            pe.wait_ge(L.s["lg_act"], L.at["lg_act"] + 4)
            later_weights_pe(pe)
            zi = Z[:, :].rearrange("p (r i g c) -> p i g r c", r=2, i=SEGI, g=G)

            def pool_rows(b):
                name = "wt_dve" if b % 2 else "wt_act"
                pe.wait_ge(L.s[name], L.at[name] + b // 2 + 1)
                for i in range(4 * b, 4 * b + 4):
                    m = pe.matmul(bank(7)[:, 128:128 + SEG * C], WT[:, i, :], zi[:, i], start=(i == 0), stop=(i == SEGI - 1))
                return m

            pe.wait_ge(L.s["w"], L.at["w"] + 1)
            for b in range(SEGI // 4):
                if b >= 2:
                    pe.wait_ge(L.s["wt_dve" if b % 2 else "wt_act"], L.at["wt_dve" if b % 2 else "wt_act"] + b // 2)
                for k in range(4):
                    i = 4 * b + k
                    m = pe.transpose(bank(b % 2)[:, k * N:(k + 1) * N], WGT[:, i * N:(i + 1) * N], ident[:, :])
                m.then_inc(L.s["wt_ps"], 1)
                if b == 1:
                    pe.wait_ge(L.s["esum"], L.at["esum"] + 1)
                    pe.matmul(bank(6)[:, 256:257], same16[:, :, :], small[:, 4:5], start=True, stop=True)\
                        .then_inc(L.s["tot_ps"], 1)
                if b >= 1:
                    pool_rows(b - 1)
            pool_rows(SEGI // 4 - 1).then_inc(L.s["pool_ps"], 1)
            pe.wait_ge(L.s["pl"], L.at["pl"] + 2)
            pe.matmul(bank(6)[0:C, 264:264 + E0], pool32[:, :], d16[:, :], start=True, stop=True).then_inc(L.s["plt_ps"], 1)
            pe.wait_ge(L.s["plt"], L.at["plt"] + 1)
            pe.wait_ge(L.s["pad"], L.at["pad"] + 2)
            pe.wait_ge(par_in, PAR_LOADS)
            for e in range(E0):
                m = pe.matmul(bank(6)[:, 288 + e:289 + e], w1[:, e, :], hid[0:C + 1, 0, e:e + 1], start=True, stop=True)
            m.then_inc(L.s["h_ps"], 1)
            pe.wait_ge(L.s["h"], L.at["h"] + 1)
            for e in range(E0):
                m = pe.matmul(bank(6)[0:C, 320 + e:321 + e], w2[:, e, :], hid[:, 1, e:e + 1], start=True, stop=True)
            m.then_inc(L.s["o_ps"], 1)
            pe.wait_ge(L.s["plt"], L.at["plt"] + 2)
            pe.matmul(bank(6)[:, 352:352 + C], o2[:, :, :], ident[0:C, 0:C], start=True, stop=True).then_inc(L.s["outm_ps"], 1)
            pe.wait_ge(L.s["outm"], L.at["outm"] + 1)
            for V in (t1, t3):
                pe.wait_ge(V.s["w_dve"], V.at["w_dve"] + TRI_W)
            for b in range(SEGI // 2):
                if b >= 4:
                    pe.wait_ge(L.s["done"], L.at["done"] + b - 3)
                for k in range(2):
                    i = 2 * b + k
                    m = pe.matmul(bank(b % 4)[:, k * SEG * C:(k + 1) * SEG * C], WGT[:, i * N:(i + 1) * N],
                                  outm[:, :, :], start=True, stop=True)
                m.then_inc(L.s["y_ps"], 1)

        def f0_act(act):
            L = f0
            for b in range(4):
                act.wait_ge(L.s["lg_ps"], L.at["lg_ps"] + b + 1)
                act.activation(LOG[:, b * BANK:(b + 1) * BANK], bank(2 + b), ACT.Identity, bias=pcol("gate_b"))\
                    .then_inc(L.s["lg_act"], 1)
            act.wait_ge(L.s["neg"], L.at["neg"] + 1)
            act.activation(PROB, LOG[:, 0:SEGT], ACT.Exp, bias=small[:, 0:1], accum_out=small[:, 1:2])\
                .then_inc(L.s["exp"], 1)
            act.wait_ge(L.s["mk"], L.at["mk"] + 2)
            act.activation(small[:, 3:4], small[:, 6:7], ACT.Exp, bias=top[:, 0, 0:1], scale=-1.0)\
                .then_inc(L.s["exp"], 1)
            warm_table(act, ACT.Gelu)
            for b in range(0, SEGI // 4, 2):
                act.wait_ge(L.s["wt_ps"], L.at["wt_ps"] + b + 1)
                act.activation(WT[:, 4 * b:4 * b + 4, :], bank(b % 2), ACT.Copy).then_inc(L.s["wt_act"], 1)
            act.wait_ge(L.s["h_ps"], L.at["h_ps"] + 1)
            act.activation(hid[:, 1, :], bank(6)[:, 288:288 + E0], ACT.Gelu).then_inc(L.s["h"], 1)

        def f0_pool(pool):
            pool.memset(LOG[:, SEGT:], -FAR).then_inc(f0.s["pad"], 1)
            pool.wait_ge(f0.s["pad"], 1)
            pool.memset(hid[C:C + 1, 0, :], 1.0).then_inc(f0.s["pad"], 1)
            pool.wait_ge(f0.s["pad"], 2)

        def f0_dve(dve):
            L = f0
            for b in range(4):
                dve.wait_ge(L.s["lg_act"], L.at["lg_act"] + b + 1)
                dve.max(best[:, b * K0:(b + 1) * K0], LOG[:, b * BANK:(b + 1) * BANK]).then_inc(L.s["best"], 1)
            dve.wait_ge(L.s["best"], L.at["best"] + 4)
            dve.max(top[:, 0, :], best[:, :]).then_inc(L.s["top"], 1)
            dve.wait_ge(L.s["top"], L.at["top"] + 1)
            dve.tensor_scalar(small[:, 0:1], top[:, 0, 0:1], -1.0, None, ALU.mult).then_inc(L.s["neg"], 1)
            dve.wait_ge(L.s["pad"], L.at["pad"] + 2)
            dve.wait_ge(L.s["cand_ps"], L.at["cand_ps"] + 1)
            nk = SEG * K0
            dve.tensor_copy(cand[:, 0, 0:nk], bank(6)[0:E0, 0:nk]).then_inc(L.s["cand"], 1)
            dve.wait_ge(L.s["cand"], L.at["cand"] + 1)
            dve.max(cand[:, 1, 0:K0], cand[:, 0, 0:nk]).then_inc(L.s["fin"], 1)
            dve.wait_ge(L.s["fin"], L.at["fin"] + 1)
            dve.match_replace(out=cand[:, 2, 0:nk], in_to_replace=cand[:, 1, 0:K0], in_values=cand[:, 0, 0:nk],
                              imm_value=-3.0 * FAR).then_inc(L.s["fin"], 1)
            dve.wait_ge(L.s["fin"], L.at["fin"] + 2)
            dve.tensor_tensor(cand[:, 3, 0:nk], cand[:, 2, 0:nk], cand[:, 0, 0:nk], ALU.not_equal).then_inc(L.s["fin"], 1)
            dve.tensor_copy(cand[:, 3, nk:nk + 1], cand[:, 1, 0:1]).then_inc(L.s["fin"], 1)
            dve.wait_ge(L.s["mk_ps"], L.at["mk_ps"] + 1)
            seg = TMP[:, 1, 0:nk].rearrange("p (s k) -> p s k", s=SEG)
            dve.tensor_tensor(seg, bank(7, nk).rearrange("p (s k) -> p s k", s=SEG),
                              m8[:, :].unsqueeze(2).to_broadcast([N, SEG, K0]), ALU.mult).then_inc(L.s["mk"], 1)
            dve.tensor_copy(small[:, 6:7], bank(7)[:, nk:nk + 1]).then_inc(L.s["mk"], 1)
            dve.wait_ge(L.s["mk"], L.at["mk"] + 1)
            dve.tensor_reduce(top[:, 1, :], seg.rearrange("p s k -> p k s"), AX.X, ALU.add).then_inc(L.s["sel"], 1)
            dve.wait_ge(L.s["sel"], L.at["sel"] + 1)
            dve.tensor_tensor(top[:, 2, :], top[:, 1, :], top[:, 0, :], ALU.mult).then_inc(L.s["sel"], 1)
            dve.tensor_scalar(top[:, 3, :], top[:, 1, :], -1.0, FAR, ALU.add, ALU.mult).then_inc(L.s["sel"], 1)
            dve.wait_ge(L.s["sel"], L.at["sel"] + 3)
            dve.tensor_tensor(top[:, 4, :], top[:, 2, :], top[:, 3, :], ALU.add).then_inc(L.s["sel"], 1)
            dve.wait_ge(L.s["sel"], L.at["sel"] + 4)
            dve.match_replace(out=REPL, in_to_replace=top[:, 4, :], in_values=LOG, imm_value=-3.0 * FAR)\
                .then_inc(L.s["sel"], 1)
            dve.wait_ge(L.s["sel"], L.at["sel"] + 5)
            dve.wait_ge(L.s["exp"], L.at["exp"] + 1)
            dve.scalar_tensor_tensor(out=WGT, in0=REPL[:, 0:SEGT], scalar=-2.0 * FAR, in1=PROB, op0=ALU.is_lt, op1=ALU.mult)\
                .then_inc(L.s["w"], 1)
            dve.wait_ge(L.s["exp"], L.at["exp"] + 2)
            dve.tensor_tensor(small[:, 4:5], small[:, 1:2], small[:, 3:4], ALU.mult).then_inc(L.s["esum"], 1)
            for b in range(1, SEGI // 4, 2):
                dve.wait_ge(L.s["wt_ps"], L.at["wt_ps"] + b + 1)
                dve.tensor_copy(WT[:, 4 * b:4 * b + 4, :], bank(b % 2)).then_inc(L.s["wt_dve"], 1)
                if b == 1:
                    dve.wait_ge(L.s["tot_ps"], L.at["tot_ps"] + 1)
                    dve.reciprocal(small[:, 2:3], bank(6)[:, 256:257]).then_inc(L.s["tot"], 1)
                    dve.wait_ge(L.s["tot"], L.at["tot"] + 1)
                    dve.tensor_tensor(small[:, 5:6], small[:, 2:3], small[:, 3:4], ALU.mult).then_inc(L.s["tot"], 1)
            later_weights_dve(dve)
            dve.wait_ge(L.s["pool_ps"], L.at["pool_ps"] + 1)
            own = m8[:, :].unsqueeze(2).to_broadcast([N, SEG, C])
            dve.wait_ge(L.s["tot"], L.at["tot"] + 2)
            dve.scalar_tensor_tensor(out=PM, in0=bank(7)[:, 128:128 + SEG * C].rearrange("p (s c) -> p s c", s=SEG),
                                     scalar=small[:, 5:6], in1=own, op0=ALU.mult, op1=ALU.mult)\
                .then_inc(L.s["pl"], 1)
            dve.wait_ge(L.s["pl"], L.at["pl"] + 1)
            dve.tensor_reduce(pool32[:, :], PM.rearrange("p s c -> p c s"), AX.X, ALU.add).then_inc(L.s["pl"], 1)
            dve.wait_ge(L.s["plt_ps"], L.at["plt_ps"] + 1)
            dve.tensor_copy(hid[0:C, 0, :], bank(6)[0:C, 264:264 + E0]).then_inc(L.s["plt"], 1)
            dve.wait_ge(L.s["o_ps"], L.at["o_ps"] + 1)
            dve.tensor_tensor(o2[:, :, :], bank(6)[0:C, 320:320 + E0].unsqueeze(1).to_broadcast([C, SEG, E0]),
                              w2l[:, :].unsqueeze(1).to_broadcast([C, SEG, E0]), ALU.add).then_inc(L.s["plt"], 1)
            dve.wait_ge(L.s["outm_ps"], L.at["outm_ps"] + 1)
            dve.scalar_tensor_tensor(out=outm[:, :, :], in0=bank(6)[:, 352:352 + C].unsqueeze(1).to_broadcast([N, SEG, C]),
                                     scalar=small[:, 5:6], in1=own, op0=ALU.mult, op1=ALU.mult)\
                .then_inc(L.s["outm"], 1)
            xi = XC[:, :].rearrange("p (s i c) -> p i s c", s=SEG, i=SEGI)
            for b in range(SEGI // 2):
                dve.wait_ge(L.s["y_ps"], L.at["y_ps"] + b + 1)
                for k in range(2):
                    x = xi[:, 2 * b + k]
                    i = dve.tensor_tensor(x, x, bank(b % 4)[:, k * SEG * C:(k + 1) * SEG * C]
                                          .rearrange("p (s c) -> p s c", s=SEG), ALU.add)
                i.then_inc(L.s["done"], 1)
                if b % 2:
                    ln_dve_step(dve, t1, b // 2)
            for u in range(SEGI // 4, LN_STEPS):
                ln_dve_step(dve, t1, u)

        Y = AB[:, 0:NC + 1]
        starts = Y[:, 0:NC:CHUNK]
        old = sb("old", [GC, 2, NCH])
        bns = sb("bns", [GC, 8, 6])
        mv = sb("mv", [GC, 12])
        flag_f = sb("flag_f", [1, 1])
        flag_i = sb("flag_i", [1, 1], I32)
        wbn = sb("wbn", [GC, GC])
        wbnt = sb("wbnt", [GC, GC])
        rec_w = {}
        for L in (r1, r2):
            rec_w[L.name] = {k: sb(f"{L.name}_{k}", [GC, GC]) for k in ("wbd", "wraw", "vt")}
            rec_w[L.name] |= {"wbn": wbn, "wbnt": wbnt}

        def rec_weights1_dve(dve, L):
            W = rec_w[L.name]
            for name, key in (("W", "wbd"), ("VT", "vt")):
                dve.tensor_tensor(W[key][:, :].rearrange("p (g c) -> p g c", g=G),
                                  pcol(f"{L.name}_{name}").unsqueeze(1).to_broadcast([GC, G, C]),
                                  m4[:, :].unsqueeze(2).to_broadcast([GC, G, C]), ALU.mult).then_inc(L.s["w_half"], 1)

        def rec_weights2_dve(dve, L):
            dve.wait_ge(L.s["w_pe"], L.at["w_pe"] + 1)
            dve.tensor_copy(rec_w[L.name]["wraw"][:, :], bank(L.wbank)[:, L.wcol:L.wcol + GC]).then_inc(L.s["w_dve"], 1)

        def rec_weights_pe(pe, L):
            pe.wait_ge(L.s["w_half"], L.at["w_half"] + 2)
            pe.transpose(bank(L.wbank)[:, L.wcol:L.wcol + GC], rec_w[L.name]["wbd"][:, :], ident[:, :])\
                .then_inc(L.s["w_pe"], 1)

        ztk = ZT[:, :, :].rearrange("p s f -> p (s f)")

        def chunks(t, off, h):
            return t[:, bass.ds(off + h * NS * CHUNK, NS, CHUNK)]

        def rec_step(pe, L, off, k, h):
            W, o = rec_w[L.name], bank(2 * h + k, NS)
            return (pe.matmul(o, W["wbnt"][:, :], chunks(ztk, off, h), start=True, stop=False),
                    lambda: pe.matmul(o, W["vt"][:, :], chunks(Y, off, h), start=False, stop=True))

        def rec_pe(pe, L):
            W = rec_w[L.name]

            def turn_y(b):
                for s in range(4 * b, 4 * b + 4):
                    m = pe.transpose(bank(4 + b % 4)[:, s % 4 * N:(s % 4 + 1) * N], Y[:, 1 + s * N:1 + (s + 1) * N],
                                     ident[:, :])
                return m

            pe.wait_ge(L.s["w_dve"], L.at["w_dve"] + 1)
            for b in range(-1, 8):
                if b < 7:
                    turn_z_pe(pe, L, b + 1)
                if b < 0:
                    continue
                if b == 0:
                    wait_all(pe, L.banks_free)
                pe.wait_ge(L.s["zt"], L.at["zt"] + b + 1)
                if b >= 4:
                    pe.wait_ge(L.s["wx"], L.at["wx"] + b - 3)
                pe.matmul(bank(2 + b % 4), W["wraw"][:, :], ZT[:, 4 * b:4 * b + 4, :], start=True, stop=True)\
                    .then_inc(L.s["wx_ps"], 1)
            same = same32[:, :, :]
            pe.wait_ge(L.s["bn"], L.at["bn"] + 1)
            pe.matmul(bank(6)[:, 0:1], same, mv[:, 0:1], start=True, stop=True).then_inc(L.s["bn_ps"], 1)
            pe.wait_ge(L.s["bn"], L.at["bn"] + 4)
            pe.matmul(bank(7)[:, 0:1], same, mv[:, 4:5], start=True, stop=True).then_inc(L.s["bn_ps"], 1)
            pe.wait_ge(L.s["bnw"], L.at["bnw"] + 4)
            pe.transpose(bank(6)[:, 0:GC], W["wbn"][:, :], ident[:, :]).then_inc(L.s["bn_ps"], 1)
            pe.wait_ge(L.s["bnw"], L.at["bnw"] + 5)
            for r, (first, steps, before) in enumerate(ROUNDS):
                if r >= 1:
                    for h in range(STREAMS):
                        pe.wait_ge(L.s[f"step_y{h}"], L.at[f"step_y{h}"] + before + 1)
                    pe.matmul(bank(4, 1), shift[:, :], Y[:, NC:NC + 1], start=True, stop=True)\
                        .then_inc(L.s["edge_ps"], 1)
                    pe.wait_ge(L.s["edge"], L.at["edge"] + 2 * r)
                for k in range(steps):
                    for h in range(STREAMS):
                        _, recur = rec_step(pe, L, first + k, k % 2, h)
                        pe.wait_ge(L.s[f"step_y{h}"], L.at[f"step_y{h}"] + before + k + 1)
                        recur().then_inc(L.s["step_ps"], 1)
            for h in range(STREAMS):
                pe.wait_ge(L.s[f"step_y{h}"], L.at[f"step_y{h}"] + STEPS + 1)
            pe.matmul(bank(0, 1), shift[:, :], Y[:, NC:NC + 1], start=True, stop=True).then_inc(L.s["edge_ps"], 1)
            turn_y(0).then_inc(L.s["y_ps"], 1)
            turn_y(1).then_inc(L.s["y_ps"], 1)
            pe.wait_ge(L.s["chk"], L.at["chk"] + 3)
            pe.transpose(bank(1)[0:1, 0:GC], mv[:, 10:11], ident[:, :]).then_inc(L.s["chk_ps"], 1)
            turn_y(2).then_inc(L.s["y_ps"], 1)
            turn_y(3).then_inc(L.s["y_ps"], 1)
            pe.wait_ge(L.s["flag"], L.at["flag"] + 2)
            differs = pe.value_load(flag_i[0:1, 0:1], min_val=0, max_val=1)
            with pe.If(differs != 0):
                with pe.Fori(0, GENERAL_ROUNDS) as r:
                    for h in range(STREAMS):
                        pe.wait_ge(L.s[f"g_y{h}"], r * CHUNK + (L.at[f"g_y{h}"] + 1))
                    pe.matmul(bank(4, 1), shift[:, :], Y[:, NC:NC + 1], start=True, stop=True)\
                        .then_inc(L.s["g_edge_ps"], 1)
                    with pe.Fori(0, CHUNK // 2) as pair:
                        for k in range(2):
                            for h in range(STREAMS):
                                if k == h == 0:
                                    pe.wait_ge(L.s["g_edge"], L.at["g_edge"] + r + 1)
                                _, recur = rec_step(pe, L, pair * 2 + k, k, h)
                                pe.wait_ge(L.s[f"g_y{h}"], r * CHUNK + pair * 2 + (L.at[f"g_y{h}"] + k + 1))
                                recur().then_inc(L.s["g_ps"], 1)
                for h in range(STREAMS):
                    pe.wait_ge(L.s[f"g_y{h}"], L.at[f"g_y{h}"] + GENERAL_ROUNDS * CHUNK + 1)
                for b in range(4):
                    m = turn_y(b)
                m.then_inc(L.s["g_turned"], 1)
            for b in range(4, S // 4):
                pe.wait_ge(L.s["done"], L.at["done"] + b - 3)
                turn_y(b).then_inc(L.s["y_ps"], 1)

        def rec_act(act, L):
            act.wait_ge(L.s["bnc"], L.at["bnc"] + 1)
            act.activation(mv[:, 6:7], mv[:, 5:6], ACT.Sqrt, bias=eps[:, 1:2]).then_inc(L.s["std1"], 1)
            warm_table(act, ACT.Sigmoid)
            act.wait_ge(L.s["bnw"], L.at["bnw"] + 3)
            bias = mv[:, 9:10]
            for first, steps, before in ROUNDS:
                for k in range(steps):
                    for h in range(STREAMS):
                        act.wait_ge(L.s["step_ps"], L.at["step_ps"] + 2 * (before + k) + h + 1)
                        act.activation(chunks(Y, first + k + 1, h), bank(2 * h + k % 2, NS), ACT.Sigmoid,
                                       bias=bias).then_inc(L.s[f"step_y{h}"], 1)
            act.wait_ge(L.s["flag"], L.at["flag"] + 2)
            differs = act.value_load(flag_i[0:1, 0:1], min_val=0, max_val=1)
            with act.If(differs != 0):
                with act.Fori(0, GENERAL_ROUNDS) as r:
                    with act.Fori(0, CHUNK // 2) as pair:
                        for k in range(2):
                            for h in range(STREAMS):
                                act.wait_ge(L.s["g_ps"], r * (2 * CHUNK) + pair * 4 + (L.at["g_ps"] + 2 * k + h + 1))
                                act.activation(chunks(Y, pair * 2 + (k + 1), h), bank(2 * h + k, NS), ACT.Sigmoid,
                                               bias=bias).then_inc(L.s[f"g_y{h}"], 1)

        def rec_pool(pool, L):
            pool.wait_ge(L.s["z"], L.at["z"] + Q)
            for h in range(STREAMS):
                pool.memset(chunks(Y, CHUNK - WARM, h), 0.0).then_inc(L.s[f"step_y{h}"], 1)

        def set_flag(dve, L, differences):
            dve.wait_ge(L.s["chk_ps"], L.at["chk_ps"] + 1)
            dve.tensor_reduce(flag_f[:, :], differences, AX.X, ALU.max).then_inc(L.s["flag"], 1)
            dve.wait_ge(L.s["flag"], L.at["flag"] + 1)
            dve.tensor_scalar(flag_i[:, :], flag_f[:, :], FIXED_TOL, None, ALU.is_gt).then_inc(L.s["flag"], 1)

        def rec_dve(dve, L, after):
            W = rec_w[L.name]
            for b in range(8):
                dve.wait_ge(L.s["wx_ps"], L.at["wx_ps"] + b + 1)
                dve.bn_stats(bns[:, b, :], bank(2 + b % 4)).then_inc(L.s["wx"], 1)
            dve.wait_ge(L.s["wx"], L.at["wx"] + 8)
            dve.bn_aggr(mv[:, 0:2], bns[:, :, :].rearrange("p b k -> p (b k)")).then_inc(L.s["bn"], 1)
            dve.wait_ge(L.s["bn_ps"], L.at["bn_ps"] + 1)
            dve.wait_ge(L.s["bn"], L.at["bn"] + 1)
            dve.tensor_tensor(mv[:, 2:3], mv[:, 0:1], bank(6, 1), ALU.subtract).then_inc(L.s["bn"], 1)
            dve.wait_ge(L.s["bn"], L.at["bn"] + 2)
            dve.tensor_tensor(mv[:, 3:4], mv[:, 2:3], mv[:, 2:3], ALU.mult).then_inc(L.s["bn"], 1)
            dve.wait_ge(L.s["bn"], L.at["bn"] + 3)
            dve.tensor_tensor(mv[:, 4:5], mv[:, 3:4], mv[:, 1:2], ALU.add).then_inc(L.s["bn"], 1)
            dve.wait_ge(L.s["bn_ps"], L.at["bn_ps"] + 2)
            dve.tensor_copy(mv[:, 5:6], bank(7, 1)).then_inc(L.s["bnc"], 1)
            dve.wait_ge(L.s["std1"], L.at["std1"] + 1)
            dve.reciprocal(mv[:, 7:8], mv[:, 6:7]).then_inc(L.s["bnw"], 1)
            dve.wait_ge(L.s["bnw"], L.at["bnw"] + 1)
            dve.tensor_tensor(mv[:, 8:9], mv[:, 7:8], pcol(f"{L.name}_gamma"), ALU.mult).then_inc(L.s["bnw"], 1)
            dve.wait_ge(L.s["bnw"], L.at["bnw"] + 2)
            dve.tensor_tensor(mv[:, 11:12], bank(6, 1), mv[:, 8:9], ALU.mult).then_inc(L.s["bnc"], 1)
            dve.wait_ge(L.s["bnc"], L.at["bnc"] + 2)
            dve.tensor_tensor(mv[:, 9:10], pcol(f"{L.name}_beta"), mv[:, 11:12], ALU.subtract).then_inc(L.s["bnw"], 1)
            dve.tensor_scalar(W["wbn"][:, :], W["wbd"][:, :], mv[:, 8:9], None, ALU.mult).then_inc(L.s["bnw"], 1)
            dve.wait_ge(L.s["bn_ps"], L.at["bn_ps"] + 3)
            dve.tensor_copy(W["wbnt"][:, :], bank(6, GC)).then_inc(L.s["bnw"], 1)
            dve.wait_ge(L.s["edge_ps"], L.at["edge_ps"] + 1)
            dve.tensor_copy(Y[:, 0:1], bank(4, 1)).then_inc(L.s["edge"], 1)
            dve.wait_ge(L.s["edge"], L.at["edge"] + 1)
            dve.tensor_copy(old[:, 0, :], starts).then_inc(L.s["edge"], 1)
            dve.wait_ge(L.s["edge_ps"], L.at["edge_ps"] + 2)
            dve.tensor_copy(Y[:, 0:1], bank(0, 1)).then_inc(L.s["chk"], 1)
            dve.wait_ge(L.s["chk"], L.at["chk"] + 1)
            dve.tensor_tensor(old[:, 1, :], old[:, 0, :], starts, ALU.subtract).then_inc(L.s["chk"], 1)
            dve.wait_ge(L.s["chk"], L.at["chk"] + 2)
            dve.tensor_reduce(mv[:, 10:11], old[:, 1, :], AX.X, ALU.max, apply_absolute_value=True)\
                .then_inc(L.s["chk"], 1)
            set_flag(dve, L, bank(1)[0:1, 0:GC])
            for h in range(STREAMS):
                dve.engine_nop().then_inc(L.s[f"g_y{h}"], 1)
            dve.wait_ge(L.s["flag"], L.at["flag"] + 2)
            differs = dve.value_load(flag_i[0:1, 0:1], min_val=0, max_val=1)
            with dve.If(differs != 0):
                with dve.Fori(0, GENERAL_ROUNDS) as r:
                    dve.wait_ge(L.s["g_edge_ps"], L.at["g_edge_ps"] + r + 1)
                    dve.tensor_copy(Y[:, 0:1], bank(4, 1)).then_inc(L.s["g_edge"], 1)
                dve.wait_ge(L.s["g_turned"], L.at["g_turned"] + 1)
            X4 = blocks(XC)
            for b in range(1 + LN_STEPS if after else S // 4):
                if b < S // 4:
                    dve.wait_ge(L.s["y_ps"], L.at["y_ps"] + b + 1)
                    x = X4[:, :, 4 * b:4 * b + 4, :].rearrange("p g s c -> p s g c")
                    dve.tensor_tensor(x, x, bank(4 + b % 4).rearrange("p (s g c) -> p s g c", s=4, g=G), ALU.add)\
                        .then_inc(L.s["done"], 1)
                if after:
                    ln_dve_step(dve, after, b - 1)

        NB = N // G
        ROWB = NB + 2
        RIN = GATE[:, :].rearrange("p (i n) -> p i n", i=N)
        SCN = AB[:, 0:(N + 1) * ROWB].rearrange("p (i n) -> p i n", n=ROWB)
        ends = SCN[:, 0:N:CHUNK, 1:1 + NB]
        kept = TMP[:, 0, 0:ROWCH * NB].rearrange("p (k n) -> p k n", n=NB)
        differ = TMP[:, 1, 0:ROWCH * NB]
        toep = sb("toep", [GC, 3, G, C])

        def scan_weights_pool(pool):
            pool.memset(toep[:, :, :, :], 0.0).then_inc(sc.s["w_dve"], 1)
            pool.wait_ge(sc.s["w_dve"], sc.at["w_dve"] + 1)
            pool.wait_ge(par_first, PAR_FIRST)
            a = PAR["conv"][0]
            for m in range(G):
                for b in range(3):
                    for mo in range(G):
                        tap = TAPS // 2 + G * (b - 1) + m - mo
                        if 0 <= tap < TAPS:
                            pool.tensor_copy(toep[m * C:(m + 1) * C, b, mo, :],
                                             par[m * C:(m + 1) * C, a + tap * C:a + (tap + 1) * C])\
                                .then_inc(sc.s["w_pool"], 1)
            pool.wait_ge(sc.s["w_pool"], SCAN_COPIES)

        def scan_rows(t, off, h):
            return t[:, bass.ds(off + h * ROWS_S * CHUNK, ROWS_S, CHUNK), :]

        def scan_pool(pool):
            L = sc
            pool.wait_ge(L.s["z"], L.at["z"] + Q)
            pool.memset(SCN[:, 0, :], 0.0).then_inc(L.s["pads"], 1)
            pool.memset(SCN[:, 1:, 0:ROWB:ROWB - 1], 0.0).then_inc(L.s["pads"], 1)
            pool.wait_ge(L.s["zt"], L.at["zt"] + NB // 4)
            for h in range(STREAMS):
                pool.tensor_copy(scan_rows(SCN[:, :, 1:1 + NB], CHUNK - WARM, h), scan_rows(RIN, CHUNK - WARM - 1, h))\
                    .then_inc(L.s[f"row{h}"], 1)

        def scan_pe(pe):
            L = sc
            turn_all_z_pe(pe, L)
            pe.wait_ge(L.s["pads"], L.at["pads"] + 2)
            pe.wait_ge(L.s["w_pool"], L.at["w_pool"] + SCAN_COPIES)

            def turn_rows(b):
                for n in range(4 * b, 4 * b + 4):
                    m = pe.transpose(bank(4 + b % 4)[:, n % 4 * N:(n % 4 + 1) * N], SCN[:, 1:, 1 + n], ident[:, :])
                return m

            def step(off, h):
                for b in range(3):
                    m = pe.matmul(bank(2 + h, ROWS_S * NB), toep[:, b, :, :], scan_rows(SCN[:, :, b:b + NB], off, h),
                                  start=(b == 0), stop=(b == 2))
                return m

            for r, (first, steps, before) in enumerate(ROUNDS):
                if r >= 1:
                    for h in range(STREAMS):
                        pe.wait_ge(L.s[f"row{h}"], L.at[f"row{h}"] + before + 1)
                    pe.wait_ge(L.s["kept"], L.at["kept"] + 1)
                for k in range(steps):
                    for h in range(STREAMS):
                        pe.wait_ge(L.s[f"row{h}"], L.at[f"row{h}"] + before + k + 1)
                        step(first + k, h).then_inc(L.s["conv"], 1)
            for h in range(STREAMS):
                pe.wait_ge(L.s[f"row{h}"], L.at[f"row{h}"] + STEPS + 1)
            turn_rows(0).then_inc(L.s["y_ps"], 1)
            turn_rows(1).then_inc(L.s["y_ps"], 1)
            pe.wait_ge(L.s["chk"], L.at["chk"] + 2)
            pe.transpose(bank(1)[0:1, 0:GC], mv[:, 10:11], ident[:, :]).then_inc(L.s["chk_ps"], 1)
            turn_rows(2).then_inc(L.s["y_ps"], 1)
            turn_rows(3).then_inc(L.s["y_ps"], 1)
            pe.wait_ge(L.s["flag"], L.at["flag"] + 2)
            differs = pe.value_load(flag_i[0:1, 0:1], min_val=0, max_val=1)
            with pe.If(differs != 0):
                with pe.Fori(0, GENERAL_SCANS) as r:
                    with pe.Fori(0, CHUNK // 2) as pair:
                        for k in range(2):
                            for h in range(STREAMS):
                                if k == h == 0:
                                    pe.wait_ge(L.s["g_row1"], r * CHUNK + (L.at["g_row1"] + 1))
                                pe.wait_ge(L.s[f"g_row{h}"], r * CHUNK + pair * 2 + (L.at[f"g_row{h}"] + k + 1))
                                step(pair * 2 + k, h).then_inc(L.s["g_conv"], 1)
                for h in range(STREAMS):
                    pe.wait_ge(L.s[f"g_row{h}"], L.at[f"g_row{h}"] + GENERAL_SCANS * CHUNK + 1)
                for b in range(4):
                    m = turn_rows(b)
                m.then_inc(L.s["g_turned"], 1)
            for b in range(4, NB // 4):
                pe.wait_ge(L.s["done"], L.at["done"] + b - 3)
                turn_rows(b).then_inc(L.s["y_ps"], 1)

        def scan_dve(dve):
            L = sc
            dve.wait_ge(L.s["zt"], L.at["zt"] + NB // 4)

            def row_step(off, h):
                return dve.scalar_tensor_tensor(
                    out=scan_rows(SCN[:, :, 1:1 + NB], off + 1, h),
                    in0=bank(2 + h, ROWS_S * NB).rearrange("p (k n) -> p k n", n=NB), scalar=0.0,
                    in1=scan_rows(RIN, off, h), op0=ALU.max, op1=ALU.add)

            for h in range(STREAMS):
                dve.wait_ge(L.s[f"row{h}"], L.at[f"row{h}"] + 1)
            for r, (first, steps, before) in enumerate(ROUNDS):
                if r >= 1:
                    dve.wait_ge(L.s["row0"], L.at["row0"] + before + 1)
                    dve.wait_ge(L.s["row1"], L.at["row1"] + before + 1)
                    dve.tensor_copy(kept, ends).then_inc(L.s["kept"], 1)
                    dve.wait_ge(L.s["kept"], L.at["kept"] + 1)
                for k in range(steps):
                    for h in range(STREAMS):
                        dve.wait_ge(L.s["conv"], L.at["conv"] + 2 * (before + k) + h + 1)
                        row_step(first + k, h).then_inc(L.s[f"row{h}"], 1)
            dve.wait_ge(L.s["row0"], L.at["row0"] + STEPS + 1)
            dve.wait_ge(L.s["row1"], L.at["row1"] + STEPS + 1)
            dve.tensor_tensor(differ.rearrange("p (k n) -> p k n", n=NB), kept, ends, ALU.subtract)\
                .then_inc(L.s["chk"], 1)
            dve.wait_ge(L.s["chk"], L.at["chk"] + 1)
            dve.tensor_reduce(mv[:, 10:11], differ, AX.X, ALU.max, apply_absolute_value=True).then_inc(L.s["chk"], 1)
            set_flag(dve, L, bank(1)[0:1, 0:GC])
            for h in range(STREAMS):
                dve.engine_nop().then_inc(L.s[f"g_row{h}"], 1)
            dve.wait_ge(L.s["flag"], L.at["flag"] + 2)
            differs = dve.value_load(flag_i[0:1, 0:1], min_val=0, max_val=1)
            with dve.If(differs != 0):
                with dve.Fori(0, GENERAL_SCANS) as r:
                    with dve.Fori(0, CHUNK // 2) as pair:
                        for k in range(2):
                            for h in range(STREAMS):
                                dve.wait_ge(L.s["g_conv"], r * (2 * CHUNK) + pair * 4 + (L.at["g_conv"] + 2 * k + h + 1))
                                row_step(pair * 2 + k, h).then_inc(L.s[f"g_row{h}"], 1)
                dve.wait_ge(L.s["g_turned"], L.at["g_turned"] + 1)
            for b in range(NB // 4):
                dve.wait_ge(L.s["y_ps"], L.at["y_ps"] + b + 1)
                x = XR[:, b * BANK:(b + 1) * BANK]
                dve.tensor_tensor(x, x, bank(4 + b % 4), ALU.add).then_inc(L.s["done"], 1)

        wr = sb("wr", [GC, G, E3])
        we = sb("we", [GC, E3, G, C])
        rank = sb("rank", [N, E3], BF16)
        NE = N * E3
        RT = [AB[:, k * NE:(k + 1) * NE].rearrange("p (n e) -> p n e", e=E3) for k in range(8)]
        M1, M2, DIF, W1S, W2S = (SQR[:, k * N:(k + 1) * N] for k in range(5))
        ranks16 = sb("ranks16", [N, 2, N, E3], BF16)
        rmax16 = sb("rmax16", [N, 2, N], BF16)
        RANK1, RANK2, R1M, R2M = ranks16[:, 0], ranks16[:, 1], rmax16[:, 0], rmax16[:, 1]
        HALF = Z[:, 0:2 * BANK].rearrange("p (h f) -> p h f", h=2)
        F3_LOGITS_READ = 6
        LOGITS = bank(2, n=2).rearrange("p (n e) -> p n e", e=E3)

        def f3_bank(s):
            return 2 + 2 * ((s + 1) % 3)

        F3_COLS = E3 + E3 * C

        def f3_weights_pool(pool):
            for e in range(E3):
                pool.memset(rank[:, e:e + 1], float(E3 - e)).then_inc(f3.s["rank"], 1)

        def f3_weights_dve(dve):
            L = f3
            dve.wait_ge(L.s["w_pe"], L.at["w_pe"] + 1)
            src = bank(L.wbank)
            dve.tensor_tensor(wr[:, :, :], src[:, 0:E3].unsqueeze(1).to_broadcast([GC, G, E3]),
                              m4[:, :].unsqueeze(2).to_broadcast([GC, G, E3]), ALU.mult).then_inc(L.s["w_dve"], 1)
            w, m = by_groups(src[:, E3:F3_COLS], E3)
            dve.tensor_tensor(we[:, :, :, :], w, m, ALU.mult).then_inc(L.s["w_dve"], 1)

        def f3_weights_pe(pe):
            a, b = PAR["router"][0], ROW["router_b"][0]
            fold_biases(pe, bank(f3.wbank)[:, 0:F3_COLS], par[:, a:a + F3_COLS], row[0:1, b:b + F3_COLS])\
                .then_inc(f3.s["w_pe"], 1)

        def f3_pe(pe):
            L = f3
            pe.wait_ge(L.s["w_dve"], L.at["w_dve"] + 2)

            def route(b):
                pe.wait_ge(L.s["zt"], L.at["zt"] + b + 1)
                for s in range(4 * b, 4 * b + 4):
                    m = pe.matmul(bank(2 + s // 16)[:, s % 16 * G * E3:(s % 16 + 1) * G * E3], ZT[:, s, :], wr[:, :, :],
                                  start=True, stop=True)
                return m

            for b in range(S // 4):
                turn_z_pe(pe, L, b)
                if b == 5:
                    wait_all(pe, L.early_banks_free)
                    for a in range(b - 1):
                        route(a)
                if b >= 5:
                    route(b - 1)
            wait_all(pe, L.banks_free)
            route(7).then_inc(L.s["rt_ps"], 1)
            for s in range(S):
                if s == 2:
                    pe.wait_ge(L.s["top"], L.at["top"] + F3_LOGITS_READ)
                if s >= 3:
                    pe.wait_ge(L.s["e_mul"], L.at["e_mul"] + s - 2)
                for h in range(2):
                    o = bank(f3_bank(s) + h)
                    e = slice(4 * h, 4 * h + 4)
                    m = pe.matmul(o, ZT[:, s, :], we[:, e, :, :], start=True, stop=True)
                m.then_inc(L.s["e_ps"], 1)

        def f3_act(act):
            L = f3
            act.wait_ge(L.s["diff"], L.at["diff"] + 1)
            act.activation(W1S, DIF, ACT.Sigmoid).then_inc(L.s["sg"], 1)
            act.activation(W2S, DIF, ACT.Sigmoid, scale=-1.0).then_inc(L.s["sg"], 1)

        def f3_dve(dve):
            L = f3
            n = [0]
            sm = L.s["top"]

            def then(ins):
                n[0] += 1
                ins.then_inc(sm, 1)
                dve.wait_ge(sm, n[0])

            def per_e(t):
                return t.unsqueeze(2).to_broadcast([N, N, E3])

            ranks = rank[:, :].unsqueeze(1).to_broadcast([N, N, E3])
            dve.wait_ge(L.s["rank"], L.at["rank"] + E3)
            dve.wait_ge(L.s["rt_ps"], L.at["rt_ps"] + 1)

            def choose(logits, m, rm, hot, r, second=False):
                then(dve.tensor_reduce(m, logits, AX.X, ALU.max))
                if second:
                    dve.tensor_tensor(DIF, M1, M2, ALU.subtract).then_inc(L.s["diff"], 1)
                then(dve.tensor_tensor(r, logits, per_e(m), ALU.is_equal))
                then(dve.tensor_tensor(r, r, ranks, ALU.mult))
                then(dve.tensor_reduce(rm, r, AX.X, ALU.max))
                then(dve.tensor_tensor(hot, r, per_e(rm), ALU.is_equal))

            choose(LOGITS, M1, R1M, RT[1], RANK1)
            then(dve.scalar_tensor_tensor(out=RT[2], in0=RT[1], scalar=-FAR, in1=LOGITS, op0=ALU.mult, op1=ALU.add))
            choose(RT[2], M2, R2M, RT[3], RANK2, second=True)
            dve.wait_ge(L.s["sg"], L.at["sg"] + 2)
            then(dve.tensor_tensor(RT[3], RT[3], per_e(W2S), ALU.mult))
            dve.wait_ge(L.s["hot"], L.at["hot"] + 1)
            then(dve.tensor_tensor(RT[4], RT[5], RT[3], ALU.add))
            wts = RT[4].rearrange("p (s g) e -> p s e g", g=G)

            def weigh(s):
                dve.wait_ge(L.s["e_ps"], L.at["e_ps"] + s + 1)
                if s >= 2:
                    dve.wait_ge(L.s["e_half"], L.at["e_half"] + s - 1)
                o = f3_bank(s) * BANK
                dve.tensor_tensor(TMP[:, s % 2, :].rearrange("p (e g c) -> p e g c", e=E3, g=G),
                                  PSUM[:, o:o + 2 * BANK].rearrange("p (e g c) -> p e g c", e=E3, g=G),
                                  wts[:, s].unsqueeze(3).to_broadcast([N, E3, G, C]), ALU.mult).then_inc(L.s["e_mul"], 1)

            def total(s):
                dve.wait_ge(L.s["e_half"], L.at["e_half"] + s + 1)
                dve.tensor_reduce(GATE[:, s * GC:(s + 1) * GC],
                                  HALF[:, s % 2, :].rearrange("p (e f) -> p f e", e=E3 // 2), AX.X, ALU.add)\
                    .then_inc(L.s["e_sum"], 1)

            for s in range(S):
                weigh(s)
                if 1 <= s < S - 1:
                    total(s - 1)
            dve.wait_ge(L.s["e_mul"], L.at["e_mul"] + S)
            dve.tensor_reduce(GATE[:, (S - 1) * GC:S * GC], TMP[:, (S - 1) % 2, :].rearrange("p (e f) -> p f e", e=E3),
                              AX.X, ALU.add).then_inc(L.s["e_sum"], 1)
            total(S - 2)
            dve.wait_ge(L.s["e_sum"], L.at["e_sum"] + S)
            dve.wait_ge(L.s["done"], L.at["done"] + S // 4 - 1)
            f3_add(dve, S // 4 - 1)

        def f3_add(eng, b):
            x = blocks(XC)[:, :, 4 * b:4 * b + 4, :].rearrange("p g s c -> p s g c")
            eng.tensor_tensor(x, x, GATE[:, b * BANK:(b + 1) * BANK].rearrange("p (s g c) -> p s g c", s=4, g=G),
                              ALU.add).then_inc(f3.s["done"], 1)

        def f3_pool(pool):
            L = f3
            pool.wait_ge(L.s["sg"], L.at["sg"] + 1)
            pool.tensor_tensor(RT[5], RT[1], W1S.unsqueeze(2).to_broadcast([N, N, E3]), ALU.mult).then_inc(L.s["hot"], 1)
            for s in range(S - 1):
                pool.wait_ge(L.s["e_mul"], L.at["e_mul"] + s + 1)
                if s >= 2:
                    pool.wait_ge(L.s["e_sum"], L.at["e_sum"] + s - 1)
                pool.tensor_tensor(HALF[:, s % 2, :], TMP[:, s % 2, 0:BANK], TMP[:, s % 2, BANK:], ALU.add)\
                    .then_inc(L.s["e_half"], 1)
                if s > 4 and s % 4 == 1:
                    pool.wait_ge(L.s["e_sum"], L.at["e_sum"] + s - 1)
                    f3_add(pool, s // 4 - 1)

        for L, b, col in ((t0, 2, 0), (t1, 2, 0), (t3, 3, 0), (f3, 4, 0), (r1, 5, 0), (r2, 5, GC)):
            L.wbank, L.wcol = b, col

        def later_weights_pe(pe):
            tri_weights_pe(pe, t1)
            tri_weights_pe(pe, t3)
            f3_weights_pe(pe)
            rec_weights_pe(pe, r1)
            rec_weights_pe(pe, r2)

        def later_weights_dve(dve):
            tri_weights2_dve(dve, t1)
            tri_weights2_dve(dve, t3)
            f3_weights_dve(dve)
            rec_weights2_dve(dve, r1)
            rec_weights2_dve(dve, r2)

        block = ctx.enter_context(nc.Block())

        @block.sync
        def _(sp):
            X4, D4 = blocks(XR), x_d.rearrange("i (g s) c -> i g (s c)", g=G)
            for q in range(LOADS):
                if q == 1:
                    sp.dma_start(par[:, :], par_d).then_inc(par_first, 16)
                    sp.dma_start(row[:, :], row_d).then_inc(par_first, 16)
                f = slice(q * NC // G // LOADS, (q + 1) * NC // G // LOADS)
                sp.dma_start(XR[:, :].rearrange("p (g f) -> p g f", g=G)[:, :, f], D4[:, :, f]).then_inc(x_in[q], 16)
            sp.dma_start(mask[:, :], mask_d).then_inc(par_in, 16)
            sp.dma_start(w1[:, :, :], w1_d).then_inc(par_in, 16)
            sp.dma_start(w2[:, :, :], w2_d).then_inc(par_in, 16)
            sp.dma_start(w2l[:, :], w2l_d).then_inc(par_in, 16)
            out4 = out_d.rearrange("(g s) j c -> j g s c", g=G)
            XC4 = blocks(XC)
            for b in range(S // 4):
                sp.wait_ge(f3.s["done"], f3.at["done"] + b + 1)
                for g in range(G):
                    sp.dma_start(out4[:, g, 4 * b:4 * b + 4, :], XC4[:, g, 4 * b:4 * b + 4, :]).then_inc(out_stored, 16)
            sp.wait_ge(out_stored, 16 * G * (S // 4))

        @block.gpsimd
        def _(pool):
            consts_pool(pool)
            f3_weights_pool(pool)
            ln_pool(pool, t0)
            scan_weights_pool(pool)
            tri_pool(pool, t0, None)
            ln_pool(pool, f0)
            f0_pool(pool)
            ln_pool(pool, t1)
            tri_pool(pool, t1, r1)
            rec_pool(pool, r1)
            ln_pool(pool, sc)
            scan_pool(pool)
            ln_pool(pool, r2)
            rec_pool(pool, r2)
            ln_pool(pool, t3)
            tri_pool(pool, t3, f3)
            f3_pool(pool)

        @block.scalar
        def _(act):
            ln_act(act, t0)
            tri_act(act, t0, None)
            turn_x_copy(act, v0, 0)
            ln_act(act, f0)
            f0_act(act)
            ln_act(act, t1)
            tri_act(act, t1, r1)
            rec_act(act, r1)
            turn_x_copy(act, v1, 0)
            ln_act(act, sc)
            turn_x_copy(act, v2, 0)
            ln_act(act, r2)
            rec_act(act, r2)
            ln_act(act, t3)
            tri_act(act, t3, f3)
            f3_act(act)

        @block.vector
        def _(dve):
            consts_dve(dve)
            ln_dve_step(dve, t0, 0)
            dve.wait_ge(par_first, PAR_FIRST)
            tri_weights1_dve(dve, t0)
            for u in range(1, LN_STEPS):
                ln_dve_step(dve, t0, u)
                if u == 1:
                    tri_weights2_dve(dve, t0)

            tri_dve(dve, t0, None, {
                4: lambda dve: tri_weights1_dve(dve, t1), 8: lambda dve: tri_weights1_dve(dve, t3), 12: lambda dve: rec_weights1_dve(dve, r1),
                16: lambda dve: rec_weights1_dve(dve, r2), 20: f0_weights_dve})
            turn_x_copy(dve, v0, 1)
            ln_dve(dve, f0)
            f0_dve(dve)
            tri_dve(dve, t1, r1)
            rec_dve(dve, r1, None)
            turn_x_copy(dve, v1, 1)
            ln_dve(dve, sc)
            scan_dve(dve)
            turn_x_copy(dve, v2, 1)
            ln_dve(dve, r2)
            rec_dve(dve, r2, t3)
            tri_dve(dve, t3, f3)
            f3_dve(dve)

        @block.tensor
        def _(pe):
            pe.wait_ge(par_first, PAR_FIRST)
            tri_weights_pe(pe, t0)
            tri_pe(pe, t0)
            turn_x_pe(pe, v0)
            f0_pe(pe)
            tri_pe(pe, t1)
            rec_pe(pe, r1)
            turn_x_pe(pe, v1)
            scan_pe(pe)
            turn_x_pe(pe, v2)
            rec_pe(pe, r2)
            tri_pe(pe, t3)
            f3_pe(pe)


def packed(inputs, np):
    def col(a, rows=N):
        a = np.asarray(a).reshape(-1, 1)
        return np.tile(a, (rows // a.shape[0], 1))

    def mat(a):
        return np.tile(np.asarray(a), (G, 1))

    L0, L1, L3, F0, F3 = "L0_conv_", "L1_conv_", "L3_conv_", "L0_ffn_", "L3_ffn_"
    i = inputs
    parts = [mat(np.concatenate([i[L0 + n] for n in ("Wga", "Wgb", "Wla", "Wlb", "Wgo")], 1)),
             mat(np.concatenate([i[L1 + n] for n in ("w_ag", "w_bg", "w_ap", "w_bp", "w_g")], 1)),
             mat(np.concatenate([i[L3 + n] for n in ("w2", "w1", "wg")], 1)),
             mat(i[L0 + "Wlo"]), mat(i[L1 + "w_z"]), mat(i[L3 + "wo"])]
    for p, names in ((L0, ("ln_in_w", "ln_in_b", "ln_o_w", "ln_o_b")), (L1, ("ln_in_w", "ln_in_b", "ln_out_w", "ln_out_b")),
                     (L3, ("norm_g", "norm_b", "onorm_g", "onorm_b"))):
        parts += [col(i[p + n]) for n in names]
    parts += [mat(np.asarray(i[F0 + "gate_w"]).T), col(i[F0 + "gate_b"]),
              mat(np.asarray(i["L2_conv_W"]).transpose(1, 0, 2).reshape(C, TAPS * C))]
    for p in ("L1_ffn_", "L2_ffn_"):
        parts += [mat(i[p + "W"]), mat(np.asarray(i[p + "V"]).T), col(i[p + "gamma"]), col(i[p + "beta"])]
    parts += [mat(i[F3 + "router_w"]), mat(np.asarray(i[F3 + "expert_w"]).transpose(1, 0, 2).reshape(C, E3 * C))]
    par = np.concatenate(parts, 1)
    rows = [i[L0 + n] for n in ("bga", "bgb", "bla", "blb", "bgo")]
    rows += [i[L1 + n] for n in ("b_ag", "b_bg", "b_ap", "b_bp", "b_g")]
    rows += [i[L3 + n] for n in ("b2", "b1", "bg")] + [i[L0 + "blo"], i[L1 + "b_z"], i[L3 + "bo"]]
    rows += [i[F3 + "router_b"], np.asarray(i[F3 + "expert_b"]).reshape(-1)]
    row = np.concatenate([np.asarray(r) for r in rows])[None, :]
    return {
        "x": np.asarray(i["x"]).reshape(N, N, C),
        "par": par,
        "row": row,
        "mask": np.asarray(i[L1 + "mask"])[0].T,
        "w1": np.asarray(i[F0 + "weight1"]).transpose(1, 0, 2),
        "w2": np.asarray(i[F0 + "weight2"])[:, 0:H0].transpose(1, 0, 2),
        "w2l": np.asarray(i[F0 + "weight2"])[:, H0].T,
    }


def kernel(**inputs):
    import numpy as _np
    import concourse.bacc as _bacc
    from concourse.bass_utils import run_bass_kernel_spmd as _run

    nc = _bacc.Bacc("TRN2", target_bir_lowering=False, num_devices=1)
    arrays, args = {}, []
    for name, a in packed(inputs, _np).items():
        a = _np.ascontiguousarray(a)
        arrays[f"in_{name}_dram"] = a
        args.append(nc.dram_tensor(f"in_{name}_dram", a.shape, mybir.dt.from_np(a.dtype), kind="ExternalInput").ap())
    out = nc.dram_tensor("out_0_dram", (N, N, C), F32, kind="ExternalOutput").ap()
    build(nc, *args, out)
    r = _run(nc, [arrays], core_ids=[0])
    return r.results[0]["out_0_dram"].reshape(1, N, N, C)
```
